# Optimizing a Trainium2 kernel written in Bass

```python
import numpy as np
import jax
import jax.numpy as jnp

def _softmax(x, axis=-1):
    return jax.nn.softmax(x, axis=axis)

def _gelu(x):
    return jax.nn.gelu(x, approximate=True)

def _silu(x):
    return jax.nn.silu(x)

def _sigmoid(x):
    return jax.nn.sigmoid(x)

def _layernorm(x, axis=-1, eps=1e-05):
    m = jnp.mean(x, axis=axis, keepdims=True)
    v = jnp.var(x, axis=axis, keepdims=True)
    return (x - m) / jnp.sqrt(v + eps)

def _scatter_add(tgt, idx, src, axis=0):
    return tgt.at[idx].add(src)

def _segment_sum(src, seg, n):
    return jax.ops.segment_sum(src, seg, n)
kernel_name = 'mk_hybrid_d1_jaxref_r8_04fd11'

def setup_inputs(seed: int=0):
    np.random.seed(seed)
    _w = jnp.asarray

    def _L0_attn_a_setup():
        import jax, jax.numpy as jnp
        import numpy as np
        DIM = 128
        HEADS = 16
        HEAD_DIM = DIM // HEADS
        SCALE = HEAD_DIM ** (-0.5)

        def apply_rope(x, theta=10000.0):
            n, d = (x.shape[2], x.shape[3])
            seq = jnp.arange(n, dtype=jnp.float32)
            inv = 1.0 / theta ** (jnp.arange(0, d, 2, dtype=jnp.float32) / d)
            freqs = seq[:, None] * inv[None, :]
            cos = jnp.cos(freqs)[None, None]
            sin = jnp.sin(freqs)[None, None]
            x1, x2 = jnp.split(x, 2, axis=-1)
            return jnp.concatenate([x1 * cos - x2 * sin, x1 * sin + x2 * cos], axis=-1)
        key = jax.random.key(seed)
        ks = jax.random.split(key, 7)
        s = DIM ** (-0.5)
        return {'x': jax.random.normal(ks[0], (2, 256, DIM), dtype=jnp.float32), 'Wqkv': jax.random.normal(ks[1], (3 * DIM, DIM), dtype=jnp.float32) * s, 'bqkv': jax.random.normal(ks[2], (3 * DIM,), dtype=jnp.float32) * 0.02, 'Wpre': jax.random.normal(ks[3], (HEADS, HEADS), dtype=jnp.float32) * HEADS ** (-0.5), 'Wpost': jax.random.normal(ks[4], (HEADS, HEADS), dtype=jnp.float32) * HEADS ** (-0.5), 'Wout': jax.random.normal(ks[5], (DIM, DIM), dtype=jnp.float32) * s, 'bout': jax.random.normal(ks[6], (DIM,), dtype=jnp.float32) * 0.02}
    _L0_attn_a_in = _L0_attn_a_setup()

    def _L0_attn_b_setup():
        import jax, jax.numpy as jnp
        import numpy as np
        B, T = (4, 256)
        D_MODEL = 128
        N_HEADS = 8
        HEAD_DIM = 32
        KV_LRANK = 64

        def _orthogonalize_per_head(w):
            chunks = w.reshape(N_HEADS, HEAD_DIM, D_MODEL)

            def ns(m):
                A = m @ m.T
                Bm = 1.5 * jnp.eye(HEAD_DIM, dtype=m.dtype) - 0.5 * A
                return Bm @ m
            return jax.vmap(ns)(chunks).reshape(w.shape)
        key = jax.random.key(seed)
        ks = jax.random.split(key, 6)

        def lin(k, out_dim, in_dim):
            bound = 1.0 / np.sqrt(in_dim)
            return jax.random.uniform(k, (out_dim, in_dim), jnp.float32, -bound, bound)
        Wq = _orthogonalize_per_head(lin(ks[0], N_HEADS * HEAD_DIM, D_MODEL))
        return {'x': jax.random.normal(ks[1], (B, T, D_MODEL), jnp.float32), 'Wq': Wq, 'Wkv_down': lin(ks[2], KV_LRANK, D_MODEL), 'Wk_up': lin(ks[3], N_HEADS * HEAD_DIM, KV_LRANK), 'Wv_up': lin(ks[4], N_HEADS * HEAD_DIM, KV_LRANK), 'Wo': lin(ks[5], D_MODEL, N_HEADS * HEAD_DIM)}
    _L0_attn_b_in = _L0_attn_b_setup()

    def _L0_ffn_setup():
        import math
        import jax, jax.numpy as jnp
        import numpy as np
        B, T, D = (4, 512, 128)
        H = 16
        HD = D // H
        CAP = int(512 * 0.125)
        DFF = int(D * 4 * 2 / 3)
        EPS = 1e-06

        def rmsnorm(x, g):
            return x * jax.lax.rsqrt(jnp.mean(x * x, axis=-1, keepdims=True) + EPS) * g
        key = jax.random.key(seed)
        ks = jax.random.split(key, 9)
        s = lambda k, shape: jax.random.normal(k, shape, jnp.float32) * 0.02
        return {'x': jax.random.normal(ks[0], (B, T, D), jnp.float32), 'w_router': s(ks[1], (D,)), 'W_qkv': s(ks[2], (3 * D, D)), 'W_out': s(ks[3], (D, D)), 'g1': jnp.ones((D,), jnp.float32), 'g2': jnp.ones((D,), jnp.float32), 'W1': s(ks[4], (DFF, D)), 'W2': s(ks[5], (DFF, D)), 'W3': s(ks[6], (D, DFF))}
    _L0_ffn_in = _L0_ffn_setup()
    _d = {'L0_attn_a_x': _L0_attn_a_in['x'], 'L0_attn_a_Wqkv': _L0_attn_a_in['Wqkv'], 'L0_attn_a_bqkv': _L0_attn_a_in['bqkv'], 'L0_attn_a_Wpre': _L0_attn_a_in['Wpre'], 'L0_attn_a_Wpost': _L0_attn_a_in['Wpost'], 'L0_attn_a_Wout': _L0_attn_a_in['Wout'], 'L0_attn_a_bout': _L0_attn_a_in['bout'], 'L0_attn_b_Wq': _L0_attn_b_in['Wq'], 'L0_attn_b_Wkv_down': _L0_attn_b_in['Wkv_down'], 'L0_attn_b_Wk_up': _L0_attn_b_in['Wk_up'], 'L0_attn_b_Wv_up': _L0_attn_b_in['Wv_up'], 'L0_attn_b_Wo': _L0_attn_b_in['Wo'], 'L0_ffn_w_router': _L0_ffn_in['w_router'], 'L0_ffn_W_qkv': _L0_ffn_in['W_qkv'], 'L0_ffn_W_out': _L0_ffn_in['W_out'], 'L0_ffn_g1': _L0_ffn_in['g1'], 'L0_ffn_g2': _L0_ffn_in['g2'], 'L0_ffn_W1': _L0_ffn_in['W1'], 'L0_ffn_W2': _L0_ffn_in['W2'], 'L0_ffn_W3': _L0_ffn_in['W3']}
    _x0 = _d['L0_attn_a_x']
    _d['L0_attn_a_x'] = jax.random.normal(jax.random.fold_in(jax.random.key(seed), 1), (4, 1024, 128), dtype=_x0.dtype)
    del _x0
    return _d

def reference(L0_attn_a_x, L0_attn_a_Wqkv, L0_attn_a_bqkv, L0_attn_a_Wpre, L0_attn_a_Wpost, L0_attn_a_Wout, L0_attn_a_bout, L0_attn_b_Wq, L0_attn_b_Wkv_down, L0_attn_b_Wk_up, L0_attn_b_Wv_up, L0_attn_b_Wo, L0_ffn_w_router, L0_ffn_W_qkv, L0_ffn_W_out, L0_ffn_g1, L0_ffn_g2, L0_ffn_W1, L0_ffn_W2, L0_ffn_W3):

    def _L0_attn_a_ref(x, Wqkv, bqkv, Wpre, Wpost, Wout, bout):
        import jax, jax.numpy as jnp
        import numpy as np
        DIM = 128
        HEADS = 16
        HEAD_DIM = DIM // HEADS
        SCALE = HEAD_DIM ** (-0.5)

        def apply_rope(x, theta=10000.0):
            n, d = (x.shape[2], x.shape[3])
            seq = jnp.arange(n, dtype=jnp.float32)
            inv = 1.0 / theta ** (jnp.arange(0, d, 2, dtype=jnp.float32) / d)
            freqs = seq[:, None] * inv[None, :]
            cos = jnp.cos(freqs)[None, None]
            sin = jnp.sin(freqs)[None, None]
            x1, x2 = jnp.split(x, 2, axis=-1)
            return jnp.concatenate([x1 * cos - x2 * sin, x1 * sin + x2 * cos], axis=-1)
        b, n, _ = x.shape
        qkv = x @ Wqkv.T + bqkv
        q, k, v = jnp.split(qkv, 3, axis=-1)
        reshape = lambda t: t.reshape(b, n, HEADS, HEAD_DIM).transpose(0, 2, 1, 3)
        q, k, v = (reshape(q), reshape(k), reshape(v))
        q = apply_rope(q)
        k = apply_rope(k)
        logits = jnp.einsum('bhid,bhjd->bhij', q, k) * SCALE
        logits = jnp.einsum('bhij,gh->bgij', logits, Wpre)
        attn = jax.nn.softmax(logits, axis=-1)
        attn = jnp.einsum('bhij,gh->bgij', attn, Wpost)
        out = jnp.einsum('bhij,bhjd->bhid', attn, v)
        out = out.transpose(0, 2, 1, 3).reshape(b, n, DIM)
        return out @ Wout.T + bout

    def _L0_attn_b_ref(x, Wq, Wkv_down, Wk_up, Wv_up, Wo):
        import jax, jax.numpy as jnp
        import numpy as np
        B, T = (4, 256)
        D_MODEL = 128
        N_HEADS = 8
        HEAD_DIM = 32
        KV_LRANK = 64

        def _orthogonalize_per_head(w):
            chunks = w.reshape(N_HEADS, HEAD_DIM, D_MODEL)

            def ns(m):
                A = m @ m.T
                Bm = 1.5 * jnp.eye(HEAD_DIM, dtype=m.dtype) - 0.5 * A
                return Bm @ m
            return jax.vmap(ns)(chunks).reshape(w.shape)
        b, t, _ = x.shape
        q = (x @ Wq.T).reshape(b, t, N_HEADS, HEAD_DIM)
        kv_latent = x @ Wkv_down.T
        k = (kv_latent @ Wk_up.T).reshape(b, t, N_HEADS, HEAD_DIM)
        v = (kv_latent @ Wv_up.T).reshape(b, t, N_HEADS, HEAD_DIM)
        scale = HEAD_DIM ** (-0.5)
        scores = jnp.einsum('bqhd,bkhd->bhqk', q, k) * scale
        attn = jax.nn.softmax(scores, axis=-1)
        out = jnp.einsum('bhqk,bkhd->bqhd', attn, v)
        out = out.reshape(b, t, N_HEADS * HEAD_DIM)
        return out @ Wo.T

    def _L0_ffn_ref(x, w_router, W_qkv, W_out, g1, g2, W1, W2, W3):
        import math
        import jax, jax.numpy as jnp
        import numpy as np
        B, T, D = (4, 512, 128)
        H = 16
        HD = D // H
        CAP = int(512 * 0.125)
        DFF = int(D * 4 * 2 / 3)
        EPS = 1e-06

        def rmsnorm(x, g):
            return x * jax.lax.rsqrt(jnp.mean(x * x, axis=-1, keepdims=True) + EPS) * g
        Bq, Tq, Dq = x.shape
        scores = x @ w_router
        _, idx = jax.lax.top_k(scores, CAP)
        x_sel = jnp.take_along_axis(x, idx[:, :, None], axis=1)
        h = rmsnorm(x_sel, g1)
        qkv = (h @ W_qkv.T).reshape(Bq, CAP, 3, H, HD)
        q, k, v = jnp.moveaxis(qkv, 2, 0)
        att = jnp.einsum('bqhd,bkhd->bhqk', q, k) / math.sqrt(HD)
        mask = jnp.triu(jnp.ones((CAP, CAP), bool), 1)
        att = jnp.where(mask, -jnp.inf, att)
        att = jax.nn.softmax(att, axis=-1)
        o = jnp.einsum('bhqk,bkhd->bqhd', att, v).reshape(Bq, CAP, Dq)
        x_attn = o @ W_out.T
        h2 = rmsnorm(x_sel + x_attn, g2)
        x_ff = jax.nn.silu(h2 @ W1.T) * (h2 @ W2.T) @ W3.T
        x_proc = x_sel + x_attn + x_ff
        out = x.at[jnp.arange(Bq)[:, None], idx].set(x_proc)
        return out
    x = L0_attn_a_x
    x = x + _L0_attn_a_ref(_layernorm(x, axis=-1), L0_attn_a_Wqkv, L0_attn_a_bqkv, L0_attn_a_Wpre, L0_attn_a_Wpost, L0_attn_a_Wout, L0_attn_a_bout)
    x = x + _L0_ffn_ref(_layernorm(x, axis=-1), L0_ffn_w_router, L0_ffn_W_qkv, L0_ffn_W_out, L0_ffn_g1, L0_ffn_g2, L0_ffn_W1, L0_ffn_W2, L0_ffn_W3)
    x = x + _L0_attn_b_ref(_layernorm(x, axis=-1), L0_attn_b_Wq, L0_attn_b_Wkv_down, L0_attn_b_Wk_up, L0_attn_b_Wv_up, L0_attn_b_Wo)
    x = x + _L0_ffn_ref(_layernorm(x, axis=-1), L0_ffn_w_router, L0_ffn_W_qkv, L0_ffn_W_out, L0_ffn_g1, L0_ffn_g2, L0_ffn_W1, L0_ffn_W2, L0_ffn_W3)
    return x

_drawn_inputs = setup_inputs


def setup_inputs(seed=0):
    import zlib

    import numpy as np

    out = dict(_drawn_inputs(seed))
    spreads = {'L0_ffn_g1': (1.0, 0.6), 'L0_ffn_g2': (1.0, 0.6)}
    factors = {'L0_attn_a_bqkv': 3.674,
     'L0_attn_b_Wq': 8.0,
     'L0_attn_b_Wkv_down': 8.0,
     'L0_attn_b_Wk_up': 8.0,
     'L0_attn_b_Wv_up': 8.0,
     'L0_attn_b_Wo': 8.0,
     'L0_ffn_w_router': 8.0,
     'L0_ffn_W_qkv': 8.0,
     'L0_ffn_W_out': 8.0,
     'L0_ffn_W1': 8.0,
     'L0_ffn_W2': 8.0,
     'L0_ffn_W3': 8.0}
    for name, (base, spread) in spreads.items():
        noise = np.random.default_rng([zlib.crc32(name.encode()), seed]).standard_normal(out[name].shape)
        drawn = base * np.exp(spread * noise) if base else spread * noise
        out[name] = jnp.asarray(drawn.astype(out[name].dtype))
    for name, factor in factors.items():
        out[name] = (out[name] * factor).astype(out[name].dtype)
    return out
```

```python
from contextlib import ExitStack

import numpy as np
import concourse.bass as bass
from concourse import mybir

ALU = mybir.AluOpType
ACT = mybir.ActivationFunctionType
AX = mybir.AxisListType
F32 = mybir.dt.float32
F16 = mybir.dt.float16

P = 128
NB, SEQ, D = 4, 1024, 128
TPB = SEQ // P
NT = NB * TPB
NTOK = NB * SEQ
CH = 512
NCH = NTOK // CH
HA, HDA = 16, 8
HB, HDB = 8, 32
RANK = 64
CAP = 64
DFF = 341
HALF = SEQ // 2
UNITS = 4
TILES = 4
JB = SEQ // P
TURN_T = UNITS * TILES
TURN_J = UNITS * JB
AHEAD = 6
LAG = 2
PSCALE = 2.0 ** 14
LN_EPS, RMS_EPS = 1e-5, 1e-6


def wait_apart(eng, passed, sem, value):
    eng.wait_ge(sem, value)
    eng.sem_inc(passed, 1)


class Store:

    def __init__(self, nc, stack):
        self.nc, self.stack, self.stage_sems = nc, stack, []

    def sem(self, name):
        self.stage_sems.append(self.nc.alloc_semaphore(name=name))
        return self.stage_sems[-1]

    def end_stage(self):
        self.nc.all_engine_barrier()
        self.nc.clear_and_free_semaphores(self.stage_sems)
        self.nc.all_engine_barrier()
        self.stage_sems = []

    def sb(self, stack, name, shape, dt=F32):
        return stack.enter_context(self.nc.sbuf_tensor(name, shape, dt))

    def ps(self, stack, name, shape, dt=F32):
        return stack.enter_context(self.nc.psum_tensor(name, shape, dt))


class LnWork:

    def __init__(self, st, stack, tag, xn):
        self.stats = st.sb(stack, tag + "_stats", [P, NT, 6])
        self.mv = st.sb(stack, tag + "_mv", [P, NT, 2])
        self.ve = st.sb(stack, tag + "_ve", [P, NT])
        self.sd = st.sb(stack, tag + "_sd", [P, NT])
        self.r0 = st.sb(stack, tag + "_r0", [P, NT])
        self.t0 = st.sb(stack, tag + "_t0", [P, NT])
        self.t1 = st.sb(stack, tag + "_t1", [P, NT])
        self.rstd = st.sb(stack, tag + "_rstd", [P, NT])
        self.xn = xn
        self.step = st.sem(tag + "_step")
        self.ve_ready = st.sem(tag + "_ve_ready")
        self.sd_ready = st.sem(tag + "_sd_ready")
        self.normed = st.sem(tag + "_normed")


def layernorm_vector(dve, w, x, wait_x):
    for t in range(NT):
        if t % TPB == 0:
            wait_x(t // TPB)
        last = dve.bn_stats(w.stats[:, t, :], x[:, t, :])
    last.then_inc(w.step, 1)
    dve.wait_ge(w.step, 1)
    for t in range(NT):
        last = dve.bn_aggr(w.mv[:, t, :], w.stats[:, t, :])
    last.then_inc(w.step, 1)
    dve.wait_ge(w.step, 2)
    dve.tensor_scalar(w.ve[:], w.mv[:, :, 1], LN_EPS, None, ALU.add).then_inc(w.ve_ready, 1)
    dve.wait_ge(w.sd_ready, 1)
    dve.reciprocal(w.r0[:], w.sd[:]).then_inc(w.step, 1)
    newton_rsqrt(dve, w.step, 3, w.ve, w.r0, w.t0, w.t1, w.rstd)
    dve.wait_ge(w.step, 7)
    for t in range(NT):
        dve.tensor_scalar(w.xn[:, t, :], x[:, t, :], w.mv[:, t, 0:1], w.rstd[:, t:t + 1],
                          ALU.subtract, ALU.mult).then_inc(w.normed, 1)


def newton_rsqrt(dve, step, n, v, r0, t0, t1, out):
    dve.wait_ge(step, n)
    dve.tensor_tensor(t0[:], r0[:], r0[:], ALU.mult).then_inc(step, 1)
    dve.wait_ge(step, n + 1)
    dve.tensor_tensor(t1[:], t0[:], v[:], ALU.mult).then_inc(step, 1)
    dve.wait_ge(step, n + 2)
    dve.tensor_scalar(t0[:], t1[:], -0.5, 1.5, ALU.mult, ALU.add).then_inc(step, 1)
    dve.wait_ge(step, n + 3)
    dve.tensor_tensor(out[:], r0[:], t0[:], ALU.mult).then_inc(step, 1)


def layernorm_scalar(act, w):
    act.wait_ge(w.ve_ready, 1)
    act.activation(w.sd[:], w.ve[:], ACT.Sqrt).then_inc(w.sd_ready, 1)


def prepare_a(st, io, x, qT, v, khi, klo, wpre, wpost):
    nc = st.nc
    with ExitStack() as s:
        xn = st.sb(s, "a_xn", [P, NT, D])
        ln = LnWork(st, s, "lna", xn)
        ident = st.sb(s, "a_ident", [P, P])
        wqk = st.sb(s, "a_wqk", [P, 4, D])
        wv = st.sb(s, "a_wv", [P, D])
        bqk = st.sb(s, "a_bqk", [P, 4])
        bv = st.sb(s, "a_bv", [P, D])
        rope = st.sb(s, "a_rope", [P, 4, SEQ])
        hT = st.sb(s, "a_hT", [P, NTOK])
        prod = st.sb(s, "a_prod", [P, 4, 2, CH])
        kT = st.sb(s, "a_kT", [P, 2, CH])
        tps = [st.ps(s, f"a_tps{i}", [P, CH]) for i in range(2)]
        qkps = [st.ps(s, f"a_qkps{i}", [P, CH]) for i in range(4)]
        vps = [st.ps(s, f"a_vps{i}", [P, CH]) for i in range(2)]
        x_in = [st.sem(f"a_x_in{b}") for b in range(NB)]
        w_in = st.sem("a_w_in")
        transposed, hT_ready = st.sem("a_transposed"), st.sem("a_hT_ready")
        qk_done, prod_ready, qk_summed = st.sem("a_qk_done"), st.sem("a_prod_ready"), st.sem("a_qk_summed")
        v_done, v_kept, khi_ready, klo_ready = (st.sem("a_v_done"), st.sem("a_v_kept"),
                                                st.sem("a_khi_ready"), st.sem("a_klo_ready"))
        block = s.enter_context(nc.Block())
        LOADS = 8

        @block.sync
        def _(sp):
            for b in range(NB):
                sp.dma_start(x[:, b * TPB:(b + 1) * TPB, :],
                             io["x"][b].rearrange("(t p) d -> p t d", p=P)).then_inc(x_in[b], 16)

        @block.scalar
        def _(act):
            act.dma_start(ident[:], io["ident"]).then_inc(w_in, 16)
            act.dma_start(wqk[:], io["wqk_T"]).then_inc(w_in, 16)
            act.dma_start(wv[:], io["wv_T"]).then_inc(w_in, 16)
            act.dma_start(bqk[:], io["bqk"]).then_inc(w_in, 16)
            act.dma_start(bv[:], io["bv"].broadcast_to([P, D])).then_inc(w_in, 16)
            act.dma_start(rope[:], io["rope"]).then_inc(w_in, 16)
            act.dma_start(wpre[:], io["wpre"]).then_inc(w_in, 16)
            act.dma_start(wpost[:], io["wpost"].broadcast_to([P, HA * D])).then_inc(w_in, 16)
            layernorm_scalar(act, ln)
            for c in range(NCH + 2):
                if c < NCH:
                    act.wait_ge(transposed, c + 1)
                    act.copy(hT[:, c * CH:(c + 1) * CH], tps[c % 2][:]).then_inc(hT_ready, 1)
                if 1 <= c <= NCH:
                    m = c - 1
                    act.wait_ge(v_done, m + 1)
                    act.copy(v[:, m * CH:(m + 1) * CH], vps[m % 2][:]).then_inc(v_kept, 1)
                if c >= 2:
                    m = c - 2
                    act.wait_ge(qk_summed, 2 * m + 2)
                    act.copy(khi[:, m * CH:(m + 1) * CH], kT[:, m % 2, :]).then_inc(khi_ready, 1)

        @block.tensor
        def _(pe):
            pe.wait_ge(w_in, 16 * LOADS)
            for c in range(NCH + 1):
                if c < NCH:
                    pe.wait_ge(ln.normed, 4 * c + 4)
                    if c >= 2:
                        pe.wait_ge(hT_ready, c - 1)
                    for k in range(4):
                        last = pe.transpose(tps[c % 2][:, k * P:(k + 1) * P], ln.xn[:, 4 * c + k, :], ident[:])
                    last.then_inc(transposed, 1)
                if c >= 1:
                    m = c - 1
                    pe.wait_ge(hT_ready, m + 1)
                    if m >= 2:
                        pe.wait_ge(v_kept, m - 1)
                    for k in range(4):
                        last = pe.matmul(vps[m % 2][:, k * D:(k + 1) * D],
                                         hT[:, m * CH + k * P:m * CH + (k + 1) * P], wv[:],
                                         start=(k == 0), stop=True, skip_group_check=True)
                    last.then_inc(v_done, 1)
                    for i in range(4):
                        if m >= 1:
                            pe.wait_ge(prod_ready, 4 * (m - 1) + i + 1)
                        pe.matmul(qkps[i][:], wqk[:, i, :], hT[:, m * CH:(m + 1) * CH],
                                  start=True, stop=True).then_inc(qk_done, 1)

        @block.vector
        def _(dve):
            layernorm_vector(dve, ln, x, lambda b: dve.wait_ge(x_in[b], 16))
            dve.wait_ge(w_in, 16 * LOADS)
            for c in range(NCH):
                at = (c * CH) % SEQ
                for i in range(4):
                    if c >= 2:
                        dve.wait_ge(qk_summed, 2 * (c - 2) + i // 2 + 1)
                    dve.wait_ge(qk_done, 4 * c + i + 1)
                    dve.scalar_tensor_tensor(out=prod[:, i, c % 2, :], in0=qkps[i][:], scalar=bqk[:, i:i + 1],
                                             in1=rope[:, i, at:at + CH], op0=ALU.add,
                                             op1=ALU.mult).then_inc(prod_ready, 1)
            for c in range(NCH):
                dve.wait_ge(v_kept, c + 1)
                vv = v[:, c * CH:(c + 1) * CH].rearrange("p (k d) -> p k d", k=4)
                dve.tensor_tensor(vv, vv, bv[:, None, :].broadcast_to([P, 4, D]), ALU.add)

        @block.gpsimd
        def _(pool):
            for c in range(NCH):
                pool.wait_ge(prod_ready, 4 * c + 2)
                pool.tensor_tensor(qT[:, c * CH:(c + 1) * CH], prod[:, 0, c % 2, :], prod[:, 1, c % 2, :],
                                   ALU.add).then_inc(qk_summed, 1)
                pool.wait_ge(prod_ready, 4 * c + 4)
                if c >= 2:
                    pool.wait_ge(khi_ready, c - 1)
                pool.tensor_tensor(kT[:, c % 2, :], prod[:, 2, c % 2, :], prod[:, 3, c % 2, :],
                                   ALU.add).then_inc(qk_summed, 1)
                pool.wait_ge(khi_ready, c + 1)
                pool.wait_ge(qk_summed, 2 * c + 2)
                pool.tensor_tensor(klo[:, c * CH:(c + 1) * CH], kT[:, c % 2, :], khi[:, c * CH:(c + 1) * CH],
                                   ALU.subtract).then_inc(klo_ready, 1)


def attend(st, kind, operands, ident):
    nc = st.nc
    a = kind == "a"
    heads = NB * (HA if a else HB)
    turns = heads // 2
    tpb = turns // NB
    vw = D if a else 2 * HDB
    n_tiles, n_blocks = turns * TURN_T, turns * TURN_J
    with ExitStack() as s:
        probs = st.sb(s, kind + "_probs", [P, TURN_T, SEQ])
        pT = st.sb(s, kind + "_pT", [P, 4, 2, HALF], F16)
        negmax = st.sb(s, kind + "_negmax", [P, TURN_T])
        den = st.sb(s, kind + "_den", [P, TURN_T])
        rden = st.sb(s, kind + "_rden", [P, TURN_T])
        if a:
            qT, v, khi, klo, wpre, wpost, accT = operands
            kcur = st.sb(s, "a_kcur", [P, 2, SEQ], F16)
            qs = st.sb(s, "a_qs", [P, 2, 2, SEQ], F16)
            qtmp = st.sb(s, "a_qtmp", [P, SEQ])
            vs = st.sb(s, "a_vs", [P, 2, 2, JB, D], F16)
            vtmp = st.sb(s, "a_vtmp", [P, JB, D])
        else:
            q_dram, k_dram, v_all, oT = operands
            qs = st.sb(s, "b_qs", [P, 2, SEQ], F16)
            ks = st.sb(s, "b_ks", [P, 2, SEQ], F16)
            vs = st.sb(s, "b_vs", [P, 2, JB, 2 * HDB], F16)
        score_ps = [st.ps(s, f"{kind}_score_ps{i}", [P, SEQ]) for i in range(2)]
        turn_ps = [st.ps(s, f"{kind}_turn_ps{i}", [P, HALF]) for i in range(2)]
        out_ps = [st.ps(s, f"{kind}_out_ps{i}", [P, HALF]) for i in range(2)]

        scored = st.sem(kind + "_scored")
        max_ready = st.sem(kind + "_max_ready")
        exp_done = st.sem(kind + "_exp_done")
        rden_ready = st.sem(kind + "_rden_ready")
        normed = st.sem(kind + "_normed")
        turned = st.sem(kind + "_turned")
        hi_ready = st.sem(kind + "_hi_ready")
        lo_ready = st.sem(kind + "_lo_ready")
        pv_done = st.sem(kind + "_pv_done")
        out_kept = st.sem(kind + "_out_kept")
        k_in = [st.sem(f"{kind}_k_in{i}") for i in range(2)]
        q_step = st.sem(kind + "_q_step")
        v_step = st.sem(kind + "_v_step")
        q_scaled = st.sem(kind + "_q_scaled")
        VS = 3 if a else 1
        act_passed, pool_passed = st.sem(kind + "_act_passed"), st.sem(kind + "_pool_passed")
        block = s.enter_context(nc.Block())

        if a:
            @block.sync
            def _(sp):
                for b in range(NB):
                    if b >= 1:
                        sp.wait_ge(scored, b * HA * 2 * TILES)
                    sp.dma_start(kcur[:, 0, :], khi[:, b * SEQ:(b + 1) * SEQ]).then_inc(k_in[0], 16)
                    sp.dma_start(kcur[:, 1, :], klo[:, b * SEQ:(b + 1) * SEQ]).then_inc(k_in[0], 16)
        else:
            @block.sync
            def _(sp):
                def load_head(g, slot):
                    for part in range(4):
                        rows = slice(part * HDB, (part + 1) * HDB)
                        sp.dma_start(qs[rows, slot, :], q_dram[part // 2, bass.ds(g, 1)]
                                     .rearrange("o d t -> (o d) t")).then_inc(k_in[slot], 16)
                        sp.dma_start(ks[rows, slot, :], k_dram[part % 2, bass.ds(g, 1)]
                                     .rearrange("o d t -> (o d) t")).then_inc(k_in[slot], 16)
                load_head(0, 0)
                load_head(1, 1)
                with sp.Fori(1, turns) as n:
                    for slot in range(2):
                        sp.wait_ge(scored, TURN_T * n - TURN_T + 2 * TILES * (slot + 1))
                        load_head(2 * n + slot, slot)

        @block.tensor
        def _(pe):
            def scores(n, t):
                n, t = n + t // TURN_T, t % TURN_T
                slot, half, k = t // 8, t // 4 % 2, t % 4
                T = TURN_T * n + t
                if not (isinstance(n, int) and T < 2):
                    pe.wait_ge(exp_done, T - 1)
                cols = slice(half * HALF + k * P, half * HALF + (k + 1) * P)
                out = score_ps[t % 2]
                if a:
                    if t % 8 == 0:
                        pe.wait_ge(q_step, 2 * (2 * n + slot + 1))
                        if slot == 0:
                            pe.wait_ge(k_in[0], 32 * (n // tpb + 1))
                    q0, q1 = qs[:, slot, 0, cols], qs[:, slot, 1, cols]
                    for c in range(2):
                        kc = slice(c * CH, (c + 1) * CH)
                        pe.matmul(out[:, kc], q0, kcur[:, 0, kc], start=True, stop=False)
                        pe.matmul(out[:, kc], q0, kcur[:, 1, kc], start=False, stop=False)
                    for c in range(2):
                        kc = slice(c * CH, (c + 1) * CH)
                        last = pe.matmul(out[:, kc], q1, kcur[:, 0, kc], start=False, stop=True)
                else:
                    if t % 8 == 0:
                        pe.wait_ge(k_in[slot], 128 * (n + 1))
                    for c in range(2):
                        kc = slice(c * CH, (c + 1) * CH)
                        last = pe.matmul(out[:, kc], qs[:, slot, cols], ks[:, slot, kc], start=True, stop=True)
                last.then_inc(scored, 1)

            def turn(n, j):
                u, jb = j // JB, j % JB
                if jb == 0:
                    pe.wait_ge(normed, TURN_T * n + TILES * (u + 1))
                if not (isinstance(n, int) and n == 0 and j < 2):
                    pe.wait_ge(lo_ready, TURN_J * n + j - 1)
                for k in range(TILES):
                    last = pe.transpose(turn_ps[j % 2][:, k * P:(k + 1) * P],
                                        probs[:, TILES * u + k, jb * P:(jb + 1) * P], ident[:])
                last.then_inc(turned, 1)

            def times_v(n, j):
                n, j = n + j // TURN_J, j % TURN_J
                u, jb = j // JB, j % JB
                slot, half = u // 2, u % 2
                pe.wait_ge(lo_ready, TURN_J * n + j + 1)
                if jb == 0:
                    if half == 0:
                        pe.wait_ge(v_step, VS * (2 * n + slot + 1))
                    if a and slot == 0 and not (isinstance(n, int) and n == 0):
                        pe.wait_ge(out_kept, 2 * n - 1 + half)
                    if not a and not (isinstance(n, int) and n == 0 and slot == 0):
                        pe.wait_ge(out_kept, UNITS * n + u - 1)
                hi, lo = pT[:, j % 4, 0, :], pT[:, j % 4, 1, :]
                if a:
                    first, final = slot == 0 and jb == 0, slot == 1 and jb == JB - 1
                    out = out_ps[half][:]
                    pe.matmul(out, vs[:, slot, 0, jb, :], hi, start=first, stop=False, skip_group_check=True)
                    pe.matmul(out, vs[:, slot, 0, jb, :], lo, start=False, stop=False, skip_group_check=True)
                    last = pe.matmul(out, vs[:, slot, 1, jb, :], hi, start=False, stop=final,
                                     skip_group_check=True)
                else:
                    out = out_ps[half][slot * vw:(slot + 1) * vw, :]
                    pe.matmul(out, vs[:, slot, jb, :], hi, start=jb == 0, stop=False, skip_group_check=True)
                    last = pe.matmul(out, vs[:, slot, jb, :], lo, start=False, stop=jb == JB - 1,
                                     skip_group_check=True)
                last.then_inc(pv_done, 1)

            def one_turn(n, first, last):
                for t in range(TURN_T):
                    if not (last and t + AHEAD >= TURN_T):
                        scores(n, t + AHEAD)
                    for j in (2 * t, 2 * t + 1):
                        turn(n, j)
                        if not (first and j < LAG):
                            times_v(n, j - LAG)

            for t in range(AHEAD):
                scores(0, t)
            one_turn(0, True, False)
            with pe.Fori(1, turns - 1) as n:
                one_turn(n, False, False)
            one_turn(turns - 1, False, True)
            for j in range(LAG):
                times_v(turns, j - LAG)

        @block.scalar
        def _(act):
            def exponentiate(n, t):
                n, t = n + t // TURN_T, t % TURN_T
                T = TURN_T * n + t
                act.wait_ge(max_ready, T + 1)
                if t % TILES == 0 and not (isinstance(n, int) and n == 0):
                    act.wait_ge(turned, TURN_J * n - TURN_J + JB * (t // TILES + 1))
                act.activation(probs[:, t, :], score_ps[t % 2][:], ACT.Exp, bias=negmax[:, t:t + 1],
                               accum_out=den[:, t:t + 1]).then_inc(exp_done, 1)

            def scale_q(g):
                if not (isinstance(g, int) and g == 0):
                    wait_apart(act, act_passed, q_step, 2 * g)
                act.activation(qtmp[:], qT[:, bass.ds((g // HA) * SEQ, SEQ)], ACT.Copy,
                               scale=wpre[:, bass.ds(g % HA, 1)]).then_inc(q_scaled, 1)

            def high(n, j):
                act.wait_ge(turned, TURN_J * n + j + 1)
                if not (isinstance(n, int) and n == 0 and j < 4):
                    act.wait_ge(pv_done, TURN_J * n + j - 3)
                act.copy(pT[:, j % 4, 0, :], turn_ps[j % 2][:]).then_inc(hi_ready, 1)

            def one_turn(n, last):
                for t in range(TURN_T):
                    high(n, 2 * t)
                    high(n, 2 * t + 1)
                    if not (last and t + AHEAD >= TURN_T):
                        exponentiate(n, t + AHEAD)
                    if a and (t + AHEAD) % 8 == 0 and not (last and t + AHEAD >= 8):
                        scale_q(2 * n + (t + AHEAD) // 8 + 1)

            if a:
                scale_q(0)
            for t in range(AHEAD):
                exponentiate(0, t)
                if a and t == 0:
                    scale_q(1)
            one_turn(0, False)
            with act.Fori(1, turns - 1) as n:
                one_turn(n, False)
            one_turn(turns - 1, True)

        @block.vector
        def _(dve):
            def row_max(n, t):
                n, t = n + t // TURN_T, t % TURN_T
                dve.wait_ge(scored, TURN_T * n + t + 1)
                dve.tensor_reduce(negmax[:, t:t + 1], score_ps[t % 2][:], AX.X, ALU.max,
                                  negate=True).then_inc(max_ready, 1)

            def invert(n, t):
                n, t = n + t // TURN_T, t % TURN_T
                dve.wait_ge(exp_done, TURN_T * n + t + 1)
                dve.reciprocal(rden[:, t:t + 1], den[:, t:t + 1]).then_inc(rden_ready, 1)

            def low(n, j):
                dve.wait_ge(hi_ready, TURN_J * n + j + 1)
                dve.tensor_tensor(pT[:, j % 4, 1, :], turn_ps[j % 2][:], pT[:, j % 4, 0, :],
                                  ALU.subtract).then_inc(lo_ready, 1)

            def keep_a(n, half):
                dve.wait_ge(pv_done, TURN_J * n + (3 + half) * JB)
                to = accT[:, bass.ds((n // tpb) * SEQ + half * HALF, HALF)]
                dve.tensor_tensor(to, out_ps[half][:], to, ALU.add).then_inc(out_kept, 1)

            def keep_b(n, u):
                slot, half = u // 2, u % 2
                rows = slice(slot * vw, (slot + 1) * vw)
                dve.wait_ge(pv_done, TURN_J * n + (u + 1) * JB)
                dve.tensor_copy(oT[rows, bass.ds(n * SEQ + half * HALF, HALF)],
                                out_ps[half][rows, :]).then_inc(out_kept, 1)

            def one_turn(n, first, last):
                for t in range(TURN_T):
                    if not (last and t + AHEAD >= TURN_T):
                        row_max(n, t + AHEAD)
                    low(n, 2 * t)
                    low(n, 2 * t + 1)
                    if not (last and t + AHEAD > TURN_T):
                        invert(n, t + AHEAD - 1)
                    if a and t == 1 and not first:
                        keep_a(n - 1, 1)
                    if a and t == 13:
                        keep_a(n, 0)
                    if not a and t % 4 == 1 and not (first and t == 1):
                        keep_b(n if t > 1 else n - 1, (t // 4 - 1) % UNITS)

            for t in range(AHEAD):
                row_max(0, t)
                if t:
                    invert(0, t - 1)
            one_turn(0, True, False)
            with dve.Fori(1, turns - 1) as n:
                one_turn(n, False, False)
            one_turn(turns - 1, False, True)
            if a:
                keep_a(turns - 1, 1)
            else:
                keep_b(turns - 1, UNITS - 1)

        @block.gpsimd
        def _(pool):
            def q_part(g, slot, i, first=False):
                if i == 0:
                    wait_apart(pool, pool_passed, q_scaled, g + 1)
                    if not first:
                        wait_apart(pool, pool_passed, scored, 2 * TILES * (g - 1))
                    pool.tensor_scalar(qs[:, slot, 0, :], qtmp[:], 1.0, 1.0, ALU.mult,
                                       ALU.mult).then_inc(q_step, 1)
                else:
                    pool.wait_ge(q_step, 2 * g + 1)
                    pool.tensor_tensor(qs[:, slot, 1, :], qtmp[:], qs[:, slot, 0, :],
                                       ALU.subtract).then_inc(q_step, 1)

            def v_part(g, slot, i, first=False):
                b, h = g // HA, g % HA
                if i == 0:
                    src = v[:, bass.ds(b * SEQ, SEQ)].rearrange("p (j d) -> p j d", j=JB)
                    w = wpost[:, bass.ds(h * D, D)][:, None, :].broadcast_to([P, JB, D])
                    pool.tensor_tensor(vtmp[:], src, w, ALU.mult).then_inc(v_step, 1)
                elif i == 1:
                    wait_apart(pool, pool_passed, v_step, 3 * g + 1)
                    if not first:
                        wait_apart(pool, pool_passed, pv_done, 2 * JB * (g - 1))
                    pool.tensor_scalar(vs[:, slot, 0, :, :], vtmp[:], 1.0, 1.0, ALU.mult,
                                       ALU.mult).then_inc(v_step, 1)
                else:
                    pool.wait_ge(v_step, 3 * g + 2)
                    pool.tensor_tensor(vs[:, slot, 1, :, :], vtmp[:], vs[:, slot, 0, :, :],
                                       ALU.subtract).then_inc(v_step, 1)

            def v_copy(n, slot, first):
                if not first:
                    wait_apart(pool, pool_passed, pv_done, TURN_J * n - TURN_J + 2 * JB * (slot + 1))
                pool.tensor_copy(vs[:, slot, :, :], v_all[:, bass.ds(2 * n + slot, 1), :, :]
                                 .rearrange("p o j d -> p (o j) d")).then_inc(v_step, 1)

            def normalise(n, t):
                wait_apart(pool, pool_passed, rden_ready, TURN_T * n + t + 1)
                pool.tensor_scalar(probs[:, t, :], probs[:, t, :], rden[:, t:t + 1], PSCALE,
                                   ALU.mult, ALU.mult).then_inc(normed, 1)

            def one_turn(n, first, last):
                for t in range(TURN_T):
                    normalise(n, t)
                    slot, k = t // 8, t % 8
                    if a:
                        more = not (last and slot == 1)
                        if k == 0 and more:
                            q_part(2 * n + slot + 1, 1 - slot, 0, first and slot == 0)
                        if k == 1 and more:
                            q_part(2 * n + slot + 1, 1 - slot, 1)
                        if k in (2, 3, 4):
                            v_part(2 * n + slot, slot, k - 2, first)
                    elif k == 2:
                        v_copy(n, slot, first)

            if a:
                for i in range(2):
                    q_part(0, 0, i, True)
            one_turn(0, True, False)
            with pool.Fori(1, turns - 1) as n:
                one_turn(n, False, False)
            one_turn(turns - 1, False, True)


def project_a(st, io, x, accT):
    nc = st.nc
    with ExitStack() as s:
        wout = st.sb(s, "pa_wout", [P, D])
        bout = st.sb(s, "pa_bout", [P, D])
        xb = st.sb(s, "pa_xb", [P, NT, D])
        y = [st.ps(s, f"pa_y{i}", [P, 4, D]) for i in range(2)]
        w_in, y_done, bias_added, y_read = (st.sem("pa_w_in"), st.sem("pa_y_done"),
                                            st.sem("pa_bias_added"), st.sem("pa_y_read"))
        block = s.enter_context(nc.Block())

        @block.sync
        def _(sp):
            sp.dma_start(wout[:], io["wout_T"]).then_inc(w_in, 16)
            sp.dma_start(bout[:], io["bout"].broadcast_to([P, D])).then_inc(w_in, 16)

        @block.tensor
        def _(pe):
            pe.wait_ge(w_in, 32)
            for c in range(NCH):
                if c >= 2:
                    pe.wait_ge(y_read, c - 1)
                for k in range(4):
                    t = 4 * c + k
                    last = pe.matmul(y[c % 2][:, k, :], accT[:, t * P:(t + 1) * P], wout[:],
                                     start=(k == 0), stop=True, skip_group_check=True)
                last.then_inc(y_done, 1)

        @block.gpsimd
        def _(pool):
            pool.wait_ge(w_in, 32)
            for c in range(NCH):
                pool.tensor_tensor(xb[:, 4 * c:4 * c + 4, :], x[:, 4 * c:4 * c + 4, :],
                                   bout[:, None, :].broadcast_to([P, 4, D]), ALU.add).then_inc(bias_added, 1)

        @block.vector
        def _(dve):
            for c in range(NCH):
                dve.wait_ge(bias_added, c + 1)
                dve.wait_ge(y_done, c + 1)
                dve.scalar_tensor_tensor(out=x[:, 4 * c:4 * c + 4, :], in0=y[c % 2][:], scalar=1.0 / PSCALE,
                                         in1=xb[:, 4 * c:4 * c + 4, :], op0=ALU.mult,
                                         op1=ALU.add).then_inc(y_read, 1)


def route(st, io, tag, x, xn, oh, ohT, xsel, xh):
    nc = st.nc
    with ExitStack() as s:
        ln = LnWork(st, s, tag + "ln", xn)
        ident = st.sb(s, tag + "ident", [P, P])
        wr = st.sb(s, tag + "wr", [P, D])
        iota = st.sb(s, tag + "iota", [P, 2, 2 * CAP])
        below = st.sb(s, tag + "below", [P, P])
        junk = st.sb(s, tag + "junk", [P, 4, SEQ])
        score = st.sb(s, tag + "score", [P, NT])
        part = st.sb(s, tag + "part", [P, NT, 4])
        rank = st.sb(s, tag + "rank", [P, NT])
        row = [st.ps(s, f"{tag}row{i}", [P, SEQ]) for i in range(2)]
        sel = [st.ps(s, f"{tag}sel{i}", [P, D]) for i in range(2)]
        tps = [st.ps(s, f"{tag}tps{i}", [P, 4, P]) for i in range(2)]
        w_in, row_ready, rank_ready = st.sem(tag + "w_in"), st.sem(tag + "row_ready"), st.sem(tag + "rank_ready")
        junked = st.sem(tag + "junked")
        zeroed = st.sem(tag + "zeroed")
        oh_ready, ohT_done, ohT_kept, sel_done = (st.sem(tag + "oh_ready"), st.sem(tag + "ohT_done"),
                                                  st.sem(tag + "ohT_kept"), st.sem(tag + "sel_done"))
        block = s.enter_context(nc.Block())

        @block.sync
        def _(sp):
            sp.dma_start(wr[:], io["w_router"].broadcast_to([P, D])).then_inc(w_in, 16)
            sp.dma_start(iota[:], io["iota"]).then_inc(w_in, 16)
            sp.dma_start(below[:], io["below"]).then_inc(w_in, 16)
            sp.dma_start(ident[:], io["ident"]).then_inc(w_in, 16)

        @block.scalar
        def _(act):
            layernorm_scalar(act, ln)
            for c in range(NCH):
                act.wait_ge(ohT_done, c + 1)
                act.copy(ohT[:, 4 * c:4 * c + 4, :], tps[c % 2][:]).then_inc(ohT_kept, 1)
            for pr in range(2):
                act.wait_ge(sel_done, pr + 1)
                act.copy(xsel[:, pr, :], sel[pr][:])

        @block.vector
        def _(dve):
            used = [0]

            def junk_slot(width):
                used[0] += 1
                if used[0] > 4:
                    dve.wait_ge(junked, used[0] - 4)
                return junk[:, used[0] % 4, 0:width]

            dve.memset(part[:], 0.0).then_inc(zeroed, 1)
            layernorm_vector(dve, ln, x, lambda b: None)
            dve.wait_ge(w_in, 64)
            dve.wait_ge(ln.normed, NT)
            for t in range(NT):
                dve.scalar_tensor_tensor(out=junk_slot(D), in0=xn[:, t, :], scalar=1.0, in1=wr[:], op0=ALU.mult,
                                         op1=ALU.mult, accum_out=score[:, t:t + 1]).then_inc(junked, 1)
            dve.wait_ge(junked, NT)
            dve.wait_ge(zeroed, 1)
            for b in range(NB):
                dve.wait_ge(row_ready, b + 1)
                bc = row[b % 2]
                for i in range(TPB):
                    t = b * TPB + i
                    own = score[:, t:t + 1]
                    if i > 0:
                        dve.tensor_scalar(junk_slot(i * P), bc[:, 0:i * P], own, None, ALU.is_ge, ALU.add,
                                          accum_out=part[:, t, 0:1]).then_inc(junked, 1)
                    if i < TPB - 1:
                        dve.tensor_scalar(junk_slot(SEQ - (i + 1) * P), bc[:, (i + 1) * P:], own, None,
                                          ALU.is_gt, ALU.add, accum_out=part[:, t, 1:2]).then_inc(junked, 1)
                    mine = bc[:, i * P:(i + 1) * P]
                    dve.tensor_scalar(junk_slot(P), mine, own, None, ALU.is_gt, ALU.add,
                                      accum_out=part[:, t, 2:3]).then_inc(junked, 1)
                    dve.scalar_tensor_tensor(out=junk_slot(P), in0=mine, scalar=own, in1=below[:],
                                             op0=ALU.is_equal, op1=ALU.mult,
                                             accum_out=part[:, t, 3:4]).then_inc(junked, 1)
                dve.wait_ge(junked, used[0])
                dve.tensor_reduce(rank[:, b * TPB:(b + 1) * TPB], part[:, b * TPB:(b + 1) * TPB, :],
                                  AX.X, ALU.add).then_inc(rank_ready, 1)

        @block.gpsimd
        def _(pool):
            pool.wait_ge(w_in, 64)
            pool.wait_ge(ln.normed, NT)
            pool.tensor_tensor(xh[:], x[:], xn[:], ALU.add)
            for t in range(NT):
                b = t // TPB
                if t % TPB == 0:
                    pool.wait_ge(rank_ready, b + 1)
                pool.tensor_scalar(oh[:, t, :], iota[:, b % 2, :], rank[:, t:t + 1], None,
                                   ALU.is_equal).then_inc(oh_ready, 1)

        @block.tensor
        def _(pe):
            pe.wait_ge(w_in, 64)
            pe.wait_ge(junked, NT)

            def rows(b):
                for i in range(TPB):
                    t = b * TPB + i
                    last = pe.transpose(row[b % 2][:, i * P:(i + 1) * P],
                                        score[:, t:t + 1].broadcast_to([P, P]), ident[:])
                last.then_inc(row_ready, 1)

            rows(0)
            rows(1)
            for b in range(NB):
                for i in range(TPB):
                    t = b * TPB + i
                    pe.wait_ge(oh_ready, t + 1)
                    last = pe.matmul(sel[b // 2][:], oh[:, t, :], xn[:, t, :], start=t % (2 * TPB) == 0,
                                     stop=t % (2 * TPB) == 2 * TPB - 1)
                    if t % (2 * TPB) == 2 * TPB - 1:
                        last.then_inc(sel_done, 1)
                if b + 2 < NB:
                    rows(b + 2)
                for c in (2 * b, 2 * b + 1):
                    if c >= 2:
                        pe.wait_ge(ohT_kept, c - 1)
                    for k in range(4):
                        last = pe.transpose(tps[c % 2][:, k, :], oh[:, 4 * c + k, :], ident[:])
                    last.then_inc(ohT_done, 1)


def picked_block(st, io, tag, x, ohT, xsel, xh):
    nc = st.nc
    QK = 2 * CAP
    with ExitStack() as s:
        def sb(name, shape):
            return st.sb(s, tag + name, shape)

        def sem(name):
            return st.sem(tag + name)

        ident = sb("ident2", [P, P])
        g = sb("g", [P, 2, D])
        wqkv = sb("wqkv", [P, 3, D])
        wout, w12 = sb("wout", [P, D]), sb("w12", [P, 2, 3 * P])
        w3 = sb("w3", [P, 3, D])
        headm, pairm = sb("headm", [P, HA]), sb("pairm", [P, D])
        causal = sb("causal", [P, CAP])
        sq, ss, ve = sb("sq", [P, 2, D]), sb("ss", [P, 2]), sb("ve", [P, 2])
        sd, r0, t0, t1, rms = (sb(n, [P, 2]) for n in ("sd", "r0", "t0", "t1", "rms"))
        hn, hnT, qT = sb("hn", [P, 2, D]), sb("hnT", [P, 2, QK]), sb("qT", [P, 2 * QK])
        kx, vx = sb("kx", [P, NB, HA, CAP]), sb("vx", [P, NB, D])
        sm, mx = sb("sm", [P, 2, HA, CAP]), sb("mx", [P, 2, HA])
        pr_, dn, rd = sb("pr", [P, 2, HA, CAP]), sb("dn", [P, 2, HA]), sb("rd", [P, 2, HA])
        pT = sb("pT", [P, 2, HA // 2, P])
        o, oT = sb("o", [P, 2, D]), sb("oT", [P, 2, QK])
        xa, mid = sb("xa", [P, 2, D]), sb("mid", [P, 2, D])
        e, u = sb("e", [P, 3, 2 * QK]), sb("u", [P, 3, 2 * QK])
        delta = sb("delta", [P, 2, D])
        twice = sb("twice", [P, NB, 2, CAP])
        A, B, C, E = (st.ps(s, tag + n, [P, CH]) for n in "ABCE")
        wide = [st.ps(s, f"{tag}wide{i}", [P, SEQ]) for i in range(2)]
        w_in, step, var_ready, root_ready = sem("w2_in"), sem("step"), sem("var_ready"), sem("root_ready")
        twice_kept = sem("twice_kept")
        hn_ready, hnT_done, hnT_kept, qkv_done = (sem("hn_ready"), sem("hnT_done"), sem("hnT_kept"),
                                                  sem("qkv_done"))
        qT_kept, kx_ready, vx_ready, att_done = sem("qT_kept"), sem("kx_ready"), sem("vx_ready"), sem("att_done")
        shifted, exped, probs_ready = sem("shifted"), sem("exped"), sem("probs_ready")
        pT_done, pT_kept, o_done, o_kept = sem("pT_done"), sem("pT_kept"), sem("o_done"), sem("o_kept")
        oT_done, oT_kept, xa_done = sem("oT_done"), sem("oT_kept"), sem("xa_done")
        up_done, up_exped, u_ready, ff_done = sem("up_done"), sem("up_exped"), sem("u_ready"), sem("ff_done")
        delta_ready, put_done, put_read = sem("delta_ready"), sem("put_done"), sem("put_read")
        block = s.enter_context(nc.Block())
        LOADS = 10

        @block.sync
        def _(sp):
            for to, name in ((ident, "ident"), (g, "g"), (wqkv, "fqkv_T"), (wout, "fout_T"), (w12, "w12_T"),
                             (w3, "w3_T"), (headm, "headm"), (pairm, "pairm"), (causal, "causal")):
                src = io[name]
                sp.dma_start(to[:], src.broadcast_to([P, 2, D]) if name == "g" else src).then_inc(w_in, 16)

        @block.vector
        def _(dve):
            chain = [0]

            def chained(ins):
                ins.then_inc(step, 1)
                chain[0] += 1
                dve.wait_ge(step, chain[0])

            def rms_rows(src, half):
                for pr in range(2):
                    last = dve.scalar_tensor_tensor(out=sq[:, pr, :], in0=src[:, pr, :], scalar=1.0, in1=src[:, pr, :],
                                                    op0=ALU.mult, op1=ALU.mult, accum_out=ss[:, pr:pr + 1])
                chained(last)
                dve.tensor_scalar(ve[:], ss[:], 1.0 / D, RMS_EPS, ALU.mult, ALU.add).then_inc(var_ready, 1)
                dve.wait_ge(root_ready, half + 1)
                chained(dve.reciprocal(r0[:], sd[:]))
                newton_rsqrt(dve, step, chain[0], ve, r0, t0, t1, rms)
                chain[0] += 4
                dve.wait_ge(step, chain[0])
                for pr in range(2):
                    last = dve.scalar_tensor_tensor(out=hn[:, pr, :], in0=src[:, pr, :], scalar=rms[:, pr:pr + 1],
                                                    in1=g[:, half, :], op0=ALU.mult, op1=ALU.mult)
                last.then_inc(hn_ready, 1)

            dve.wait_ge(w_in, 16 * (LOADS - 1))
            rms_rows(xsel, 0)
            dve.wait_ge(qkv_done, 1)
            for b in range(NB):
                k = E[:, b * CAP:(b + 1) * CAP][:, None, :].broadcast_to([P, HA, CAP])
                dve.tensor_tensor(kx[:, b, :, :], k, headm[:, :, None].broadcast_to([P, HA, CAP]),
                                  ALU.mult).then_inc(kx_ready, 1)
            dve.tensor_tensor(vx[:], C[:].rearrange("p (b d) -> p b d", b=NB),
                              pairm[:, None, :].broadcast_to([P, NB, D]), ALU.mult).then_inc(vx_ready, 1)
            for pr in range(2):
                dve.wait_ge(att_done, pr + 1)
                w = wide[pr][:].rearrange("p (h k) -> p h k", h=HA)
                chained(dve.tensor_tensor(sm[:, pr], w, causal[:, None, :].broadcast_to([P, HA, CAP]), ALU.add))
                chained(dve.tensor_reduce(mx[:, pr], sm[:, pr], AX.X, ALU.max))
                dve.tensor_tensor(sm[:, pr], sm[:, pr], mx[:, pr, :, None].broadcast_to([P, HA, CAP]),
                                  ALU.subtract).then_inc(shifted, 1)
            for pr in range(2):
                dve.wait_ge(exped, pr + 1)
                chained(dve.tensor_reduce(dn[:, pr], pr_[:, pr], AX.X, ALU.add))
                chained(dve.reciprocal(rd[:, pr], dn[:, pr]))
                dve.tensor_tensor(pr_[:, pr], pr_[:, pr], rd[:, pr, :, None].broadcast_to([P, HA, CAP]),
                                  ALU.mult).then_inc(probs_ready, 1)
            dve.wait_ge(o_done, 1)
            dve.tensor_copy(o[:], A[:, 0:2 * D].rearrange("p (r d) -> p r d", r=2)).then_inc(o_kept, 1)
            dve.wait_ge(xa_done, 1)
            chained(dve.tensor_copy(xa[:], C[:, 0:2 * D].rearrange("p (r d) -> p r d", r=2)))
            chained(dve.tensor_tensor(mid[:], xsel[:], xa[:], ALU.add))
            rms_rows(mid, 1)
            dve.wait_ge(up_exped, 1)
            chained(dve.tensor_scalar(e[:], e[:], 1.0, None, ALU.add))
            chained(dve.reciprocal(e[:], e[:]))
            a3, b3 = (w[:, 0:6 * QK].rearrange("p (c t) -> p c t", c=3) for w in wide)
            chained(dve.tensor_tensor(e[:], a3, e[:], ALU.mult))
            dve.tensor_tensor(u[:], b3, e[:], ALU.mult).then_inc(u_ready, 1)
            dve.wait_ge(ff_done, 1)
            dve.tensor_tensor(delta[:], A[:, 0:2 * D].rearrange("p (r d) -> p r d", r=2), xa[:],
                              ALU.add).then_inc(delta_ready, 1)
            for c in range(NCH):
                dve.wait_ge(put_done, c + 1)
                dve.tensor_tensor(x[:, 4 * c:4 * c + 4, :],
                                  (B, C, E)[c % 3][:].rearrange("p (k d) -> p k d", k=4),
                                  xh[:, 4 * c:4 * c + 4, :], ALU.add).then_inc(put_read, 1)

        @block.scalar
        def _(act):
            def root(half):
                act.wait_ge(var_ready, half + 1)
                act.activation(sd[:], ve[:], ACT.Sqrt).then_inc(root_ready, 1)

            root(0)
            act.wait_ge(hnT_done, 1)
            act.copy(twice[:], A[:, 0:2 * QK].rearrange("p (b t) -> p b t", b=NB)[:, :, None, :]
                     .broadcast_to([P, NB, 2, CAP])).then_inc(twice_kept, 1)
            act.copy(hnT[:], A[:, 0:2 * QK].rearrange("p (r t) -> p r t", r=2)).then_inc(hnT_kept, 1)
            act.wait_ge(qkv_done, 1)
            act.copy(qT[:], B[:, 0:2 * QK]).then_inc(qT_kept, 1)
            for pr in range(2):
                act.wait_ge(shifted, pr + 1)
                act.activation(pr_[:, pr], sm[:, pr], ACT.Exp).then_inc(exped, 1)
            for pr in range(2):
                act.wait_ge(pT_done, pr + 1)
                act.copy(pT[:, pr], wide[pr][:].rearrange("p (h t) -> p h t", t=P)).then_inc(pT_kept, 1)
            act.wait_ge(oT_done, 1)
            act.copy(oT[:], B[:, 0:2 * QK].rearrange("p (r t) -> p r t", r=2)).then_inc(oT_kept, 1)
            root(1)
            act.wait_ge(hnT_done, 2)
            act.copy(hnT[:], E[:, 0:2 * QK].rearrange("p (r t) -> p r t", r=2)).then_inc(hnT_kept, 1)
            act.wait_ge(up_done, 1)
            act.activation(e[:], wide[0][:, 0:6 * QK].rearrange("p (c t) -> p c t", c=3), ACT.Exp,
                           scale=-1.0).then_inc(up_exped, 1)

        @block.tensor
        def _(pe):
            def turned(half, to):
                pe.wait_ge(hn_ready, half + 1)
                for pr in range(2):
                    last = pe.transpose(to[:, pr * QK:(pr + 1) * QK], hn[:, pr, :], ident[:])
                last.then_inc(hnT_done, 1)
                pe.wait_ge(hnT_kept, half + 1)

            pe.wait_ge(w_in, 16 * (LOADS - 1))
            turned(0, A)
            pe.matmul(B[:, 0:2 * QK], wqkv[:, 0, :], hnT[:], start=True, stop=True)
            pe.matmul(E[:, 0:2 * QK], wqkv[:, 1, :], hnT[:], start=True, stop=True)
            pe.wait_ge(twice_kept, 1)
            for b in range(NB):
                last = pe.matmul(C[:, b * D:(b + 1) * D], twice[:, b, :, :], wqkv[:, 2, :], start=True, stop=True)
            last.then_inc(qkv_done, 1)
            pe.wait_ge(qT_kept, 1)
            for pr in range(2):
                pe.wait_ge(kx_ready, 2 * pr + 2)
                for b in (2 * pr, 2 * pr + 1):
                    rows = slice((b % 2) * CAP, (b % 2 + 1) * CAP)
                    for c in range(2):
                        last = pe.matmul(wide[pr][rows, c * CH:(c + 1) * CH], qT[:, b * CAP:(b + 1) * CAP],
                                         kx[:, b, c * HA // 2:(c + 1) * HA // 2, :], start=True, stop=True)
                last.then_inc(att_done, 1)
            for pr in range(2):
                pe.wait_ge(probs_ready, pr + 1)
                for h in range(HA // 2):
                    last = pe.transpose(wide[pr][:, h * P:(h + 1) * P], pr_[:, pr, 2 * h:2 * h + 2, :], ident[:])
                last.then_inc(pT_done, 1)
            pe.wait_ge(vx_ready, 1)
            for pr in range(2):
                pe.wait_ge(pT_kept, pr + 1)
                for b in (2 * pr, 2 * pr + 1):
                    rows = slice((b % 2) * CAP, (b % 2 + 1) * CAP)
                    for h in range(HA // 2):
                        last = pe.matmul(A[rows, pr * D + 2 * h * HDA:pr * D + 2 * (h + 1) * HDA],
                                         pT[:, pr, h, rows], vx[:, b, 2 * h * HDA:2 * (h + 1) * HDA],
                                         start=True, stop=True)
            last.then_inc(o_done, 1)
            pe.wait_ge(o_kept, 1)
            for pr in range(2):
                last = pe.transpose(B[:, pr * QK:(pr + 1) * QK], o[:, pr, :], ident[:])
            last.then_inc(oT_done, 1)
            pe.wait_ge(oT_kept, 1)
            for pr in range(2):
                last = pe.matmul(C[:, pr * D:(pr + 1) * D], oT[:, pr, :], wout[:], start=True, stop=True)
            last.then_inc(xa_done, 1)
            turned(1, E)
            for i in range(2):
                for c in range(3):
                    last = pe.matmul(wide[i][:, c * 2 * QK:(c + 1) * 2 * QK], w12[:, i, c * P:(c + 1) * P], hnT[:],
                                     start=True, stop=True)
            last.then_inc(up_done, 1)
            pe.wait_ge(u_ready, 1)
            for pr in range(2):
                for c in range(3):
                    last = pe.matmul(A[:, pr * D:(pr + 1) * D], u[:, c, pr * QK:(pr + 1) * QK], w3[:, c, :],
                                     start=c == 0, stop=c == 2)
            last.then_inc(ff_done, 1)
            pe.wait_ge(delta_ready, 1)
            for c in range(NCH):
                if c >= 3:
                    pe.wait_ge(put_read, c - 2)
                for k in range(4):
                    t = 4 * c + k
                    last = pe.matmul((B, C, E)[c % 3][:, k * D:(k + 1) * D], ohT[:, t, :],
                                     delta[:, t // (2 * TPB), :], start=True, stop=True)
                last.then_inc(put_done, 1)


def feed_forward(st, io, tag, x):
    with ExitStack() as s:
        ohT = st.sb(s, tag + "ohT", [P, NT, P])
        xsel = st.sb(s, tag + "xsel", [P, 2, D])
        xh = st.sb(s, tag + "xh", [P, NT, D])
        with ExitStack() as r:
            xn = st.sb(r, tag + "xn", [P, NT, D])
            oh = st.sb(r, tag + "oh", [P, NT, P])
            route(st, io, tag, x, xn, oh, ohT, xsel, xh)
        picked_block(st, io, tag, x, ohT, xsel, xh)


def prepare_b(st, io, x, q_dram, k_dram, v_all):
    nc = st.nc
    with ExitStack() as s:
        xn = st.sb(s, "b_xn", [P, NT, D])
        ln = LnWork(st, s, "lnb", xn)
        ident = st.sb(s, "b_ident", [P, P])
        wq, wdown = st.sb(s, "b_wq", [P, 2, P]), st.sb(s, "b_wdown", [P, RANK])
        wk, wv = st.sb(s, "b_wk", [RANK, 2, P]), st.sb(s, "b_wv", [RANK, HB * HDB])
        hT = st.sb(s, "b_hT", [P, 2, CH])
        lat = st.sb(s, "b_lat", [RANK, 2, CH])
        parts = st.sb(s, "b_parts", [P, 2, 4, 2, CH], F16)
        tps = st.ps(s, "b_tps", [P, CH])
        lps = st.ps(s, "b_lps", [RANK, CH])
        qkps = [st.ps(s, f"b_qkps{i}", [P, CH]) for i in range(4)]
        vps = [st.ps(s, f"b_vps{i}", [P, CH]) for i in range(2)]
        w_in, transposed, hT_ready = st.sem("b_w_in"), st.sem("b_transposed"), st.sem("b_hT_ready")
        lat_done, lat_ready, qk_done = st.sem("b_lat_done"), st.sem("b_lat_ready"), st.sem("b_qk_done")
        v_done, hi_made, lo_made = st.sem("b_v_done"), st.sem("b_hi_made"), st.sem("b_lo_made")
        stored = [st.sem(f"b_stored{i}") for i in range(2)]
        block = s.enter_context(nc.Block())
        scale = float(HDB) ** -0.5

        @block.sync
        def _(sp):
            for to, name in ((ident, "ident"), (wq, "bq_T"), (wdown, "bdown_T"), (wk, "bk_T"), (wv, "bv_T")):
                sp.dma_start(to[:], io[name]).then_inc(w_in, 16)
            for c in range(NCH):
                b, at = c // 2, c % 2 * CH
                for i in range(4):
                    sp.wait_ge(lo_made, 6 * c + i + 1)
                    dram = q_dram if i < 2 else k_dram
                    for part in range(2):
                        h0 = b * HB + i % 2 * 4
                        to = dram[part, h0:h0 + 4].rearrange("h d t -> (h d) t")[:, at:at + CH]
                        sp.dma_start(to, parts[:, c % 2, i, part, :]).then_inc(stored[c % 2], 16)
            for i in range(2):
                sp.wait_ge(stored[i], 16 * 8 * NCH // 2)

        @block.tensor
        def _(pe):
            pe.wait_ge(w_in, 80)
            for c in range(NCH):
                pe.wait_ge(ln.normed, 4 * c + 4)
                for k in range(4):
                    if c and k == 0:
                        pe.wait_ge(hT_ready, c)
                    last = pe.transpose(tps[:, k * P:(k + 1) * P], xn[:, 4 * c + k, :], ident[:])
                last.then_inc(transposed, 1)
                pe.wait_ge(hT_ready, c + 1)
                if c:
                    pe.wait_ge(lat_ready, c)
                pe.matmul(lps[:], wdown[:], hT[:, c % 2, :], start=True, stop=True).then_inc(lat_done, 1)
                for i in range(2):
                    if c:
                        pe.wait_ge(lo_made, 6 * (c - 1) + i + 1)
                    pe.matmul(qkps[i][:], wq[:, i, :], hT[:, c % 2, :], start=True, stop=True).then_inc(qk_done, 1)
                pe.wait_ge(lat_ready, c + 1)
                for i in range(2):
                    if c:
                        pe.wait_ge(lo_made, 6 * (c - 1) + i + 3)
                    pe.matmul(qkps[2 + i][:], wk[:, i, :], lat[:, c % 2, :], start=True,
                              stop=True).then_inc(qk_done, 1)
                for i in range(2):
                    if c:
                        pe.wait_ge(lo_made, 6 * (c - 1) + i + 5)
                    for k in range(2):
                        tok = (2 * i + k) * P
                        last = pe.matmul(vps[i][:, k * 256:(k + 1) * 256], lat[:, c % 2, tok:tok + P], wv[:],
                                         start=True, stop=True)
                    last.then_inc(v_done, 1)

        def v_view(c, i, part):
            b, j = c // 2, c % 2 * 4 + 2 * i
            return v_all[:, b * HB:(b + 1) * HB, j:j + 2, part * HDB:(part + 1) * HDB].rearrange(
                "p h j d -> p j h d")

        @block.scalar
        def _(act):
            layernorm_scalar(act, ln)
            for c in range(NCH):
                act.wait_ge(transposed, c + 1)
                if c >= 2:
                    act.wait_ge(qk_done, 4 * (c - 2) + 2)
                act.copy(hT[:, c % 2, :], tps[:]).then_inc(hT_ready, 1)
                act.wait_ge(lat_done, c + 1)
                if c >= 2:
                    act.wait_ge(v_done, 2 * (c - 1))
                act.copy(lat[:, c % 2, :], lps[:]).then_inc(lat_ready, 1)
                for i in range(4):
                    act.wait_ge(qk_done, 4 * c + i + 1)
                    if i == 0 and c >= 2:
                        act.wait_ge(stored[c % 2], 16 * 8 * (c // 2))
                    act.activation(parts[:, c % 2, i, 0, :], qkps[i][:], ACT.Copy,
                                   scale=scale if i < 2 else 1.0).then_inc(hi_made, 1)
                for i in range(2):
                    act.wait_ge(v_done, 2 * c + i + 1)
                    src = vps[i][:].rearrange("p (j h d) -> p j h d", j=2, h=HB)
                    for k in range(2):
                        last = act.copy(v_view(c, i, 0)[:, k], src[:, k])
                    last.then_inc(hi_made, 1)

        @block.vector
        def _(dve):
            layernorm_vector(dve, ln, x, lambda b: None)
            for c in range(NCH):
                for i in range(4):
                    dve.wait_ge(hi_made, 6 * c + i + 1)
                    dve.scalar_tensor_tensor(out=parts[:, c % 2, i, 1, :], in0=qkps[i][:],
                                             scalar=scale if i < 2 else 1.0, in1=parts[:, c % 2, i, 0, :],
                                             op0=ALU.mult, op1=ALU.subtract).then_inc(lo_made, 1)
                for i in range(2):
                    dve.wait_ge(hi_made, 6 * c + i + 5)
                    src = vps[i][:].rearrange("p (j h d) -> p j h d", j=2, h=HB)
                    for k in range(2):
                        last = dve.tensor_tensor(v_view(c, i, 1)[:, k], src[:, k], v_view(c, i, 0)[:, k],
                                                 ALU.subtract)
                    last.then_inc(lo_made, 1)


def project_b(st, io, x, oT):
    nc = st.nc
    with ExitStack() as s:
        wo = st.sb(s, "pb_wo", [P, HB // 2, D])
        y = [st.ps(s, f"pb_y{i}", [P, 4, D]) for i in range(2)]
        w_in, y_done, y_read = st.sem("pb_w_in"), st.sem("pb_y_done"), st.sem("pb_y_read")
        block = s.enter_context(nc.Block())

        @block.sync
        def _(sp):
            sp.dma_start(wo[:], io["wo_T"]).then_inc(w_in, 16)

        @block.tensor
        def _(pe):
            pe.wait_ge(w_in, 16)
            for c in range(NCH):
                if c >= 2:
                    pe.wait_ge(y_read, c - 1)
                for k in range(4):
                    b, at = c // 2, (c % 2 * 4 + k) * P
                    for h in range(HB // 2):
                        col = (b * HB // 2 + h) * SEQ + at
                        last = pe.matmul(y[c % 2][:, k, :], oT[:, col:col + P], wo[:, h, :],
                                         start=h == 0, stop=h == HB // 2 - 1)
                last.then_inc(y_done, 1)

        @block.vector
        def _(dve):
            for c in range(NCH):
                dve.wait_ge(y_done, c + 1)
                dve.scalar_tensor_tensor(out=x[:, 4 * c:4 * c + 4, :], in0=y[c % 2][:], scalar=1.0 / PSCALE,
                                         in1=x[:, 4 * c:4 * c + 4, :], op0=ALU.mult,
                                         op1=ALU.add).then_inc(y_read, 1)


def store_x(st, x, out):
    nc = st.nc
    stored = st.sem("stored")
    with nc.Block() as block:
        @block.sync
        def _(sp):
            for b in range(NB):
                sp.dma_start(out[b].rearrange("(t p) d -> p t d", p=P),
                             x[:, b * TPB:(b + 1) * TPB, :]).then_inc(stored, 16)
            sp.wait_ge(stored, 16 * NB)


def build(nc, io, out, stage=4):
    with ExitStack() as whole:
        st = Store(nc, whole)
        x = st.sb(whole, "x", [P, NT, D])
        with ExitStack() as s:
            qT = st.sb(s, "qT", [P, NTOK])
            v = st.sb(s, "v", [P, NTOK])
            khi = st.sb(s, "khi", [P, NTOK], F16)
            klo = st.sb(s, "klo", [P, NTOK], F16)
            wpre = st.sb(s, "wpre", [P, HA])
            wpost = st.sb(s, "wpost", [P, HA * D])
            prepare_a(st, io, x, qT, v, khi, klo, wpre, wpost)
            accT = st.sb(s, "accT", [P, NTOK])
            identa = st.sb(s, "identa", [P, P])
            zero_and_load(st, io, accT, identa)
            attend(st, "a", (qT, v, khi, klo, wpre, wpost, accT), identa)
            project_a(st, io, x, accT)
        st.end_stage()
        if stage > 1:
            feed_forward(st, io, "f1_", x)
            st.end_stage()
        if stage > 2:
            q_dram = nc.dram_tensor("q_parts", (2, NB * HB, HDB, SEQ), F16, kind="Internal").ap()
            k_dram = nc.dram_tensor("k_parts", (2, NB * HB, HDB, SEQ), F16, kind="Internal").ap()
            with ExitStack() as s:
                v_all = st.sb(s, "v_all", [P, NB * HB, JB, 2 * HDB], F16)
                prepare_b(st, io, x, q_dram, k_dram, v_all)
                oT = st.sb(s, "oT", [P, NB * HB // 2 * SEQ])
                identb = st.sb(s, "identb", [P, P])
                load_ident(st, io, identb)
                attend(st, "b", (q_dram, k_dram, v_all, oT), identb)
                project_b(st, io, x, oT)
            st.end_stage()
        if stage > 3:
            feed_forward(st, io, "f2_", x)
        store_x(st, x, out)


def load_ident(st, io, ident):
    loaded = st.sem("zb_loaded")
    with st.nc.Block() as block:
        @block.sync
        def _(sp):
            sp.dma_start(ident[:], io["ident"]).then_inc(loaded, 16)
            sp.wait_ge(loaded, 16)


def zero_and_load(st, io, accT, ident):
    loaded = st.sem("z_loaded")
    with st.nc.Block() as block:
        @block.vector
        def _(dve):
            dve.memset(accT[:], 0.0)

        @block.sync
        def _(sp):
            sp.dma_start(ident[:], io["ident"]).then_inc(loaded, 16)
            sp.wait_ge(loaded, 16)


def layouts(i):
    f = np.float32
    rows = np.ascontiguousarray
    wqkv, bqkv = i["L0_attn_a_Wqkv"], i["L0_attn_a_bqkv"]
    half = HDA // 2
    partner = np.arange(D).reshape(HA, 2, half)[:, ::-1].reshape(D)
    q, k = np.arange(D), D + np.arange(D)
    picks = [q, q[partner], k, k[partner]]
    inv = (f(1.0) / np.power(f(10000.0), np.arange(0, HDA, 2, dtype=f) / f(HDA))).astype(f)
    ang = np.arange(SEQ, dtype=f)[:, None] * inv[None, :]
    cos, sin = np.cos(ang).T, np.sin(ang).T
    sq = f(HDA) ** f(-0.5)
    rope = np.stack([np.tile(np.concatenate([cos, cos]), (HA, 1)),
                     np.tile(np.concatenate([-sin, sin]), (HA, 1))], axis=1).astype(f)
    rope = np.concatenate([rope * sq, rope], axis=1)

    def pad(w):
        return np.concatenate([w, np.zeros((3 * P - DFF, w.shape[1]), f)])

    return {
        "x": rows(i["L0_attn_a_x"]),
        "ident": np.eye(P, dtype=f),
        "wqk_T": rows(np.stack([wqkv[p].T for p in picks], axis=1)),
        "wv_T": rows(wqkv[2 * D:].T),
        "bqk": rows(np.stack([bqkv[p] for p in picks], axis=1)),
        "bv": rows(bqkv[None, 2 * D:]),
        "rope": rows(rope),
        "wpre": rows(np.repeat(i["L0_attn_a_Wpre"].T, HDA, axis=0)),
        "wpost": rows(np.repeat(i["L0_attn_a_Wpost"].T, HDA, axis=1).reshape(1, -1)),
        "wout_T": rows(i["L0_attn_a_Wout"].T),
        "bout": rows(i["L0_attn_a_bout"][None]),
        "w_router": rows(i["L0_ffn_w_router"][None]),
        "iota": rows(np.broadcast_to(np.stack([np.r_[np.arange(CAP), -np.ones(CAP)],
                                               np.r_[-np.ones(CAP), np.arange(CAP)]]), (P, 2, P)).astype(f)),
        "below": np.tril(np.ones((P, P), f), -1),
        "g": rows(np.stack([i["L0_ffn_g1"], i["L0_ffn_g2"]])[None]),
        "fqkv_T": rows(np.stack([i["L0_ffn_W_qkv"][k * D:(k + 1) * D].T for k in range(3)], axis=1)),
        "fout_T": rows(i["L0_ffn_W_out"].T),
        "w12_T": rows(np.stack([pad(i["L0_ffn_W1"]).T, pad(i["L0_ffn_W2"]).T], axis=1)),
        "w3_T": rows(pad(i["L0_ffn_W3"].T).reshape(3, P, D).transpose(1, 0, 2)),
        "headm": (np.kron(np.eye(HA), np.ones((HDA, 1))) * HDA ** -0.5).astype(f),
        "pairm": np.tile(np.kron(np.eye(2), np.ones((CAP, HDA))), (1, HA // 2)).astype(f),
        "causal": np.tile(np.triu(np.full((CAP, CAP), -1e30), 1), (2, 1)).astype(f),
        "bq_T": rows(i["L0_attn_b_Wq"].T.reshape(D, 2, P)),
        "bdown_T": rows(i["L0_attn_b_Wkv_down"].T),
        "bk_T": rows(i["L0_attn_b_Wk_up"].T.reshape(RANK, 2, P)),
        "bv_T": rows(i["L0_attn_b_Wv_up"].T),
        "wo_T": rows(np.repeat(i["L0_attn_b_Wo"].T.reshape(HB // 2, 2, 1, HDB, D), 2, axis=2)
                     .reshape(HB // 2, P, D).transpose(1, 0, 2)),
    }


def kernel(**inputs):
    import concourse.bacc as bacc
    from concourse.bass_utils import run_bass_kernel_spmd

    arrays = layouts({k: np.asarray(v) for k, v in inputs.items()})
    nc = bacc.Bacc("TRN2", target_bir_lowering=False, num_devices=1)
    io = {n: nc.dram_tensor(n + "_dram", a.shape, mybir.dt.from_np(a.dtype), kind="ExternalInput").ap()
          for n, a in arrays.items()}
    out = nc.dram_tensor("out_dram", (NB, SEQ, D), F32, kind="ExternalOutput").ap()
    build(nc, io, out)
    result = run_bass_kernel_spmd(nc, [{n + "_dram": a for n, a in arrays.items()}], core_ids=[0])
    return result.results[0]["out_dram"]
```

```python
from contextlib import ExitStack

import numpy as np
import concourse.bass as bass
from concourse import mybir

ALU = mybir.AluOpType
ACT = mybir.ActivationFunctionType
AX = mybir.AxisListType
F32 = mybir.dt.float32
F16 = mybir.dt.float16

P = 128
NB, SEQ, D = 4, 1024, 128
TPB = SEQ // P
NT = NB * TPB
NTOK = NB * SEQ
CH = 512
NCH = NTOK // CH
HA, HDA = 16, 8
HB, HDB = 8, 32
RANK = 64
CAP = 64
DFF = 341
HALF = SEQ // 2
UNITS = 4
TILES = 4
JB = SEQ // P
TURN_T = UNITS * TILES
TURN_J = UNITS * JB
AHEAD = 6
AHEAD_A = 10
LAG = 2
PSCALE = 2.0 ** 14
K_LOAD_AT = 8
LN_EPS, RMS_EPS = 1e-5, 1e-6


def wait_apart(eng, passed, sem, value):
    eng.wait_ge(sem, value)
    eng.sem_inc(passed, 1)


class Store:

    def __init__(self, nc, stack):
        self.nc, self.stack, self.stage_sems = nc, stack, []

    def sem(self, name):
        self.stage_sems.append(self.nc.alloc_semaphore(name=name))
        return self.stage_sems[-1]

    def end_stage(self):
        self.nc.all_engine_barrier()
        self.nc.clear_and_free_semaphores(self.stage_sems)
        self.nc.all_engine_barrier()
        self.stage_sems = []

    def sb(self, stack, name, shape, dt=F32):
        return stack.enter_context(self.nc.sbuf_tensor(name, shape, dt))

    def ps(self, stack, name, shape, dt=F32):
        return stack.enter_context(self.nc.psum_tensor(name, shape, dt))


class LnWork:

    def __init__(self, st, stack, tag, xn):
        self.stats = st.sb(stack, tag + "_stats", [P, NT, 6])
        self.mv = st.sb(stack, tag + "_mv", [P, NT, 2])
        self.ve = st.sb(stack, tag + "_ve", [P, NT])
        self.sd = st.sb(stack, tag + "_sd", [P, NT])
        self.r0 = st.sb(stack, tag + "_r0", [P, NT])
        self.t0 = st.sb(stack, tag + "_t0", [P, NT])
        self.t1 = st.sb(stack, tag + "_t1", [P, NT])
        self.rstd = st.sb(stack, tag + "_rstd", [P, NT])
        self.xn = xn
        self.step = st.sem(tag + "_step")
        self.ve_ready = st.sem(tag + "_ve_ready")
        self.sd_ready = st.sem(tag + "_sd_ready")
        self.normed = st.sem(tag + "_normed")


def layernorm_vector(dve, w, x, wait_x):
    for t in range(NT):
        if t % TPB == 0:
            wait_x(t // TPB)
        last = dve.bn_stats(w.stats[:, t, :], x[:, t, :])
    last.then_inc(w.step, 1)
    dve.wait_ge(w.step, 1)
    for t in range(NT):
        last = dve.bn_aggr(w.mv[:, t, :], w.stats[:, t, :])
    last.then_inc(w.step, 1)
    dve.wait_ge(w.step, 2)
    dve.tensor_scalar(w.ve[:], w.mv[:, :, 1], LN_EPS, None, ALU.add).then_inc(w.ve_ready, 1)
    dve.wait_ge(w.sd_ready, 1)
    dve.reciprocal(w.r0[:], w.sd[:]).then_inc(w.step, 1)
    newton_rsqrt(dve, w.step, 3, w.ve, w.r0, w.t0, w.t1, w.rstd)
    dve.wait_ge(w.step, 7)
    for t in range(NT):
        dve.tensor_scalar(w.xn[:, t, :], x[:, t, :], w.mv[:, t, 0:1], w.rstd[:, t:t + 1],
                          ALU.subtract, ALU.mult).then_inc(w.normed, 1)


def newton_rsqrt(dve, step, n, v, r0, t0, t1, out):
    dve.wait_ge(step, n)
    dve.tensor_tensor(t0[:], r0[:], r0[:], ALU.mult).then_inc(step, 1)
    dve.wait_ge(step, n + 1)
    dve.tensor_tensor(t1[:], t0[:], v[:], ALU.mult).then_inc(step, 1)
    dve.wait_ge(step, n + 2)
    dve.tensor_scalar(t0[:], t1[:], -0.5, 1.5, ALU.mult, ALU.add).then_inc(step, 1)
    dve.wait_ge(step, n + 3)
    dve.tensor_tensor(out[:], r0[:], t0[:], ALU.mult).then_inc(step, 1)


def layernorm_scalar(act, w):
    act.wait_ge(w.ve_ready, 1)
    act.activation(w.sd[:], w.ve[:], ACT.Sqrt).then_inc(w.sd_ready, 1)


def prepare_a(st, io, x, qT, v, k_dram, wpre, wpost):
    nc = st.nc
    with ExitStack() as s:
        xn = st.sb(s, "a_xn", [P, NT, D])
        ln = LnWork(st, s, "lna", xn)
        ident = st.sb(s, "a_ident", [P, P])
        wqk = st.sb(s, "a_wqk", [P, 4, D])
        wv = st.sb(s, "a_wv", [P, D])
        bqk = st.sb(s, "a_bqk", [P, 4])
        bv = st.sb(s, "a_bv", [P, D])
        rope = st.sb(s, "a_rope", [P, 4, SEQ])
        hT = st.sb(s, "a_hT", [P, NTOK])
        khi = st.sb(s, "a_khi", [P, NTOK], F16)
        klo = st.sb(s, "a_klo", [P, NTOK], F16)
        prod = st.sb(s, "a_prod", [P, 4, 2, CH])
        kT = st.sb(s, "a_kT", [P, 2, CH])
        tps = [st.ps(s, f"a_tps{i}", [P, CH]) for i in range(2)]
        qkps = [st.ps(s, f"a_qkps{i}", [P, CH]) for i in range(4)]
        vps = [st.ps(s, f"a_vps{i}", [P, CH]) for i in range(2)]
        x_in = [st.sem(f"a_x_in{b}") for b in range(NB)]
        w_in = st.sem("a_w_in")
        transposed, hT_ready = st.sem("a_transposed"), st.sem("a_hT_ready")
        qk_done, prod_ready, qk_summed = st.sem("a_qk_done"), st.sem("a_prod_ready"), st.sem("a_qk_summed")
        k_stored = st.sem("a_k_stored")
        v_done, v_kept, khi_ready, klo_ready = (st.sem("a_v_done"), st.sem("a_v_kept"),
                                                st.sem("a_khi_ready"), st.sem("a_klo_ready"))
        block = s.enter_context(nc.Block())
        LOADS = 8

        @block.sync
        def _(sp):
            for b in range(NB):
                sp.dma_start(x[:, b * TPB:(b + 1) * TPB, :],
                             io["x"][b].rearrange("(t p) d -> p t d", p=P)).then_inc(x_in[b], 16)
            for b in range(NB):
                own = slice(b * SEQ, (b + 1) * SEQ)
                sp.wait_ge(klo_ready, 2 * b + 2)
                sp.dma_start(k_dram[0, :, own], khi[:, own]).then_inc(k_stored, 16)
                sp.dma_start(k_dram[1, :, own], klo[:, own]).then_inc(k_stored, 16)
            sp.wait_ge(k_stored, 32 * NB)

        @block.scalar
        def _(act):
            act.dma_start(ident[:], io["ident"]).then_inc(w_in, 16)
            act.dma_start(wqk[:], io["wqk_T"]).then_inc(w_in, 16)
            act.dma_start(wv[:], io["wv_T"]).then_inc(w_in, 16)
            act.dma_start(bqk[:], io["bqk"]).then_inc(w_in, 16)
            act.dma_start(bv[:], io["bv"].broadcast_to([P, D])).then_inc(w_in, 16)
            act.dma_start(rope[:], io["rope"]).then_inc(w_in, 16)
            act.dma_start(wpre[:], io["wpre"]).then_inc(w_in, 16)
            act.dma_start(wpost[:], io["wpost"].broadcast_to([P, HA * D])).then_inc(w_in, 16)
            layernorm_scalar(act, ln)
            for c in range(NCH + 2):
                if c < NCH:
                    act.wait_ge(transposed, c + 1)
                    act.copy(hT[:, c * CH:(c + 1) * CH], tps[c % 2][:]).then_inc(hT_ready, 1)
                if 1 <= c <= NCH:
                    m = c - 1
                    act.wait_ge(v_done, m + 1)
                    act.copy(v[:, m * CH:(m + 1) * CH], vps[m % 2][:]).then_inc(v_kept, 1)
                if c >= 2:
                    m = c - 2
                    act.wait_ge(qk_summed, 2 * m + 2)
                    act.copy(khi[:, m * CH:(m + 1) * CH], kT[:, m % 2, :]).then_inc(khi_ready, 1)

        @block.tensor
        def _(pe):
            pe.wait_ge(w_in, 16 * LOADS)
            for c in range(NCH + 1):
                if c < NCH:
                    pe.wait_ge(ln.normed, 4 * c + 4)
                    if c >= 2:
                        pe.wait_ge(hT_ready, c - 1)
                    for k in range(4):
                        last = pe.transpose(tps[c % 2][:, k * P:(k + 1) * P], ln.xn[:, 4 * c + k, :], ident[:])
                    last.then_inc(transposed, 1)
                if c >= 1:
                    m = c - 1
                    pe.wait_ge(hT_ready, m + 1)
                    if m >= 2:
                        pe.wait_ge(v_kept, m - 1)
                    for k in range(4):
                        last = pe.matmul(vps[m % 2][:, k * D:(k + 1) * D],
                                         hT[:, m * CH + k * P:m * CH + (k + 1) * P], wv[:],
                                         start=(k == 0), stop=True, skip_group_check=True)
                    last.then_inc(v_done, 1)
                    for i in range(4):
                        if m >= 1:
                            pe.wait_ge(prod_ready, 4 * (m - 1) + i + 1)
                        pe.matmul(qkps[i][:], wqk[:, i, :], hT[:, m * CH:(m + 1) * CH],
                                  start=True, stop=True).then_inc(qk_done, 1)

        @block.vector
        def _(dve):
            layernorm_vector(dve, ln, x, lambda b: dve.wait_ge(x_in[b], 16))
            dve.wait_ge(w_in, 16 * LOADS)
            for c in range(NCH):
                at = (c * CH) % SEQ
                for i in range(4):
                    if c >= 2:
                        dve.wait_ge(qk_summed, 2 * (c - 2) + i // 2 + 1)
                    dve.wait_ge(qk_done, 4 * c + i + 1)
                    dve.scalar_tensor_tensor(out=prod[:, i, c % 2, :], in0=qkps[i][:], scalar=bqk[:, i:i + 1],
                                             in1=rope[:, i, at:at + CH], op0=ALU.add,
                                             op1=ALU.mult).then_inc(prod_ready, 1)
            for c in range(NCH):
                dve.wait_ge(v_kept, c + 1)
                vv = v[:, c * CH:(c + 1) * CH].rearrange("p (k d) -> p k d", k=4)
                dve.tensor_tensor(vv, vv, bv[:, None, :].broadcast_to([P, 4, D]), ALU.add)

        @block.gpsimd
        def _(pool):
            for c in range(NCH):
                pool.wait_ge(prod_ready, 4 * c + 2)
                pool.tensor_tensor(qT[:, c * CH:(c + 1) * CH], prod[:, 0, c % 2, :], prod[:, 1, c % 2, :],
                                   ALU.add).then_inc(qk_summed, 1)
                pool.wait_ge(prod_ready, 4 * c + 4)
                if c >= 2:
                    pool.wait_ge(khi_ready, c - 1)
                pool.tensor_tensor(kT[:, c % 2, :], prod[:, 2, c % 2, :], prod[:, 3, c % 2, :],
                                   ALU.add).then_inc(qk_summed, 1)
                pool.wait_ge(khi_ready, c + 1)
                pool.wait_ge(qk_summed, 2 * c + 2)
                pool.tensor_tensor(klo[:, c * CH:(c + 1) * CH], kT[:, c % 2, :], khi[:, c * CH:(c + 1) * CH],
                                   ALU.subtract).then_inc(klo_ready, 1)


def attend_a(st, qT, v, k_dram, wpre, wpost, accT):
    nc = st.nc
    heads = NB * HA
    turns = heads // 2
    tpb = turns // NB
    with ExitStack() as s:
        probs = st.sb(s, "a_probs", [P, 4, SEQ])
        parts = st.sb(s, "a_parts", [P, 4, 2, SEQ], F16)
        pT = st.sb(s, "a_pT", [P, UNITS, 2, JB, HALF], F16)
        negmax = st.sb(s, "a_negmax", [P, TURN_T])
        den = st.sb(s, "a_den", [P, TURN_T])
        dens = st.sb(s, "a_dens", [P, TURN_T])
        rden = st.sb(s, "a_rden", [P, TURN_T])
        kcur = st.sb(s, "a_kcur", [P, 2, SEQ], F16)
        qs = st.sb(s, "a_qs", [P, 2, 2, SEQ], F16)
        qtmp = st.sb(s, "a_qtmp", [P, SEQ])
        vs = st.sb(s, "a_vs", [P, 2, 2, JB, D], F16)
        vtmp = st.sb(s, "a_vtmp", [P, JB, D])
        score_ps = [st.ps(s, f"a_score_ps{i}", [P, SEQ]) for i in range(2)]
        out_ps = [st.ps(s, f"a_out_ps{i}", [P, HALF]) for i in range(2)]

        k_in = st.sem("a_k_in")
        q_scaled = st.sem("a_q_scaled")
        q_step = st.sem("a_q_step")
        v_step = st.sem("a_v_step")
        scored = st.sem("a_scored")
        max_ready = st.sem("a_max_ready")
        exp_done = st.sem("a_exp_done")
        dens_ready = st.sem("a_dens_ready")
        rden_ready = st.sem("a_rden_ready")
        hi_ready = st.sem("a_hi_ready")
        lo_ready = st.sem("a_lo_ready")
        hi_turned = [st.sem(f"a_hi_turned{i}") for i in range(4)]
        lo_turned = [st.sem(f"a_lo_turned{i}") for i in range(4)]
        pv_done = st.sem("a_pv_done")
        out_kept = st.sem("a_out_kept")
        sp_passed = st.sem("a_sp_passed")
        act_passed, pool_passed = st.sem("a_act_passed"), st.sem("a_pool_passed")
        block = s.enter_context(nc.Block())

        @block.sync
        def _(sp):
            def load_k(b):
                for part in range(2):
                    sp.dma_start(kcur[:, part, :], k_dram[part, :, bass.ds(b * SEQ, SEQ)]).then_inc(k_in, 16)

            def transpose_tile(n, t):
                u, k = t // TILES, t % TILES
                if k == 0 and not (isinstance(n, int) and n == 0):
                    wait_apart(sp, sp_passed, pv_done, TURN_J * n - TURN_J + JB * (u + 1))
                T = TURN_T * n + t
                wait_apart(sp, sp_passed, hi_ready, T + 1)
                sp.dma_start_transpose(pT[:, u, 0, :, k * P:(k + 1) * P],
                                       parts[:, k, 0, :]).then_inc(hi_turned[k], 16)
                wait_apart(sp, sp_passed, lo_ready, T + 1)
                sp.dma_start_transpose(pT[:, u, 1, :, k * P:(k + 1) * P],
                                       parts[:, k, 1, :]).then_inc(lo_turned[k], 16)

            load_k(0)
            for t in range(TURN_T):
                transpose_tile(0, t)

            def one_turn(n):
                for t in range(TURN_T):
                    transpose_tile(n, t)

            for b in range(NB):
                with sp.Fori(b * tpb + (b == 0), (b + 1) * tpb - 1) as n:
                    one_turn(n)
                n = (b + 1) * tpb - 1
                for t in range(TURN_T):
                    if t == K_LOAD_AT and b + 1 < NB:
                        sp.wait_ge(scored, TURN_T * (n + 1))
                        load_k(b + 1)
                    transpose_tile(n, t)

        @block.tensor
        def _(pe):
            def scores(n, t):
                n, t = n + t // TURN_T, t % TURN_T
                slot, half, k = t // 8, t // 4 % 2, t % 4
                T = TURN_T * n + t
                if not (isinstance(n, int) and T < 2):
                    pe.wait_ge(exp_done, T - 1)
                cols = slice(half * HALF + k * P, half * HALF + (k + 1) * P)
                out = score_ps[t % 2]
                if t % 8 == 0:
                    pe.wait_ge(q_step, 2 * (2 * n + slot + 1))
                    if slot == 0:
                        pe.wait_ge(k_in, 32 * (n // tpb + 1))
                q0, q1 = qs[:, slot, 0, cols], qs[:, slot, 1, cols]
                for c in range(2):
                    kc = slice(c * CH, (c + 1) * CH)
                    pe.matmul(out[:, kc], q0, kcur[:, 0, kc], start=True, stop=False)
                    pe.matmul(out[:, kc], q0, kcur[:, 1, kc], start=False, stop=False)
                for c in range(2):
                    kc = slice(c * CH, (c + 1) * CH)
                    last = pe.matmul(out[:, kc], q1, kcur[:, 0, kc], start=False, stop=True)
                last.then_inc(scored, 1)

            def times_v(n, j):
                u, jb = j // JB, j % JB
                slot, half = u // 2, u % 2
                if jb == 0:
                    for k in range(TILES):
                        count = 16 * (UNITS * n + u + 1)
                        pe.wait_ge(hi_turned[k], count)
                        pe.wait_ge(lo_turned[k], count)
                    if half == 0:
                        pe.wait_ge(v_step, 3 * (2 * n + slot + 1))
                    if slot == 0 and not (isinstance(n, int) and n == 0):
                        pe.wait_ge(out_kept, 2 * n - 1 + half)
                hi, lo = pT[:, u, 0, jb, :], pT[:, u, 1, jb, :]
                first, final = slot == 0 and jb == 0, slot == 1 and jb == JB - 1
                out = out_ps[half][:]
                pe.matmul(out, vs[:, slot, 0, jb, :], hi, start=first, stop=False, skip_group_check=True)
                pe.matmul(out, vs[:, slot, 0, jb, :], lo, start=False, stop=False, skip_group_check=True)
                pe.matmul(out, vs[:, slot, 1, jb, :], hi, start=False, stop=final,
                          skip_group_check=True).then_inc(pv_done, 1)

            def one_turn(n, last):
                for t in range(TURN_T):
                    if not (last and t + AHEAD_A >= TURN_T):
                        scores(n, t + AHEAD_A)
                    times_v(n, 2 * t)
                    times_v(n, 2 * t + 1)

            for t in range(AHEAD_A):
                scores(0, t)
            one_turn(0, False)
            with pe.Fori(1, turns - 1) as n:
                one_turn(n, False)
            one_turn(turns - 1, True)

        @block.scalar
        def _(act):
            def exponentiate(n, t):
                n, t = n + t // TURN_T, t % TURN_T
                T = TURN_T * n + t
                act.wait_ge(max_ready, T + 1)
                if not (isinstance(n, int) and n == 0 and t < 4):
                    act.wait_ge(lo_ready, T - 3)
                act.activation(probs[:, t % 4, :], score_ps[t % 2][:], ACT.Exp, bias=negmax[:, t:t + 1],
                               accum_out=den[:, t:t + 1]).then_inc(exp_done, 1)
                act.wait_ge(exp_done, T + 1)
                act.mul(dens[:, t:t + 1], den[:, t:t + 1], 1.0 / PSCALE).then_inc(dens_ready, 1)

            def scale_q(g):
                if not (isinstance(g, int) and g == 0):
                    wait_apart(act, act_passed, q_step, 2 * g)
                act.activation(qtmp[:], qT[:, bass.ds((g // HA) * SEQ, SEQ)], ACT.Copy,
                               scale=wpre[:, bass.ds(g % HA, 1)]).then_inc(q_scaled, 1)

            def one_turn(n, last):
                for t in range(AHEAD_A, AHEAD_A + TURN_T):
                    if not (last and t >= TURN_T):
                        exponentiate(n, t)
                        if t % 8 == 2 and not last:
                            scale_q(2 * n + t // 8 + 1)

            scale_q(0)
            for t in range(AHEAD_A):
                exponentiate(0, t)
                if t == 2:
                    scale_q(1)
            one_turn(0, False)
            with act.Fori(1, turns - 1) as n:
                one_turn(n, False)
            one_turn(turns - 1, True)

        @block.vector
        def _(dve):
            def row_max(n, t):
                n, t = n + t // TURN_T, t % TURN_T
                dve.wait_ge(scored, TURN_T * n + t + 1)
                dve.tensor_reduce(negmax[:, t:t + 1], score_ps[t % 2][:], AX.X, ALU.max,
                                  negate=True).then_inc(max_ready, 1)

            def invert(n, t):
                n, t = n + t // TURN_T, t % TURN_T
                dve.wait_ge(dens_ready, TURN_T * n + t + 1)
                dve.reciprocal(rden[:, t:t + 1], dens[:, t:t + 1]).then_inc(rden_ready, 1)

            def low(n, t):
                n, t = n + t // TURN_T, t % TURN_T
                T = TURN_T * n + t
                dve.wait_ge(hi_ready, T + 1)
                if not (isinstance(n, int) and n == 0 and t < 4):
                    dve.wait_ge(lo_turned[t % 4], 16 * (UNITS * n + t // TILES))
                dve.scalar_tensor_tensor(out=parts[:, t % 4, 1, :], in0=probs[:, t % 4, :],
                                         scalar=rden[:, t:t + 1], in1=parts[:, t % 4, 0, :],
                                         op0=ALU.mult, op1=ALU.subtract).then_inc(lo_ready, 1)

            def keep(n, half):
                dve.wait_ge(pv_done, TURN_J * n + (3 + half) * JB)
                to = accT[:, bass.ds((n // tpb) * SEQ + half * HALF, HALF)]
                dve.tensor_tensor(to, out_ps[half][:], to, ALU.add).then_inc(out_kept, 1)

            def one_turn(n, first, last):
                for t in range(TURN_T):
                    ahead = t + AHEAD_A
                    if not (last and ahead >= TURN_T):
                        row_max(n, ahead)
                    if not (last and ahead > TURN_T):
                        invert(n, ahead - 1)
                    if not (last and ahead > TURN_T + 1):
                        low(n, ahead - 2)
                    if t == 1 and not first:
                        keep(n - 1, 1)
                    if t == 13:
                        keep(n, 0)

            for t in range(AHEAD_A):
                row_max(0, t)
                if t > 0:
                    invert(0, t - 1)
                if t > 1:
                    low(0, t - 2)
            one_turn(0, True, False)
            with dve.Fori(1, turns - 1) as n:
                one_turn(n, False, False)
            one_turn(turns - 1, False, True)
            keep(turns - 1, 1)

        @block.gpsimd
        def _(pool):
            def q_part(g, slot, i, first=False):
                if i == 0:
                    wait_apart(pool, pool_passed, q_scaled, g + 1)
                    if not first:
                        wait_apart(pool, pool_passed, scored, 2 * TILES * (g - 1))
                    pool.tensor_scalar(qs[:, slot, 0, :], qtmp[:], 1.0, 1.0, ALU.mult,
                                       ALU.mult).then_inc(q_step, 1)
                else:
                    pool.wait_ge(q_step, 2 * g + 1)
                    pool.tensor_tensor(qs[:, slot, 1, :], qtmp[:], qs[:, slot, 0, :],
                                       ALU.subtract).then_inc(q_step, 1)

            def v_part(g, slot, i, first=False):
                b, h = g // HA, g % HA
                if i == 0:
                    src = v[:, bass.ds(b * SEQ, SEQ)].rearrange("p (j d) -> p j d", j=JB)
                    w = wpost[:, bass.ds(h * D, D)][:, None, :].broadcast_to([P, JB, D])
                    pool.tensor_tensor(vtmp[:], src, w, ALU.mult).then_inc(v_step, 1)
                elif i == 1:
                    wait_apart(pool, pool_passed, v_step, 3 * g + 1)
                    if not first:
                        wait_apart(pool, pool_passed, pv_done, 2 * JB * (g - 1))
                    pool.tensor_scalar(vs[:, slot, 0, :, :], vtmp[:], 1.0, 1.0, ALU.mult,
                                       ALU.mult).then_inc(v_step, 1)
                else:
                    pool.wait_ge(v_step, 3 * g + 2)
                    pool.tensor_tensor(vs[:, slot, 1, :, :], vtmp[:], vs[:, slot, 0, :, :],
                                       ALU.subtract).then_inc(v_step, 1)

            def high(n, t):
                if not (isinstance(n, int) and n == 0 and t < 4):
                    wait_apart(pool, pool_passed, hi_turned[t % 4], 16 * (UNITS * n + t // TILES))
                wait_apart(pool, pool_passed, rden_ready, TURN_T * n + t + 1)
                pool.tensor_scalar(parts[:, t % 4, 0, :], probs[:, t % 4, :], rden[:, t:t + 1], 1.0,
                                   ALU.mult, ALU.mult).then_inc(hi_ready, 1)

            def one_turn(n, first, last):
                for t in range(TURN_T):
                    high(n, t)
                    slot, k = t // 8, t % 8
                    more = not (last and slot == 1)
                    if k == 2 and more:
                        q_part(2 * n + slot + 1, 1 - slot, 0, first and slot == 0)
                    if k == 3 and more:
                        q_part(2 * n + slot + 1, 1 - slot, 1)
                    if k in (4, 5, 6):
                        v_part(2 * n + slot, slot, k - 4, first)

            for i in range(2):
                q_part(0, 0, i, True)
            one_turn(0, True, False)
            with pool.Fori(1, turns - 1) as n:
                one_turn(n, False, False)
            one_turn(turns - 1, False, True)


def attend(st, kind, operands, ident):
    nc = st.nc
    a = kind == "a"
    heads = NB * (HA if a else HB)
    turns = heads // 2
    tpb = turns // NB
    vw = D if a else 2 * HDB
    n_tiles, n_blocks = turns * TURN_T, turns * TURN_J
    with ExitStack() as s:
        probs = st.sb(s, kind + "_probs", [P, TURN_T, SEQ])
        pT = st.sb(s, kind + "_pT", [P, 4, 2, HALF], F16)
        negmax = st.sb(s, kind + "_negmax", [P, TURN_T])
        den = st.sb(s, kind + "_den", [P, TURN_T])
        rden = st.sb(s, kind + "_rden", [P, TURN_T])
        if a:
            qT, v, khi, klo, wpre, wpost, accT = operands
            kcur = st.sb(s, "a_kcur", [P, 2, SEQ], F16)
            qs = st.sb(s, "a_qs", [P, 2, 2, SEQ], F16)
            qtmp = st.sb(s, "a_qtmp", [P, SEQ])
            vs = st.sb(s, "a_vs", [P, 2, 2, JB, D], F16)
            vtmp = st.sb(s, "a_vtmp", [P, JB, D])
        else:
            q_dram, k_dram, v_all, oT = operands
            qs = st.sb(s, "b_qs", [P, 2, SEQ], F16)
            ks = st.sb(s, "b_ks", [P, 2, SEQ], F16)
            vs = st.sb(s, "b_vs", [P, 2, JB, 2 * HDB], F16)
        score_ps = [st.ps(s, f"{kind}_score_ps{i}", [P, SEQ]) for i in range(2)]
        turn_ps = [st.ps(s, f"{kind}_turn_ps{i}", [P, HALF]) for i in range(2)]
        out_ps = [st.ps(s, f"{kind}_out_ps{i}", [P, HALF]) for i in range(2)]

        scored = st.sem(kind + "_scored")
        max_ready = st.sem(kind + "_max_ready")
        exp_done = st.sem(kind + "_exp_done")
        rden_ready = st.sem(kind + "_rden_ready")
        normed = st.sem(kind + "_normed")
        turned = st.sem(kind + "_turned")
        hi_ready = st.sem(kind + "_hi_ready")
        lo_ready = st.sem(kind + "_lo_ready")
        pv_done = st.sem(kind + "_pv_done")
        out_kept = st.sem(kind + "_out_kept")
        k_in = [st.sem(f"{kind}_k_in{i}") for i in range(2)]
        q_step = st.sem(kind + "_q_step")
        v_step = st.sem(kind + "_v_step")
        q_scaled = st.sem(kind + "_q_scaled")
        VS = 3 if a else 1
        act_passed, pool_passed = st.sem(kind + "_act_passed"), st.sem(kind + "_pool_passed")
        block = s.enter_context(nc.Block())

        if a:
            @block.sync
            def _(sp):
                for b in range(NB):
                    if b >= 1:
                        sp.wait_ge(scored, b * HA * 2 * TILES)
                    sp.dma_start(kcur[:, 0, :], khi[:, b * SEQ:(b + 1) * SEQ]).then_inc(k_in[0], 16)
                    sp.dma_start(kcur[:, 1, :], klo[:, b * SEQ:(b + 1) * SEQ]).then_inc(k_in[0], 16)
        else:
            @block.sync
            def _(sp):
                def load_head(g, slot):
                    for part in range(4):
                        rows = slice(part * HDB, (part + 1) * HDB)
                        sp.dma_start(qs[rows, slot, :], q_dram[part // 2, bass.ds(g, 1)]
                                     .rearrange("o d t -> (o d) t")).then_inc(k_in[slot], 16)
                        sp.dma_start(ks[rows, slot, :], k_dram[part % 2, bass.ds(g, 1)]
                                     .rearrange("o d t -> (o d) t")).then_inc(k_in[slot], 16)
                load_head(0, 0)
                load_head(1, 1)
                with sp.Fori(1, turns) as n:
                    for slot in range(2):
                        sp.wait_ge(scored, TURN_T * n - TURN_T + 2 * TILES * (slot + 1))
                        load_head(2 * n + slot, slot)

        @block.tensor
        def _(pe):
            def scores(n, t):
                n, t = n + t // TURN_T, t % TURN_T
                slot, half, k = t // 8, t // 4 % 2, t % 4
                T = TURN_T * n + t
                if not (isinstance(n, int) and T < 2):
                    pe.wait_ge(exp_done, T - 1)
                cols = slice(half * HALF + k * P, half * HALF + (k + 1) * P)
                out = score_ps[t % 2]
                if a:
                    if t % 8 == 0:
                        pe.wait_ge(q_step, 2 * (2 * n + slot + 1))
                        if slot == 0:
                            pe.wait_ge(k_in[0], 32 * (n // tpb + 1))
                    q0, q1 = qs[:, slot, 0, cols], qs[:, slot, 1, cols]
                    for c in range(2):
                        kc = slice(c * CH, (c + 1) * CH)
                        pe.matmul(out[:, kc], q0, kcur[:, 0, kc], start=True, stop=False)
                        pe.matmul(out[:, kc], q0, kcur[:, 1, kc], start=False, stop=False)
                    for c in range(2):
                        kc = slice(c * CH, (c + 1) * CH)
                        last = pe.matmul(out[:, kc], q1, kcur[:, 0, kc], start=False, stop=True)
                else:
                    if t % 8 == 0:
                        pe.wait_ge(k_in[slot], 128 * (n + 1))
                    for c in range(2):
                        kc = slice(c * CH, (c + 1) * CH)
                        last = pe.matmul(out[:, kc], qs[:, slot, cols], ks[:, slot, kc], start=True, stop=True)
                last.then_inc(scored, 1)

            def turn(n, j):
                u, jb = j // JB, j % JB
                if jb == 0:
                    pe.wait_ge(normed, TURN_T * n + TILES * (u + 1))
                if not (isinstance(n, int) and n == 0 and j < 2):
                    pe.wait_ge(lo_ready, TURN_J * n + j - 1)
                for k in range(TILES):
                    last = pe.transpose(turn_ps[j % 2][:, k * P:(k + 1) * P],
                                        probs[:, TILES * u + k, jb * P:(jb + 1) * P], ident[:])
                last.then_inc(turned, 1)

            def times_v(n, j):
                n, j = n + j // TURN_J, j % TURN_J
                u, jb = j // JB, j % JB
                slot, half = u // 2, u % 2
                pe.wait_ge(lo_ready, TURN_J * n + j + 1)
                if jb == 0:
                    if half == 0:
                        pe.wait_ge(v_step, VS * (2 * n + slot + 1))
                    if a and slot == 0 and not (isinstance(n, int) and n == 0):
                        pe.wait_ge(out_kept, 2 * n - 1 + half)
                    if not a and not (isinstance(n, int) and n == 0 and slot == 0):
                        pe.wait_ge(out_kept, UNITS * n + u - 1)
                hi, lo = pT[:, j % 4, 0, :], pT[:, j % 4, 1, :]
                if a:
                    first, final = slot == 0 and jb == 0, slot == 1 and jb == JB - 1
                    out = out_ps[half][:]
                    pe.matmul(out, vs[:, slot, 0, jb, :], hi, start=first, stop=False, skip_group_check=True)
                    pe.matmul(out, vs[:, slot, 0, jb, :], lo, start=False, stop=False, skip_group_check=True)
                    last = pe.matmul(out, vs[:, slot, 1, jb, :], hi, start=False, stop=final,
                                     skip_group_check=True)
                else:
                    out = out_ps[half][slot * vw:(slot + 1) * vw, :]
                    pe.matmul(out, vs[:, slot, jb, :], hi, start=jb == 0, stop=False, skip_group_check=True)
                    last = pe.matmul(out, vs[:, slot, jb, :], lo, start=False, stop=jb == JB - 1,
                                     skip_group_check=True)
                last.then_inc(pv_done, 1)

            def one_turn(n, first, last):
                for t in range(TURN_T):
                    if not (last and t + AHEAD >= TURN_T):
                        scores(n, t + AHEAD)
                    for j in (2 * t, 2 * t + 1):
                        turn(n, j)
                        if not (first and j < LAG):
                            times_v(n, j - LAG)

            for t in range(AHEAD):
                scores(0, t)
            one_turn(0, True, False)
            with pe.Fori(1, turns - 1) as n:
                one_turn(n, False, False)
            one_turn(turns - 1, False, True)
            for j in range(LAG):
                times_v(turns, j - LAG)

        @block.scalar
        def _(act):
            def exponentiate(n, t):
                n, t = n + t // TURN_T, t % TURN_T
                T = TURN_T * n + t
                act.wait_ge(max_ready, T + 1)
                if t % TILES == 0 and not (isinstance(n, int) and n == 0):
                    act.wait_ge(turned, TURN_J * n - TURN_J + JB * (t // TILES + 1))
                act.activation(probs[:, t, :], score_ps[t % 2][:], ACT.Exp, bias=negmax[:, t:t + 1],
                               accum_out=den[:, t:t + 1]).then_inc(exp_done, 1)

            def scale_q(g):
                if not (isinstance(g, int) and g == 0):
                    wait_apart(act, act_passed, q_step, 2 * g)
                act.activation(qtmp[:], qT[:, bass.ds((g // HA) * SEQ, SEQ)], ACT.Copy,
                               scale=wpre[:, bass.ds(g % HA, 1)]).then_inc(q_scaled, 1)

            def high(n, j):
                act.wait_ge(turned, TURN_J * n + j + 1)
                if not (isinstance(n, int) and n == 0 and j < 4):
                    act.wait_ge(pv_done, TURN_J * n + j - 3)
                act.copy(pT[:, j % 4, 0, :], turn_ps[j % 2][:]).then_inc(hi_ready, 1)

            def one_turn(n, last):
                for t in range(TURN_T):
                    high(n, 2 * t)
                    high(n, 2 * t + 1)
                    if not (last and t + AHEAD >= TURN_T):
                        exponentiate(n, t + AHEAD)
                    if a and (t + AHEAD) % 8 == 0 and not (last and t + AHEAD >= 8):
                        scale_q(2 * n + (t + AHEAD) // 8 + 1)

            if a:
                scale_q(0)
            for t in range(AHEAD):
                exponentiate(0, t)
                if a and t == 0:
                    scale_q(1)
            one_turn(0, False)
            with act.Fori(1, turns - 1) as n:
                one_turn(n, False)
            one_turn(turns - 1, True)

        @block.vector
        def _(dve):
            def row_max(n, t):
                n, t = n + t // TURN_T, t % TURN_T
                dve.wait_ge(scored, TURN_T * n + t + 1)
                dve.tensor_reduce(negmax[:, t:t + 1], score_ps[t % 2][:], AX.X, ALU.max,
                                  negate=True).then_inc(max_ready, 1)

            def invert(n, t):
                n, t = n + t // TURN_T, t % TURN_T
                dve.wait_ge(exp_done, TURN_T * n + t + 1)
                dve.reciprocal(rden[:, t:t + 1], den[:, t:t + 1]).then_inc(rden_ready, 1)

            def low(n, j):
                dve.wait_ge(hi_ready, TURN_J * n + j + 1)
                dve.tensor_tensor(pT[:, j % 4, 1, :], turn_ps[j % 2][:], pT[:, j % 4, 0, :],
                                  ALU.subtract).then_inc(lo_ready, 1)

            def keep_a(n, half):
                dve.wait_ge(pv_done, TURN_J * n + (3 + half) * JB)
                to = accT[:, bass.ds((n // tpb) * SEQ + half * HALF, HALF)]
                dve.tensor_tensor(to, out_ps[half][:], to, ALU.add).then_inc(out_kept, 1)

            def keep_b(n, u):
                slot, half = u // 2, u % 2
                rows = slice(slot * vw, (slot + 1) * vw)
                dve.wait_ge(pv_done, TURN_J * n + (u + 1) * JB)
                dve.tensor_copy(oT[rows, bass.ds(n * SEQ + half * HALF, HALF)],
                                out_ps[half][rows, :]).then_inc(out_kept, 1)

            def one_turn(n, first, last):
                for t in range(TURN_T):
                    if not (last and t + AHEAD >= TURN_T):
                        row_max(n, t + AHEAD)
                    low(n, 2 * t)
                    low(n, 2 * t + 1)
                    if not (last and t + AHEAD > TURN_T):
                        invert(n, t + AHEAD - 1)
                    if a and t == 1 and not first:
                        keep_a(n - 1, 1)
                    if a and t == 13:
                        keep_a(n, 0)
                    if not a and t % 4 == 1 and not (first and t == 1):
                        keep_b(n if t > 1 else n - 1, (t // 4 - 1) % UNITS)

            for t in range(AHEAD):
                row_max(0, t)
                if t:
                    invert(0, t - 1)
            one_turn(0, True, False)
            with dve.Fori(1, turns - 1) as n:
                one_turn(n, False, False)
            one_turn(turns - 1, False, True)
            if a:
                keep_a(turns - 1, 1)
            else:
                keep_b(turns - 1, UNITS - 1)

        @block.gpsimd
        def _(pool):
            def q_part(g, slot, i, first=False):
                if i == 0:
                    wait_apart(pool, pool_passed, q_scaled, g + 1)
                    if not first:
                        wait_apart(pool, pool_passed, scored, 2 * TILES * (g - 1))
                    pool.tensor_scalar(qs[:, slot, 0, :], qtmp[:], 1.0, 1.0, ALU.mult,
                                       ALU.mult).then_inc(q_step, 1)
                else:
                    pool.wait_ge(q_step, 2 * g + 1)
                    pool.tensor_tensor(qs[:, slot, 1, :], qtmp[:], qs[:, slot, 0, :],
                                       ALU.subtract).then_inc(q_step, 1)

            def v_part(g, slot, i, first=False):
                b, h = g // HA, g % HA
                if i == 0:
                    src = v[:, bass.ds(b * SEQ, SEQ)].rearrange("p (j d) -> p j d", j=JB)
                    w = wpost[:, bass.ds(h * D, D)][:, None, :].broadcast_to([P, JB, D])
                    pool.tensor_tensor(vtmp[:], src, w, ALU.mult).then_inc(v_step, 1)
                elif i == 1:
                    wait_apart(pool, pool_passed, v_step, 3 * g + 1)
                    if not first:
                        wait_apart(pool, pool_passed, pv_done, 2 * JB * (g - 1))
                    pool.tensor_scalar(vs[:, slot, 0, :, :], vtmp[:], 1.0, 1.0, ALU.mult,
                                       ALU.mult).then_inc(v_step, 1)
                else:
                    pool.wait_ge(v_step, 3 * g + 2)
                    pool.tensor_tensor(vs[:, slot, 1, :, :], vtmp[:], vs[:, slot, 0, :, :],
                                       ALU.subtract).then_inc(v_step, 1)

            def v_copy(n, slot, first):
                if not first:
                    wait_apart(pool, pool_passed, pv_done, TURN_J * n - TURN_J + 2 * JB * (slot + 1))
                pool.tensor_copy(vs[:, slot, :, :], v_all[:, bass.ds(2 * n + slot, 1), :, :]
                                 .rearrange("p o j d -> p (o j) d")).then_inc(v_step, 1)

            def normalise(n, t):
                wait_apart(pool, pool_passed, rden_ready, TURN_T * n + t + 1)
                pool.tensor_scalar(probs[:, t, :], probs[:, t, :], rden[:, t:t + 1], PSCALE,
                                   ALU.mult, ALU.mult).then_inc(normed, 1)

            def one_turn(n, first, last):
                for t in range(TURN_T):
                    normalise(n, t)
                    slot, k = t // 8, t % 8
                    if a:
                        more = not (last and slot == 1)
                        if k == 0 and more:
                            q_part(2 * n + slot + 1, 1 - slot, 0, first and slot == 0)
                        if k == 1 and more:
                            q_part(2 * n + slot + 1, 1 - slot, 1)
                        if k in (2, 3, 4):
                            v_part(2 * n + slot, slot, k - 2, first)
                    elif k == 2:
                        v_copy(n, slot, first)

            if a:
                for i in range(2):
                    q_part(0, 0, i, True)
            one_turn(0, True, False)
            with pool.Fori(1, turns - 1) as n:
                one_turn(n, False, False)
            one_turn(turns - 1, False, True)


def project_a(st, io, x, accT):
    nc = st.nc
    with ExitStack() as s:
        wout = st.sb(s, "pa_wout", [P, D])
        bout = st.sb(s, "pa_bout", [P, D])
        xb = st.sb(s, "pa_xb", [P, NT, D])
        y = [st.ps(s, f"pa_y{i}", [P, 4, D]) for i in range(2)]
        w_in, y_done, bias_added, y_read = (st.sem("pa_w_in"), st.sem("pa_y_done"),
                                            st.sem("pa_bias_added"), st.sem("pa_y_read"))
        block = s.enter_context(nc.Block())

        @block.sync
        def _(sp):
            sp.dma_start(wout[:], io["wout_T"]).then_inc(w_in, 16)
            sp.dma_start(bout[:], io["bout"].broadcast_to([P, D])).then_inc(w_in, 16)

        @block.tensor
        def _(pe):
            pe.wait_ge(w_in, 32)
            for c in range(NCH):
                if c >= 2:
                    pe.wait_ge(y_read, c - 1)
                for k in range(4):
                    t = 4 * c + k
                    last = pe.matmul(y[c % 2][:, k, :], accT[:, t * P:(t + 1) * P], wout[:],
                                     start=(k == 0), stop=True, skip_group_check=True)
                last.then_inc(y_done, 1)

        @block.gpsimd
        def _(pool):
            pool.wait_ge(w_in, 32)
            for c in range(NCH):
                pool.tensor_tensor(xb[:, 4 * c:4 * c + 4, :], x[:, 4 * c:4 * c + 4, :],
                                   bout[:, None, :].broadcast_to([P, 4, D]), ALU.add).then_inc(bias_added, 1)

        @block.vector
        def _(dve):
            for c in range(NCH):
                dve.wait_ge(bias_added, c + 1)
                dve.wait_ge(y_done, c + 1)
                dve.scalar_tensor_tensor(out=x[:, 4 * c:4 * c + 4, :], in0=y[c % 2][:], scalar=1.0 / PSCALE,
                                         in1=xb[:, 4 * c:4 * c + 4, :], op0=ALU.mult,
                                         op1=ALU.add).then_inc(y_read, 1)


def route(st, io, tag, x, xn, oh, ohT, xsel, xh):
    nc = st.nc
    with ExitStack() as s:
        ln = LnWork(st, s, tag + "ln", xn)
        ident = st.sb(s, tag + "ident", [P, P])
        wr = st.sb(s, tag + "wr", [P, D])
        iota = st.sb(s, tag + "iota", [P, 2, 2 * CAP])
        below = st.sb(s, tag + "below", [P, P])
        junk = st.sb(s, tag + "junk", [P, 4, SEQ])
        score = st.sb(s, tag + "score", [P, NT])
        part = st.sb(s, tag + "part", [P, NT, 4])
        rank = st.sb(s, tag + "rank", [P, NT])
        row = [st.ps(s, f"{tag}row{i}", [P, SEQ]) for i in range(2)]
        sel = [st.ps(s, f"{tag}sel{i}", [P, D]) for i in range(2)]
        tps = [st.ps(s, f"{tag}tps{i}", [P, 4, P]) for i in range(2)]
        w_in, row_ready, rank_ready = st.sem(tag + "w_in"), st.sem(tag + "row_ready"), st.sem(tag + "rank_ready")
        junked = st.sem(tag + "junked")
        zeroed = st.sem(tag + "zeroed")
        oh_ready, ohT_done, ohT_kept, sel_done = (st.sem(tag + "oh_ready"), st.sem(tag + "ohT_done"),
                                                  st.sem(tag + "ohT_kept"), st.sem(tag + "sel_done"))
        block = s.enter_context(nc.Block())

        @block.sync
        def _(sp):
            sp.dma_start(wr[:], io["w_router"].broadcast_to([P, D])).then_inc(w_in, 16)
            sp.dma_start(iota[:], io["iota"]).then_inc(w_in, 16)
            sp.dma_start(below[:], io["below"]).then_inc(w_in, 16)
            sp.dma_start(ident[:], io["ident"]).then_inc(w_in, 16)

        @block.scalar
        def _(act):
            layernorm_scalar(act, ln)
            for c in range(NCH):
                act.wait_ge(ohT_done, c + 1)
                act.copy(ohT[:, 4 * c:4 * c + 4, :], tps[c % 2][:]).then_inc(ohT_kept, 1)
            for pr in range(2):
                act.wait_ge(sel_done, pr + 1)
                act.copy(xsel[:, pr, :], sel[pr][:])

        @block.vector
        def _(dve):
            used = [0]

            def junk_slot(width):
                used[0] += 1
                if used[0] > 4:
                    dve.wait_ge(junked, used[0] - 4)
                return junk[:, used[0] % 4, 0:width]

            dve.memset(part[:], 0.0).then_inc(zeroed, 1)
            layernorm_vector(dve, ln, x, lambda b: None)
            dve.wait_ge(w_in, 64)
            dve.wait_ge(ln.normed, NT)
            for t in range(NT):
                dve.scalar_tensor_tensor(out=junk_slot(D), in0=xn[:, t, :], scalar=1.0, in1=wr[:], op0=ALU.mult,
                                         op1=ALU.mult, accum_out=score[:, t:t + 1]).then_inc(junked, 1)
            dve.wait_ge(junked, NT)
            dve.wait_ge(zeroed, 1)
            for b in range(NB):
                dve.wait_ge(row_ready, b + 1)
                bc = row[b % 2]
                for i in range(TPB):
                    t = b * TPB + i
                    own = score[:, t:t + 1]
                    if i > 0:
                        dve.tensor_scalar(junk_slot(i * P), bc[:, 0:i * P], own, None, ALU.is_ge, ALU.add,
                                          accum_out=part[:, t, 0:1]).then_inc(junked, 1)
                    if i < TPB - 1:
                        dve.tensor_scalar(junk_slot(SEQ - (i + 1) * P), bc[:, (i + 1) * P:], own, None,
                                          ALU.is_gt, ALU.add, accum_out=part[:, t, 1:2]).then_inc(junked, 1)
                    mine = bc[:, i * P:(i + 1) * P]
                    dve.tensor_scalar(junk_slot(P), mine, own, None, ALU.is_gt, ALU.add,
                                      accum_out=part[:, t, 2:3]).then_inc(junked, 1)
                    dve.scalar_tensor_tensor(out=junk_slot(P), in0=mine, scalar=own, in1=below[:],
                                             op0=ALU.is_equal, op1=ALU.mult,
                                             accum_out=part[:, t, 3:4]).then_inc(junked, 1)
                dve.wait_ge(junked, used[0])
                dve.tensor_reduce(rank[:, b * TPB:(b + 1) * TPB], part[:, b * TPB:(b + 1) * TPB, :],
                                  AX.X, ALU.add).then_inc(rank_ready, 1)

        @block.gpsimd
        def _(pool):
            pool.wait_ge(w_in, 64)
            pool.wait_ge(ln.normed, NT)
            pool.tensor_tensor(xh[:], x[:], xn[:], ALU.add)
            for t in range(NT):
                b = t // TPB
                if t % TPB == 0:
                    pool.wait_ge(rank_ready, b + 1)
                pool.tensor_scalar(oh[:, t, :], iota[:, b % 2, :], rank[:, t:t + 1], None,
                                   ALU.is_equal).then_inc(oh_ready, 1)

        @block.tensor
        def _(pe):
            pe.wait_ge(w_in, 64)
            pe.wait_ge(junked, NT)

            def rows(b):
                for i in range(TPB):
                    t = b * TPB + i
                    last = pe.transpose(row[b % 2][:, i * P:(i + 1) * P],
                                        score[:, t:t + 1].broadcast_to([P, P]), ident[:])
                last.then_inc(row_ready, 1)

            rows(0)
            rows(1)
            for b in range(NB):
                for i in range(TPB):
                    t = b * TPB + i
                    pe.wait_ge(oh_ready, t + 1)
                    last = pe.matmul(sel[b // 2][:], oh[:, t, :], xn[:, t, :], start=t % (2 * TPB) == 0,
                                     stop=t % (2 * TPB) == 2 * TPB - 1)
                    if t % (2 * TPB) == 2 * TPB - 1:
                        last.then_inc(sel_done, 1)
                if b + 2 < NB:
                    rows(b + 2)
                for c in (2 * b, 2 * b + 1):
                    if c >= 2:
                        pe.wait_ge(ohT_kept, c - 1)
                    for k in range(4):
                        last = pe.transpose(tps[c % 2][:, k, :], oh[:, 4 * c + k, :], ident[:])
                    last.then_inc(ohT_done, 1)


def picked_block(st, io, tag, x, ohT, xsel, xh):
    nc = st.nc
    QK = 2 * CAP
    with ExitStack() as s:
        def sb(name, shape):
            return st.sb(s, tag + name, shape)

        def sem(name):
            return st.sem(tag + name)

        ident = sb("ident2", [P, P])
        g = sb("g", [P, 2, D])
        wqkv = sb("wqkv", [P, 3, D])
        wout, w12 = sb("wout", [P, D]), sb("w12", [P, 2, 3 * P])
        w3 = sb("w3", [P, 3, D])
        headm, pairm = sb("headm", [P, HA]), sb("pairm", [P, D])
        causal = sb("causal", [P, CAP])
        sq, ss, ve = sb("sq", [P, 2, D]), sb("ss", [P, 2]), sb("ve", [P, 2])
        sd, r0, t0, t1, rms = (sb(n, [P, 2]) for n in ("sd", "r0", "t0", "t1", "rms"))
        hn, hnT, qT = sb("hn", [P, 2, D]), sb("hnT", [P, 2, QK]), sb("qT", [P, 2 * QK])
        kx, vx = sb("kx", [P, NB, HA, CAP]), sb("vx", [P, NB, D])
        sm, mx = sb("sm", [P, 2, HA, CAP]), sb("mx", [P, 2, HA])
        pr_, dn, rd = sb("pr", [P, 2, HA, CAP]), sb("dn", [P, 2, HA]), sb("rd", [P, 2, HA])
        pT = sb("pT", [P, 2, HA // 2, P])
        o, oT = sb("o", [P, 2, D]), sb("oT", [P, 2, QK])
        xa, mid = sb("xa", [P, 2, D]), sb("mid", [P, 2, D])
        e, u = sb("e", [P, 3, 2 * QK]), sb("u", [P, 3, 2 * QK])
        delta = sb("delta", [P, 2, D])
        twice = sb("twice", [P, NB, 2, CAP])
        A, B, C, E = (st.ps(s, tag + n, [P, CH]) for n in "ABCE")
        wide = [st.ps(s, f"{tag}wide{i}", [P, SEQ]) for i in range(2)]
        w_in, step, var_ready, root_ready = sem("w2_in"), sem("step"), sem("var_ready"), sem("root_ready")
        twice_kept = sem("twice_kept")
        hn_ready, hnT_done, hnT_kept, qkv_done = (sem("hn_ready"), sem("hnT_done"), sem("hnT_kept"),
                                                  sem("qkv_done"))
        qT_kept, kx_ready, vx_ready, att_done = sem("qT_kept"), sem("kx_ready"), sem("vx_ready"), sem("att_done")
        shifted, exped, probs_ready = sem("shifted"), sem("exped"), sem("probs_ready")
        pT_done, pT_kept, o_done, o_kept = sem("pT_done"), sem("pT_kept"), sem("o_done"), sem("o_kept")
        oT_done, oT_kept, xa_done = sem("oT_done"), sem("oT_kept"), sem("xa_done")
        up_done, up_exped, u_ready, ff_done = sem("up_done"), sem("up_exped"), sem("u_ready"), sem("ff_done")
        delta_ready, put_done, put_read = sem("delta_ready"), sem("put_done"), sem("put_read")
        block = s.enter_context(nc.Block())
        LOADS = 10

        @block.sync
        def _(sp):
            for to, name in ((ident, "ident"), (g, "g"), (wqkv, "fqkv_T"), (wout, "fout_T"), (w12, "w12_T"),
                             (w3, "w3_T"), (headm, "headm"), (pairm, "pairm"), (causal, "causal")):
                src = io[name]
                sp.dma_start(to[:], src.broadcast_to([P, 2, D]) if name == "g" else src).then_inc(w_in, 16)

        @block.vector
        def _(dve):
            chain = [0]

            def chained(ins):
                ins.then_inc(step, 1)
                chain[0] += 1
                dve.wait_ge(step, chain[0])

            def rms_rows(src, half):
                for pr in range(2):
                    last = dve.scalar_tensor_tensor(out=sq[:, pr, :], in0=src[:, pr, :], scalar=1.0, in1=src[:, pr, :],
                                                    op0=ALU.mult, op1=ALU.mult, accum_out=ss[:, pr:pr + 1])
                chained(last)
                dve.tensor_scalar(ve[:], ss[:], 1.0 / D, RMS_EPS, ALU.mult, ALU.add).then_inc(var_ready, 1)
                dve.wait_ge(root_ready, half + 1)
                chained(dve.reciprocal(r0[:], sd[:]))
                newton_rsqrt(dve, step, chain[0], ve, r0, t0, t1, rms)
                chain[0] += 4
                dve.wait_ge(step, chain[0])
                for pr in range(2):
                    last = dve.scalar_tensor_tensor(out=hn[:, pr, :], in0=src[:, pr, :], scalar=rms[:, pr:pr + 1],
                                                    in1=g[:, half, :], op0=ALU.mult, op1=ALU.mult)
                last.then_inc(hn_ready, 1)

            dve.wait_ge(w_in, 16 * (LOADS - 1))
            rms_rows(xsel, 0)
            dve.wait_ge(qkv_done, 1)
            for b in range(NB):
                k = E[:, b * CAP:(b + 1) * CAP][:, None, :].broadcast_to([P, HA, CAP])
                dve.tensor_tensor(kx[:, b, :, :], k, headm[:, :, None].broadcast_to([P, HA, CAP]),
                                  ALU.mult).then_inc(kx_ready, 1)
            dve.tensor_tensor(vx[:], C[:].rearrange("p (b d) -> p b d", b=NB),
                              pairm[:, None, :].broadcast_to([P, NB, D]), ALU.mult).then_inc(vx_ready, 1)
            for pr in range(2):
                dve.wait_ge(att_done, pr + 1)
                w = wide[pr][:].rearrange("p (h k) -> p h k", h=HA)
                chained(dve.tensor_tensor(sm[:, pr], w, causal[:, None, :].broadcast_to([P, HA, CAP]), ALU.add))
                chained(dve.tensor_reduce(mx[:, pr], sm[:, pr], AX.X, ALU.max))
                dve.tensor_tensor(sm[:, pr], sm[:, pr], mx[:, pr, :, None].broadcast_to([P, HA, CAP]),
                                  ALU.subtract).then_inc(shifted, 1)
            for pr in range(2):
                dve.wait_ge(exped, pr + 1)
                chained(dve.tensor_reduce(dn[:, pr], pr_[:, pr], AX.X, ALU.add))
                chained(dve.reciprocal(rd[:, pr], dn[:, pr]))
                dve.tensor_tensor(pr_[:, pr], pr_[:, pr], rd[:, pr, :, None].broadcast_to([P, HA, CAP]),
                                  ALU.mult).then_inc(probs_ready, 1)
            dve.wait_ge(o_done, 1)
            dve.tensor_copy(o[:], A[:, 0:2 * D].rearrange("p (r d) -> p r d", r=2)).then_inc(o_kept, 1)
            dve.wait_ge(xa_done, 1)
            chained(dve.tensor_copy(xa[:], C[:, 0:2 * D].rearrange("p (r d) -> p r d", r=2)))
            chained(dve.tensor_tensor(mid[:], xsel[:], xa[:], ALU.add))
            rms_rows(mid, 1)
            dve.wait_ge(up_exped, 1)
            chained(dve.tensor_scalar(e[:], e[:], 1.0, None, ALU.add))
            chained(dve.reciprocal(e[:], e[:]))
            a3, b3 = (w[:, 0:6 * QK].rearrange("p (c t) -> p c t", c=3) for w in wide)
            chained(dve.tensor_tensor(e[:], a3, e[:], ALU.mult))
            dve.tensor_tensor(u[:], b3, e[:], ALU.mult).then_inc(u_ready, 1)
            dve.wait_ge(ff_done, 1)
            dve.tensor_tensor(delta[:], A[:, 0:2 * D].rearrange("p (r d) -> p r d", r=2), xa[:],
                              ALU.add).then_inc(delta_ready, 1)
            for c in range(NCH):
                dve.wait_ge(put_done, c + 1)
                dve.tensor_tensor(x[:, 4 * c:4 * c + 4, :],
                                  (B, C, E)[c % 3][:].rearrange("p (k d) -> p k d", k=4),
                                  xh[:, 4 * c:4 * c + 4, :], ALU.add).then_inc(put_read, 1)

        @block.scalar
        def _(act):
            def root(half):
                act.wait_ge(var_ready, half + 1)
                act.activation(sd[:], ve[:], ACT.Sqrt).then_inc(root_ready, 1)

            root(0)
            act.wait_ge(hnT_done, 1)
            act.copy(twice[:], A[:, 0:2 * QK].rearrange("p (b t) -> p b t", b=NB)[:, :, None, :]
                     .broadcast_to([P, NB, 2, CAP])).then_inc(twice_kept, 1)
            act.copy(hnT[:], A[:, 0:2 * QK].rearrange("p (r t) -> p r t", r=2)).then_inc(hnT_kept, 1)
            act.wait_ge(qkv_done, 1)
            act.copy(qT[:], B[:, 0:2 * QK]).then_inc(qT_kept, 1)
            for pr in range(2):
                act.wait_ge(shifted, pr + 1)
                act.activation(pr_[:, pr], sm[:, pr], ACT.Exp).then_inc(exped, 1)
            for pr in range(2):
                act.wait_ge(pT_done, pr + 1)
                act.copy(pT[:, pr], wide[pr][:].rearrange("p (h t) -> p h t", t=P)).then_inc(pT_kept, 1)
            act.wait_ge(oT_done, 1)
            act.copy(oT[:], B[:, 0:2 * QK].rearrange("p (r t) -> p r t", r=2)).then_inc(oT_kept, 1)
            root(1)
            act.wait_ge(hnT_done, 2)
            act.copy(hnT[:], E[:, 0:2 * QK].rearrange("p (r t) -> p r t", r=2)).then_inc(hnT_kept, 1)
            act.wait_ge(up_done, 1)
            act.activation(e[:], wide[0][:, 0:6 * QK].rearrange("p (c t) -> p c t", c=3), ACT.Exp,
                           scale=-1.0).then_inc(up_exped, 1)

        @block.tensor
        def _(pe):
            def turned(half, to):
                pe.wait_ge(hn_ready, half + 1)
                for pr in range(2):
                    last = pe.transpose(to[:, pr * QK:(pr + 1) * QK], hn[:, pr, :], ident[:])
                last.then_inc(hnT_done, 1)
                pe.wait_ge(hnT_kept, half + 1)

            pe.wait_ge(w_in, 16 * (LOADS - 1))
            turned(0, A)
            pe.matmul(B[:, 0:2 * QK], wqkv[:, 0, :], hnT[:], start=True, stop=True)
            pe.matmul(E[:, 0:2 * QK], wqkv[:, 1, :], hnT[:], start=True, stop=True)
            pe.wait_ge(twice_kept, 1)
            for b in range(NB):
                last = pe.matmul(C[:, b * D:(b + 1) * D], twice[:, b, :, :], wqkv[:, 2, :], start=True, stop=True)
            last.then_inc(qkv_done, 1)
            pe.wait_ge(qT_kept, 1)
            for pr in range(2):
                pe.wait_ge(kx_ready, 2 * pr + 2)
                for b in (2 * pr, 2 * pr + 1):
                    rows = slice((b % 2) * CAP, (b % 2 + 1) * CAP)
                    for c in range(2):
                        last = pe.matmul(wide[pr][rows, c * CH:(c + 1) * CH], qT[:, b * CAP:(b + 1) * CAP],
                                         kx[:, b, c * HA // 2:(c + 1) * HA // 2, :], start=True, stop=True)
                last.then_inc(att_done, 1)
            for pr in range(2):
                pe.wait_ge(probs_ready, pr + 1)
                for h in range(HA // 2):
                    last = pe.transpose(wide[pr][:, h * P:(h + 1) * P], pr_[:, pr, 2 * h:2 * h + 2, :], ident[:])
                last.then_inc(pT_done, 1)
            pe.wait_ge(vx_ready, 1)
            for pr in range(2):
                pe.wait_ge(pT_kept, pr + 1)
                for b in (2 * pr, 2 * pr + 1):
                    rows = slice((b % 2) * CAP, (b % 2 + 1) * CAP)
                    for h in range(HA // 2):
                        last = pe.matmul(A[rows, pr * D + 2 * h * HDA:pr * D + 2 * (h + 1) * HDA],
                                         pT[:, pr, h, rows], vx[:, b, 2 * h * HDA:2 * (h + 1) * HDA],
                                         start=True, stop=True)
            last.then_inc(o_done, 1)
            pe.wait_ge(o_kept, 1)
            for pr in range(2):
                last = pe.transpose(B[:, pr * QK:(pr + 1) * QK], o[:, pr, :], ident[:])
            last.then_inc(oT_done, 1)
            pe.wait_ge(oT_kept, 1)
            for pr in range(2):
                last = pe.matmul(C[:, pr * D:(pr + 1) * D], oT[:, pr, :], wout[:], start=True, stop=True)
            last.then_inc(xa_done, 1)
            turned(1, E)
            for i in range(2):
                for c in range(3):
                    last = pe.matmul(wide[i][:, c * 2 * QK:(c + 1) * 2 * QK], w12[:, i, c * P:(c + 1) * P], hnT[:],
                                     start=True, stop=True)
            last.then_inc(up_done, 1)
            pe.wait_ge(u_ready, 1)
            for pr in range(2):
                for c in range(3):
                    last = pe.matmul(A[:, pr * D:(pr + 1) * D], u[:, c, pr * QK:(pr + 1) * QK], w3[:, c, :],
                                     start=c == 0, stop=c == 2)
            last.then_inc(ff_done, 1)
            pe.wait_ge(delta_ready, 1)
            for c in range(NCH):
                if c >= 3:
                    pe.wait_ge(put_read, c - 2)
                for k in range(4):
                    t = 4 * c + k
                    last = pe.matmul((B, C, E)[c % 3][:, k * D:(k + 1) * D], ohT[:, t, :],
                                     delta[:, t // (2 * TPB), :], start=True, stop=True)
                last.then_inc(put_done, 1)


def feed_forward(st, io, tag, x):
    with ExitStack() as s:
        ohT = st.sb(s, tag + "ohT", [P, NT, P])
        xsel = st.sb(s, tag + "xsel", [P, 2, D])
        xh = st.sb(s, tag + "xh", [P, NT, D])
        with ExitStack() as r:
            xn = st.sb(r, tag + "xn", [P, NT, D])
            oh = st.sb(r, tag + "oh", [P, NT, P])
            route(st, io, tag, x, xn, oh, ohT, xsel, xh)
        picked_block(st, io, tag, x, ohT, xsel, xh)


def prepare_b(st, io, x, q_dram, k_dram, v_all):
    nc = st.nc
    with ExitStack() as s:
        xn = st.sb(s, "b_xn", [P, NT, D])
        ln = LnWork(st, s, "lnb", xn)
        ident = st.sb(s, "b_ident", [P, P])
        wq, wdown = st.sb(s, "b_wq", [P, 2, P]), st.sb(s, "b_wdown", [P, RANK])
        wk, wv = st.sb(s, "b_wk", [RANK, 2, P]), st.sb(s, "b_wv", [RANK, HB * HDB])
        hT = st.sb(s, "b_hT", [P, 2, CH])
        lat = st.sb(s, "b_lat", [RANK, 2, CH])
        parts = st.sb(s, "b_parts", [P, 2, 4, 2, CH], F16)
        tps = st.ps(s, "b_tps", [P, CH])
        lps = st.ps(s, "b_lps", [RANK, CH])
        qkps = [st.ps(s, f"b_qkps{i}", [P, CH]) for i in range(4)]
        vps = [st.ps(s, f"b_vps{i}", [P, CH]) for i in range(2)]
        w_in, transposed, hT_ready = st.sem("b_w_in"), st.sem("b_transposed"), st.sem("b_hT_ready")
        lat_done, lat_ready, qk_done = st.sem("b_lat_done"), st.sem("b_lat_ready"), st.sem("b_qk_done")
        v_done, hi_made, lo_made = st.sem("b_v_done"), st.sem("b_hi_made"), st.sem("b_lo_made")
        stored = [st.sem(f"b_stored{i}") for i in range(2)]
        block = s.enter_context(nc.Block())
        scale = float(HDB) ** -0.5

        @block.sync
        def _(sp):
            for to, name in ((ident, "ident"), (wq, "bq_T"), (wdown, "bdown_T"), (wk, "bk_T"), (wv, "bv_T")):
                sp.dma_start(to[:], io[name]).then_inc(w_in, 16)
            for c in range(NCH):
                b, at = c // 2, c % 2 * CH
                for i in range(4):
                    sp.wait_ge(lo_made, 6 * c + i + 1)
                    dram = q_dram if i < 2 else k_dram
                    for part in range(2):
                        h0 = b * HB + i % 2 * 4
                        to = dram[part, h0:h0 + 4].rearrange("h d t -> (h d) t")[:, at:at + CH]
                        sp.dma_start(to, parts[:, c % 2, i, part, :]).then_inc(stored[c % 2], 16)
            for i in range(2):
                sp.wait_ge(stored[i], 16 * 8 * NCH // 2)

        @block.tensor
        def _(pe):
            pe.wait_ge(w_in, 80)
            for c in range(NCH):
                pe.wait_ge(ln.normed, 4 * c + 4)
                for k in range(4):
                    if c and k == 0:
                        pe.wait_ge(hT_ready, c)
                    last = pe.transpose(tps[:, k * P:(k + 1) * P], xn[:, 4 * c + k, :], ident[:])
                last.then_inc(transposed, 1)
                pe.wait_ge(hT_ready, c + 1)
                if c:
                    pe.wait_ge(lat_ready, c)
                pe.matmul(lps[:], wdown[:], hT[:, c % 2, :], start=True, stop=True).then_inc(lat_done, 1)
                for i in range(2):
                    if c:
                        pe.wait_ge(lo_made, 6 * (c - 1) + i + 1)
                    pe.matmul(qkps[i][:], wq[:, i, :], hT[:, c % 2, :], start=True, stop=True).then_inc(qk_done, 1)
                pe.wait_ge(lat_ready, c + 1)
                for i in range(2):
                    if c:
                        pe.wait_ge(lo_made, 6 * (c - 1) + i + 3)
                    pe.matmul(qkps[2 + i][:], wk[:, i, :], lat[:, c % 2, :], start=True,
                              stop=True).then_inc(qk_done, 1)
                for i in range(2):
                    if c:
                        pe.wait_ge(lo_made, 6 * (c - 1) + i + 5)
                    for k in range(2):
                        tok = (2 * i + k) * P
                        last = pe.matmul(vps[i][:, k * 256:(k + 1) * 256], lat[:, c % 2, tok:tok + P], wv[:],
                                         start=True, stop=True)
                    last.then_inc(v_done, 1)

        def v_view(c, i, part):
            b, j = c // 2, c % 2 * 4 + 2 * i
            return v_all[:, b * HB:(b + 1) * HB, j:j + 2, part * HDB:(part + 1) * HDB].rearrange(
                "p h j d -> p j h d")

        @block.scalar
        def _(act):
            layernorm_scalar(act, ln)
            for c in range(NCH):
                act.wait_ge(transposed, c + 1)
                if c >= 2:
                    act.wait_ge(qk_done, 4 * (c - 2) + 2)
                act.copy(hT[:, c % 2, :], tps[:]).then_inc(hT_ready, 1)
                act.wait_ge(lat_done, c + 1)
                if c >= 2:
                    act.wait_ge(v_done, 2 * (c - 1))
                act.copy(lat[:, c % 2, :], lps[:]).then_inc(lat_ready, 1)
                for i in range(4):
                    act.wait_ge(qk_done, 4 * c + i + 1)
                    if i == 0 and c >= 2:
                        act.wait_ge(stored[c % 2], 16 * 8 * (c // 2))
                    act.activation(parts[:, c % 2, i, 0, :], qkps[i][:], ACT.Copy,
                                   scale=scale if i < 2 else 1.0).then_inc(hi_made, 1)
                for i in range(2):
                    act.wait_ge(v_done, 2 * c + i + 1)
                    src = vps[i][:].rearrange("p (j h d) -> p j h d", j=2, h=HB)
                    for k in range(2):
                        last = act.copy(v_view(c, i, 0)[:, k], src[:, k])
                    last.then_inc(hi_made, 1)

        @block.vector
        def _(dve):
            layernorm_vector(dve, ln, x, lambda b: None)
            for c in range(NCH):
                for i in range(4):
                    dve.wait_ge(hi_made, 6 * c + i + 1)
                    dve.scalar_tensor_tensor(out=parts[:, c % 2, i, 1, :], in0=qkps[i][:],
                                             scalar=scale if i < 2 else 1.0, in1=parts[:, c % 2, i, 0, :],
                                             op0=ALU.mult, op1=ALU.subtract).then_inc(lo_made, 1)
                for i in range(2):
                    dve.wait_ge(hi_made, 6 * c + i + 5)
                    src = vps[i][:].rearrange("p (j h d) -> p j h d", j=2, h=HB)
                    for k in range(2):
                        last = dve.tensor_tensor(v_view(c, i, 1)[:, k], src[:, k], v_view(c, i, 0)[:, k],
                                                 ALU.subtract)
                    last.then_inc(lo_made, 1)


def project_b(st, io, x, oT):
    nc = st.nc
    with ExitStack() as s:
        wo = st.sb(s, "pb_wo", [P, HB // 2, D])
        y = [st.ps(s, f"pb_y{i}", [P, 4, D]) for i in range(2)]
        w_in, y_done, y_read = st.sem("pb_w_in"), st.sem("pb_y_done"), st.sem("pb_y_read")
        block = s.enter_context(nc.Block())

        @block.sync
        def _(sp):
            sp.dma_start(wo[:], io["wo_T"]).then_inc(w_in, 16)

        @block.tensor
        def _(pe):
            pe.wait_ge(w_in, 16)
            for c in range(NCH):
                if c >= 2:
                    pe.wait_ge(y_read, c - 1)
                for k in range(4):
                    b, at = c // 2, (c % 2 * 4 + k) * P
                    for h in range(HB // 2):
                        col = (b * HB // 2 + h) * SEQ + at
                        last = pe.matmul(y[c % 2][:, k, :], oT[:, col:col + P], wo[:, h, :],
                                         start=h == 0, stop=h == HB // 2 - 1)
                last.then_inc(y_done, 1)

        @block.vector
        def _(dve):
            for c in range(NCH):
                dve.wait_ge(y_done, c + 1)
                dve.scalar_tensor_tensor(out=x[:, 4 * c:4 * c + 4, :], in0=y[c % 2][:], scalar=1.0 / PSCALE,
                                         in1=x[:, 4 * c:4 * c + 4, :], op0=ALU.mult,
                                         op1=ALU.add).then_inc(y_read, 1)


def store_x(st, x, out):
    nc = st.nc
    stored = st.sem("stored")
    with nc.Block() as block:
        @block.sync
        def _(sp):
            for b in range(NB):
                sp.dma_start(out[b].rearrange("(t p) d -> p t d", p=P),
                             x[:, b * TPB:(b + 1) * TPB, :]).then_inc(stored, 16)
            sp.wait_ge(stored, 16 * NB)


def build(nc, io, out, stage=4):
    with ExitStack() as whole:
        st = Store(nc, whole)
        x = st.sb(whole, "x", [P, NT, D])
        ka_dram = nc.dram_tensor("ka_parts", (2, P, NTOK), F16, kind="Internal").ap()
        with ExitStack() as s:
            qT = st.sb(s, "qT", [P, NTOK])
            v = st.sb(s, "v", [P, NTOK])
            wpre = st.sb(s, "wpre", [P, HA])
            wpost = st.sb(s, "wpost", [P, HA * D])
            prepare_a(st, io, x, qT, v, ka_dram, wpre, wpost)
            accT = st.sb(s, "accT", [P, NTOK])
            zero(st, accT)
            attend_a(st, qT, v, ka_dram, wpre, wpost, accT)
            project_a(st, io, x, accT)
        st.end_stage()
        if stage > 1:
            feed_forward(st, io, "f1_", x)
            st.end_stage()
        if stage > 2:
            q_dram = nc.dram_tensor("q_parts", (2, NB * HB, HDB, SEQ), F16, kind="Internal").ap()
            k_dram = nc.dram_tensor("k_parts", (2, NB * HB, HDB, SEQ), F16, kind="Internal").ap()
            with ExitStack() as s:
                v_all = st.sb(s, "v_all", [P, NB * HB, JB, 2 * HDB], F16)
                prepare_b(st, io, x, q_dram, k_dram, v_all)
                oT = st.sb(s, "oT", [P, NB * HB // 2 * SEQ])
                identb = st.sb(s, "identb", [P, P])
                load_ident(st, io, identb)
                attend(st, "b", (q_dram, k_dram, v_all, oT), identb)
                project_b(st, io, x, oT)
            st.end_stage()
        if stage > 3:
            feed_forward(st, io, "f2_", x)
        store_x(st, x, out)


def load_ident(st, io, ident):
    loaded = st.sem("zb_loaded")
    with st.nc.Block() as block:
        @block.sync
        def _(sp):
            sp.dma_start(ident[:], io["ident"]).then_inc(loaded, 16)
            sp.wait_ge(loaded, 16)


def zero(st, accT):
    with st.nc.Block() as block:
        @block.vector
        def _(dve):
            dve.memset(accT[:], 0.0)


def layouts(i):
    f = np.float32
    rows = np.ascontiguousarray
    wqkv, bqkv = i["L0_attn_a_Wqkv"], i["L0_attn_a_bqkv"]
    half = HDA // 2
    partner = np.arange(D).reshape(HA, 2, half)[:, ::-1].reshape(D)
    q, k = np.arange(D), D + np.arange(D)
    picks = [q, q[partner], k, k[partner]]
    inv = (f(1.0) / np.power(f(10000.0), np.arange(0, HDA, 2, dtype=f) / f(HDA))).astype(f)
    ang = np.arange(SEQ, dtype=f)[:, None] * inv[None, :]
    cos, sin = np.cos(ang).T, np.sin(ang).T
    sq = f(HDA) ** f(-0.5)
    rope = np.stack([np.tile(np.concatenate([cos, cos]), (HA, 1)),
                     np.tile(np.concatenate([-sin, sin]), (HA, 1))], axis=1).astype(f)
    rope = np.concatenate([rope * sq, rope], axis=1)

    def pad(w):
        return np.concatenate([w, np.zeros((3 * P - DFF, w.shape[1]), f)])

    return {
        "x": rows(i["L0_attn_a_x"]),
        "ident": np.eye(P, dtype=f),
        "wqk_T": rows(np.stack([wqkv[p].T for p in picks], axis=1)),
        "wv_T": rows(wqkv[2 * D:].T),
        "bqk": rows(np.stack([bqkv[p] for p in picks], axis=1)),
        "bv": rows(bqkv[None, 2 * D:]),
        "rope": rows(rope),
        "wpre": rows(np.repeat(i["L0_attn_a_Wpre"].T, HDA, axis=0)),
        "wpost": rows(np.repeat(i["L0_attn_a_Wpost"].T, HDA, axis=1).reshape(1, -1)),
        "wout_T": rows(i["L0_attn_a_Wout"].T),
        "bout": rows(i["L0_attn_a_bout"][None]),
        "w_router": rows(i["L0_ffn_w_router"][None]),
        "iota": rows(np.broadcast_to(np.stack([np.r_[np.arange(CAP), -np.ones(CAP)],
                                               np.r_[-np.ones(CAP), np.arange(CAP)]]), (P, 2, P)).astype(f)),
        "below": np.tril(np.ones((P, P), f), -1),
        "g": rows(np.stack([i["L0_ffn_g1"], i["L0_ffn_g2"]])[None]),
        "fqkv_T": rows(np.stack([i["L0_ffn_W_qkv"][k * D:(k + 1) * D].T for k in range(3)], axis=1)),
        "fout_T": rows(i["L0_ffn_W_out"].T),
        "w12_T": rows(np.stack([pad(i["L0_ffn_W1"]).T, pad(i["L0_ffn_W2"]).T], axis=1)),
        "w3_T": rows(pad(i["L0_ffn_W3"].T).reshape(3, P, D).transpose(1, 0, 2)),
        "headm": (np.kron(np.eye(HA), np.ones((HDA, 1))) * HDA ** -0.5).astype(f),
        "pairm": np.tile(np.kron(np.eye(2), np.ones((CAP, HDA))), (1, HA // 2)).astype(f),
        "causal": np.tile(np.triu(np.full((CAP, CAP), -1e30), 1), (2, 1)).astype(f),
        "bq_T": rows(i["L0_attn_b_Wq"].T.reshape(D, 2, P)),
        "bdown_T": rows(i["L0_attn_b_Wkv_down"].T),
        "bk_T": rows(i["L0_attn_b_Wk_up"].T.reshape(RANK, 2, P)),
        "bv_T": rows(i["L0_attn_b_Wv_up"].T),
        "wo_T": rows(np.repeat(i["L0_attn_b_Wo"].T.reshape(HB // 2, 2, 1, HDB, D), 2, axis=2)
                     .reshape(HB // 2, P, D).transpose(1, 0, 2)),
    }


def kernel(**inputs):
    import concourse.bacc as bacc
    from concourse.bass_utils import run_bass_kernel_spmd

    arrays = layouts({k: np.asarray(v) for k, v in inputs.items()})
    nc = bacc.Bacc("TRN2", target_bir_lowering=False, num_devices=1)
    io = {n: nc.dram_tensor(n + "_dram", a.shape, mybir.dt.from_np(a.dtype), kind="ExternalInput").ap()
          for n, a in arrays.items()}
    out = nc.dram_tensor("out_dram", (NB, SEQ, D), F32, kind="ExternalOutput").ap()
    build(nc, io, out)
    result = run_bass_kernel_spmd(nc, [{n + "_dram": a for n, a in arrays.items()}], core_ids=[0])
    return result.results[0]["out_dram"]
```

```python
from contextlib import ExitStack

import numpy as np
import concourse.bass as bass
from concourse import mybir

ALU = mybir.AluOpType
ACT = mybir.ActivationFunctionType
AX = mybir.AxisListType
F32 = mybir.dt.float32
F16 = mybir.dt.float16

P = 128
NB, SEQ, D = 4, 1024, 128
TPB = SEQ // P
NT = NB * TPB
NTOK = NB * SEQ
CH = 512
NCH = NTOK // CH
HA, HDA = 16, 8
HB, HDB = 8, 32
RANK = 64
CAP = 64
DFF = 341
HALF = SEQ // 2
UNITS = 4
TILES = 4
JB = SEQ // P
TURN_T = UNITS * TILES
TURN_J = UNITS * JB
AHEAD_A = 10
AHEAD_B = 10
LAG = 3
ORDER = (0, 1, 2, 7, 3, 4, 5, 6)
SENT, FULL = (3,), (1, 2, 4, 5, 6, 7)
DVE_FULL = (7,)
SPLIT_RING, FULL_RING = 2, 3
LOAD_AFTER = 1
V_LOAD_AFTER = (13, 5)
TURN_BANKS = 2
PSCALE = 2.0 ** 14
K_LOAD_AT = 8
GT_RING = 4
LN_EPS, RMS_EPS = 1e-5, 1e-6


def wait_apart(eng, passed, sem, value):
    eng.wait_ge(sem, value)
    eng.sem_inc(passed, 1)


class Store:

    def __init__(self, nc, stack):
        self.nc, self.stack, self.stage_sems = nc, stack, []

    def sem(self, name):
        self.stage_sems.append(self.nc.alloc_semaphore(name=name))
        return self.stage_sems[-1]

    def end_stage(self):
        self.nc.all_engine_barrier()
        self.nc.clear_and_free_semaphores(self.stage_sems)
        self.nc.all_engine_barrier()
        self.stage_sems = []

    def sb(self, stack, name, shape, dt=F32):
        return stack.enter_context(self.nc.sbuf_tensor(name, shape, dt))

    def ps(self, stack, name, shape, dt=F32):
        return stack.enter_context(self.nc.psum_tensor(name, shape, dt))


class LnWork:

    def __init__(self, st, stack, tag, xn):
        self.stats = st.sb(stack, tag + "_stats", [P, NT, 6])
        self.mv = st.sb(stack, tag + "_mv", [P, NT, 2])
        self.ve = st.sb(stack, tag + "_ve", [P, NT])
        self.sd = st.sb(stack, tag + "_sd", [P, NT])
        self.r0 = st.sb(stack, tag + "_r0", [P, NT])
        self.t0 = st.sb(stack, tag + "_t0", [P, NT])
        self.t1 = st.sb(stack, tag + "_t1", [P, NT])
        self.rstd = st.sb(stack, tag + "_rstd", [P, NT])
        self.xn = xn
        self.step = st.sem(tag + "_step")
        self.ve_ready = st.sem(tag + "_ve_ready")
        self.sd_ready = st.sem(tag + "_sd_ready")
        self.normed = st.sem(tag + "_normed")


def layernorm_vector(dve, w, x, wait_x):
    for t in range(NT):
        if t % TPB == 0:
            wait_x(t // TPB)
        last = dve.bn_stats(w.stats[:, t, :], x[:, t, :])
    last.then_inc(w.step, 1)
    dve.wait_ge(w.step, 1)
    for t in range(NT):
        last = dve.bn_aggr(w.mv[:, t, :], w.stats[:, t, :])
    last.then_inc(w.step, 1)
    dve.wait_ge(w.step, 2)
    dve.tensor_scalar(w.ve[:], w.mv[:, :, 1], LN_EPS, None, ALU.add).then_inc(w.ve_ready, 1)
    dve.wait_ge(w.sd_ready, 1)
    dve.reciprocal(w.r0[:], w.sd[:]).then_inc(w.step, 1)
    newton_rsqrt(dve, w.step, 3, w.ve, w.r0, w.t0, w.t1, w.rstd)
    dve.wait_ge(w.step, 7)
    for t in range(NT):
        dve.tensor_scalar(w.xn[:, t, :], x[:, t, :], w.mv[:, t, 0:1], w.rstd[:, t:t + 1],
                          ALU.subtract, ALU.mult).then_inc(w.normed, 1)


def newton_rsqrt(dve, step, n, v, r0, t0, t1, out):
    dve.wait_ge(step, n)
    dve.tensor_tensor(t0[:], r0[:], r0[:], ALU.mult).then_inc(step, 1)
    dve.wait_ge(step, n + 1)
    dve.tensor_tensor(t1[:], t0[:], v[:], ALU.mult).then_inc(step, 1)
    dve.wait_ge(step, n + 2)
    dve.tensor_scalar(t0[:], t1[:], -0.5, 1.5, ALU.mult, ALU.add).then_inc(step, 1)
    dve.wait_ge(step, n + 3)
    dve.tensor_tensor(out[:], r0[:], t0[:], ALU.mult).then_inc(step, 1)


def layernorm_scalar(act, w):
    act.wait_ge(w.ve_ready, 1)
    act.activation(w.sd[:], w.ve[:], ACT.Sqrt).then_inc(w.sd_ready, 1)


def prepare_a(st, io, x, qT, v, k_dram, wpre, wpost, accT):
    nc = st.nc
    with ExitStack() as s:
        xn = st.sb(s, "a_xn", [P, NT, D])
        ln = LnWork(st, s, "lna", xn)
        ident = st.sb(s, "a_ident", [P, P])
        wqk = st.sb(s, "a_wqk", [P, 4, D])
        wv = st.sb(s, "a_wv", [P, D])
        bqk = st.sb(s, "a_bqk", [P, 4])
        bv = st.sb(s, "a_bv", [P, D])
        rope = st.sb(s, "a_rope", [P, 4, SEQ])
        hT = st.sb(s, "a_hT", [P, NTOK])
        khi = st.sb(s, "a_khi", [P, NTOK], F16)
        klo = st.sb(s, "a_klo", [P, NTOK], F16)
        prod = st.sb(s, "a_prod", [P, 4, 2, CH])
        kT = st.sb(s, "a_kT", [P, 2, CH])
        tps = [st.ps(s, f"a_tps{i}", [P, CH]) for i in range(2)]
        qkps = [st.ps(s, f"a_qkps{i}", [P, CH]) for i in range(4)]
        vps = [st.ps(s, f"a_vps{i}", [P, CH]) for i in range(2)]
        x_in = [st.sem(f"a_x_in{b}") for b in range(NB)]
        w_in = st.sem("a_w_in")
        transposed, hT_ready = st.sem("a_transposed"), st.sem("a_hT_ready")
        qk_done, prod_ready, qk_summed = st.sem("a_qk_done"), st.sem("a_prod_ready"), st.sem("a_qk_summed")
        k_stored = st.sem("a_k_stored")
        v_done, v_kept, khi_ready, klo_ready = (st.sem("a_v_done"), st.sem("a_v_kept"),
                                                st.sem("a_khi_ready"), st.sem("a_klo_ready"))
        block = s.enter_context(nc.Block())
        LOADS = 8

        @block.sync
        def _(sp):
            for b in range(NB):
                sp.dma_start(x[:, b * TPB:(b + 1) * TPB, :],
                             io["x"][b].rearrange("(t p) d -> p t d", p=P)).then_inc(x_in[b], 16)
            for b in range(NB):
                own = slice(b * SEQ, (b + 1) * SEQ)
                sp.wait_ge(klo_ready, 2 * b + 2)
                sp.dma_start(k_dram[0, :, own], khi[:, own]).then_inc(k_stored, 16)
                sp.dma_start(k_dram[1, :, own], klo[:, own]).then_inc(k_stored, 16)
            sp.wait_ge(k_stored, 32 * NB)

        @block.scalar
        def _(act):
            act.dma_start(ident[:], io["ident"]).then_inc(w_in, 16)
            act.dma_start(wqk[:], io["wqk_T"]).then_inc(w_in, 16)
            act.dma_start(wv[:], io["wv_T"]).then_inc(w_in, 16)
            act.dma_start(bqk[:], io["bqk"]).then_inc(w_in, 16)
            act.dma_start(bv[:], io["bv"].broadcast_to([P, D])).then_inc(w_in, 16)
            act.dma_start(rope[:], io["rope"]).then_inc(w_in, 16)
            act.dma_start(wpre[:], io["wpre"]).then_inc(w_in, 16)
            act.dma_start(wpost[:], io["wpost"].broadcast_to([P, HA * D])).then_inc(w_in, 16)
            layernorm_scalar(act, ln)
            for c in range(NCH + 2):
                if c < NCH:
                    act.wait_ge(transposed, c + 1)
                    act.copy(hT[:, c * CH:(c + 1) * CH], tps[c % 2][:]).then_inc(hT_ready, 1)
                if 1 <= c <= NCH:
                    m = c - 1
                    act.wait_ge(v_done, m + 1)
                    act.copy(v[:, m * CH:(m + 1) * CH], vps[m % 2][:]).then_inc(v_kept, 1)
                if c >= 2:
                    m = c - 2
                    act.wait_ge(qk_summed, 2 * m + 2)
                    act.copy(khi[:, m * CH:(m + 1) * CH], kT[:, m % 2, :]).then_inc(khi_ready, 1)

        @block.tensor
        def _(pe):
            pe.wait_ge(w_in, 16 * LOADS)
            for c in range(NCH + 1):
                if c < NCH:
                    pe.wait_ge(ln.normed, 4 * c + 4)
                    if c >= 2:
                        pe.wait_ge(hT_ready, c - 1)
                    for k in range(4):
                        last = pe.transpose(tps[c % 2][:, k * P:(k + 1) * P], ln.xn[:, 4 * c + k, :], ident[:])
                    last.then_inc(transposed, 1)
                if c >= 1:
                    m = c - 1
                    pe.wait_ge(hT_ready, m + 1)
                    if m >= 2:
                        pe.wait_ge(v_kept, m - 1)
                    for k in range(4):
                        last = pe.matmul(vps[m % 2][:, k * D:(k + 1) * D],
                                         hT[:, m * CH + k * P:m * CH + (k + 1) * P], wv[:],
                                         start=(k == 0), stop=True, skip_group_check=True)
                    last.then_inc(v_done, 1)
                    for i in range(4):
                        if m >= 1:
                            pe.wait_ge(prod_ready, 4 * (m - 1) + i + 1)
                        pe.matmul(qkps[i][:], wqk[:, i, :], hT[:, m * CH:(m + 1) * CH],
                                  start=True, stop=True).then_inc(qk_done, 1)

        @block.vector
        def _(dve):
            layernorm_vector(dve, ln, x, lambda b: dve.wait_ge(x_in[b], 16))
            dve.wait_ge(w_in, 16 * LOADS)

            def bias_v(c):
                dve.wait_ge(v_kept, c + 1)
                vv = v[:, c * CH:(c + 1) * CH].rearrange("p (k d) -> p k d", k=4)
                dve.tensor_tensor(vv, vv, bv[:, None, :].broadcast_to([P, 4, D]), ALU.add)

            for c in range(NCH):
                at = (c * CH) % SEQ
                for i in range(4):
                    if c >= 2:
                        dve.wait_ge(qk_summed, 2 * (c - 2) + i // 2 + 1)
                    dve.wait_ge(qk_done, 4 * c + i + 1)
                    dve.scalar_tensor_tensor(out=prod[:, i, c % 2, :], in0=qkps[i][:], scalar=bqk[:, i:i + 1],
                                             in1=rope[:, i, at:at + CH], op0=ALU.add,
                                             op1=ALU.mult).then_inc(prod_ready, 1)
                bias_v(c)

        @block.gpsimd
        def _(pool):
            pool.memset(accT[:], 0.0)
            for c in range(NCH):
                pool.wait_ge(prod_ready, 4 * c + 2)
                pool.tensor_tensor(qT[:, c * CH:(c + 1) * CH], prod[:, 0, c % 2, :], prod[:, 1, c % 2, :],
                                   ALU.add).then_inc(qk_summed, 1)
                pool.wait_ge(prod_ready, 4 * c + 4)
                if c >= 2:
                    pool.wait_ge(khi_ready, c - 1)
                pool.tensor_tensor(kT[:, c % 2, :], prod[:, 2, c % 2, :], prod[:, 3, c % 2, :],
                                   ALU.add).then_inc(qk_summed, 1)
                pool.wait_ge(khi_ready, c + 1)
                pool.wait_ge(qk_summed, 2 * c + 2)
                pool.tensor_tensor(klo[:, c * CH:(c + 1) * CH], kT[:, c % 2, :], khi[:, c * CH:(c + 1) * CH],
                                   ALU.subtract).then_inc(klo_ready, 1)


def attend_a(st, qT, v, k_dram, wpre, wpost, accT):
    nc = st.nc
    heads = NB * HA
    turns = heads // 2
    tpb = turns // NB
    with ExitStack() as s:
        probs = st.sb(s, "a_probs", [P, 4, SEQ])
        parts = st.sb(s, "a_parts", [P, 4, 2, SEQ], F16)
        pT = st.sb(s, "a_pT", [P, UNITS, 2, JB, HALF], F16)
        negmax = st.sb(s, "a_negmax", [P, TURN_T])
        den = st.sb(s, "a_den", [P, TURN_T])
        dens = st.sb(s, "a_dens", [P, TURN_T])
        rden = st.sb(s, "a_rden", [P, TURN_T])
        kcur = st.sb(s, "a_kcur", [P, 2, SEQ], F16)
        qs = st.sb(s, "a_qs", [P, 2, 2, SEQ], F16)
        qtmp = st.sb(s, "a_qtmp", [P, SEQ])
        vs = st.sb(s, "a_vs", [P, 2, 2, JB, D], F16)
        vtmp = st.sb(s, "a_vtmp", [P, JB, D])
        score_ps = [st.ps(s, f"a_score_ps{i}", [P, SEQ]) for i in range(2)]
        out_ps = [st.ps(s, f"a_out_ps{i}", [P, HALF]) for i in range(2)]

        k_in = st.sem("a_k_in")
        q_scaled = st.sem("a_q_scaled")
        q_step = st.sem("a_q_step")
        v_step = st.sem("a_v_step")
        scored = st.sem("a_scored")
        max_ready = st.sem("a_max_ready")
        exp_done = st.sem("a_exp_done")
        dens_ready = st.sem("a_dens_ready")
        rden_ready = st.sem("a_rden_ready")
        hi_ready = st.sem("a_hi_ready")
        lo_ready = st.sem("a_lo_ready")
        hi_turned = [st.sem(f"a_hi_turned{i}") for i in range(4)]
        lo_turned = [st.sem(f"a_lo_turned{i}") for i in range(4)]
        pv_done = st.sem("a_pv_done")
        out_kept = st.sem("a_out_kept")
        sp_passed = st.sem("a_sp_passed")
        act_passed, pool_passed = st.sem("a_act_passed"), st.sem("a_pool_passed")
        block = s.enter_context(nc.Block())

        @block.sync
        def _(sp):
            def load_k(b):
                for part in range(2):
                    sp.dma_start(kcur[:, part, :], k_dram[part, :, bass.ds(b * SEQ, SEQ)]).then_inc(k_in, 16)

            def transpose_tile(n, t):
                u, k = t // TILES, t % TILES
                if k == 0 and not (isinstance(n, int) and n == 0):
                    wait_apart(sp, sp_passed, pv_done, TURN_J * n - TURN_J + JB * (u + 1))
                T = TURN_T * n + t
                wait_apart(sp, sp_passed, hi_ready, T + 1)
                sp.dma_start_transpose(pT[:, u, 0, :, k * P:(k + 1) * P],
                                       parts[:, k, 0, :]).then_inc(hi_turned[k], 16)
                wait_apart(sp, sp_passed, lo_ready, T + 1)
                sp.dma_start_transpose(pT[:, u, 1, :, k * P:(k + 1) * P],
                                       parts[:, k, 1, :]).then_inc(lo_turned[k], 16)

            load_k(0)
            for t in range(TURN_T):
                transpose_tile(0, t)

            def one_turn(n):
                for t in range(TURN_T):
                    transpose_tile(n, t)

            for b in range(NB):
                with sp.Fori(b * tpb + (b == 0), (b + 1) * tpb - 1) as n:
                    one_turn(n)
                n = (b + 1) * tpb - 1
                for t in range(TURN_T):
                    if t == K_LOAD_AT and b + 1 < NB:
                        sp.wait_ge(scored, TURN_T * (n + 1))
                        load_k(b + 1)
                    transpose_tile(n, t)

        @block.tensor
        def _(pe):
            def scores(n, t):
                n, t = n + t // TURN_T, t % TURN_T
                slot, half, k = t // 8, t // 4 % 2, t % 4
                T = TURN_T * n + t
                if not (isinstance(n, int) and T < 2):
                    pe.wait_ge(exp_done, T - 1)
                cols = slice(half * HALF + k * P, half * HALF + (k + 1) * P)
                out = score_ps[t % 2]
                if t % 8 == 0:
                    pe.wait_ge(q_step, 2 * (2 * n + slot + 1))
                    if slot == 0:
                        pe.wait_ge(k_in, 32 * (n // tpb + 1))
                q0, q1 = qs[:, slot, 0, cols], qs[:, slot, 1, cols]
                for c in range(2):
                    kc = slice(c * CH, (c + 1) * CH)
                    pe.matmul(out[:, kc], q0, kcur[:, 0, kc], start=True, stop=False)
                    pe.matmul(out[:, kc], q0, kcur[:, 1, kc], start=False, stop=False)
                for c in range(2):
                    kc = slice(c * CH, (c + 1) * CH)
                    last = pe.matmul(out[:, kc], q1, kcur[:, 0, kc], start=False, stop=True)
                last.then_inc(scored, 1)

            def times_v(n, j):
                u, jb = j // JB, j % JB
                slot, half = u // 2, u % 2
                if jb == 0:
                    for k in range(TILES):
                        count = 16 * (UNITS * n + u + 1)
                        pe.wait_ge(hi_turned[k], count)
                        pe.wait_ge(lo_turned[k], count)
                    if half == 0:
                        pe.wait_ge(v_step, 3 * (2 * n + slot + 1))
                    if slot == 0 and not (isinstance(n, int) and n == 0):
                        pe.wait_ge(out_kept, 2 * n - 1 + half)
                hi, lo = pT[:, u, 0, jb, :], pT[:, u, 1, jb, :]
                first, final = slot == 0 and jb == 0, slot == 1 and jb == JB - 1
                out = out_ps[half][:]
                pe.matmul(out, vs[:, slot, 0, jb, :], hi, start=first, stop=False, skip_group_check=True)
                pe.matmul(out, vs[:, slot, 0, jb, :], lo, start=False, stop=False, skip_group_check=True)
                pe.matmul(out, vs[:, slot, 1, jb, :], hi, start=False, stop=final,
                          skip_group_check=True).then_inc(pv_done, 1)

            def one_turn(n, last):
                for t in range(TURN_T):
                    if not (last and t + AHEAD_A >= TURN_T):
                        scores(n, t + AHEAD_A)
                    times_v(n, 2 * t)
                    times_v(n, 2 * t + 1)

            for t in range(AHEAD_A):
                scores(0, t)
            one_turn(0, False)
            with pe.Fori(1, turns - 1) as n:
                one_turn(n, False)
            one_turn(turns - 1, True)

        @block.scalar
        def _(act):
            def exponentiate(n, t):
                n, t = n + t // TURN_T, t % TURN_T
                T = TURN_T * n + t
                act.wait_ge(max_ready, T + 1)
                if not (isinstance(n, int) and n == 0 and t < 4):
                    act.wait_ge(lo_ready, T - 3)
                act.activation(probs[:, t % 4, :], score_ps[t % 2][:], ACT.Exp, bias=negmax[:, t:t + 1],
                               accum_out=den[:, t:t + 1]).then_inc(exp_done, 1)
                act.wait_ge(exp_done, T + 1)
                act.mul(dens[:, t:t + 1], den[:, t:t + 1], 1.0 / PSCALE).then_inc(dens_ready, 1)

            def scale_q(g):
                if not (isinstance(g, int) and g == 0):
                    wait_apart(act, act_passed, q_step, 2 * g)
                act.activation(qtmp[:], qT[:, bass.ds((g // HA) * SEQ, SEQ)], ACT.Copy,
                               scale=wpre[:, bass.ds(g % HA, 1)]).then_inc(q_scaled, 1)

            def one_turn(n, last):
                for t in range(AHEAD_A, AHEAD_A + TURN_T):
                    if not (last and t >= TURN_T):
                        exponentiate(n, t)
                        if t % 8 == 2 and not last:
                            scale_q(2 * n + t // 8 + 1)

            scale_q(0)
            for t in range(AHEAD_A):
                exponentiate(0, t)
                if t == 2:
                    scale_q(1)
            one_turn(0, False)
            with act.Fori(1, turns - 1) as n:
                one_turn(n, False)
            one_turn(turns - 1, True)

        @block.vector
        def _(dve):
            def row_max(n, t):
                n, t = n + t // TURN_T, t % TURN_T
                dve.wait_ge(scored, TURN_T * n + t + 1)
                dve.tensor_reduce(negmax[:, t:t + 1], score_ps[t % 2][:], AX.X, ALU.max,
                                  negate=True).then_inc(max_ready, 1)

            def invert(n, t):
                n, t = n + t // TURN_T, t % TURN_T
                dve.wait_ge(dens_ready, TURN_T * n + t + 1)
                dve.reciprocal(rden[:, t:t + 1], dens[:, t:t + 1]).then_inc(rden_ready, 1)

            def low(n, t):
                n, t = n + t // TURN_T, t % TURN_T
                T = TURN_T * n + t
                dve.wait_ge(hi_ready, T + 1)
                if not (isinstance(n, int) and n == 0 and t < 4):
                    dve.wait_ge(lo_turned[t % 4], 16 * (UNITS * n + t // TILES))
                dve.scalar_tensor_tensor(out=parts[:, t % 4, 1, :], in0=probs[:, t % 4, :],
                                         scalar=rden[:, t:t + 1], in1=parts[:, t % 4, 0, :],
                                         op0=ALU.mult, op1=ALU.subtract).then_inc(lo_ready, 1)

            def keep(n, half):
                dve.wait_ge(pv_done, TURN_J * n + (3 + half) * JB)
                to = accT[:, bass.ds((n // tpb) * SEQ + half * HALF, HALF)]
                dve.tensor_tensor(to, out_ps[half][:], to, ALU.add).then_inc(out_kept, 1)

            def one_turn(n, first, last):
                for t in range(TURN_T):
                    ahead = t + AHEAD_A
                    if not (last and ahead >= TURN_T):
                        row_max(n, ahead)
                    if not (last and ahead > TURN_T):
                        invert(n, ahead - 1)
                    if not (last and ahead > TURN_T + 1):
                        low(n, ahead - 2)
                    if t == 1 and not first:
                        keep(n - 1, 1)
                    if t == 13:
                        keep(n, 0)

            for t in range(AHEAD_A):
                row_max(0, t)
                if t > 0:
                    invert(0, t - 1)
                if t > 1:
                    low(0, t - 2)
            one_turn(0, True, False)
            with dve.Fori(1, turns - 1) as n:
                one_turn(n, False, False)
            one_turn(turns - 1, False, True)
            keep(turns - 1, 1)

        @block.gpsimd
        def _(pool):
            def q_part(g, slot, i, first=False):
                if i == 0:
                    wait_apart(pool, pool_passed, q_scaled, g + 1)
                    if not first:
                        wait_apart(pool, pool_passed, scored, 2 * TILES * (g - 1))
                    pool.tensor_scalar(qs[:, slot, 0, :], qtmp[:], 1.0, 1.0, ALU.mult,
                                       ALU.mult).then_inc(q_step, 1)
                else:
                    pool.wait_ge(q_step, 2 * g + 1)
                    pool.tensor_tensor(qs[:, slot, 1, :], qtmp[:], qs[:, slot, 0, :],
                                       ALU.subtract).then_inc(q_step, 1)

            def v_part(g, slot, i, first=False):
                b, h = g // HA, g % HA
                if i == 0:
                    src = v[:, bass.ds(b * SEQ, SEQ)].rearrange("p (j d) -> p j d", j=JB)
                    w = wpost[:, bass.ds(h * D, D)][:, None, :].broadcast_to([P, JB, D])
                    pool.tensor_tensor(vtmp[:], src, w, ALU.mult).then_inc(v_step, 1)
                elif i == 1:
                    wait_apart(pool, pool_passed, v_step, 3 * g + 1)
                    if not first:
                        wait_apart(pool, pool_passed, pv_done, 2 * JB * (g - 1))
                    pool.tensor_scalar(vs[:, slot, 0, :, :], vtmp[:], 1.0, 1.0, ALU.mult,
                                       ALU.mult).then_inc(v_step, 1)
                else:
                    pool.wait_ge(v_step, 3 * g + 2)
                    pool.tensor_tensor(vs[:, slot, 1, :, :], vtmp[:], vs[:, slot, 0, :, :],
                                       ALU.subtract).then_inc(v_step, 1)

            def high(n, t):
                if not (isinstance(n, int) and n == 0 and t < 4):
                    wait_apart(pool, pool_passed, hi_turned[t % 4], 16 * (UNITS * n + t // TILES))
                wait_apart(pool, pool_passed, rden_ready, TURN_T * n + t + 1)
                pool.tensor_scalar(parts[:, t % 4, 0, :], probs[:, t % 4, :], rden[:, t:t + 1], 1.0,
                                   ALU.mult, ALU.mult).then_inc(hi_ready, 1)

            def one_turn(n, first, last):
                for t in range(TURN_T):
                    high(n, t)
                    slot, k = t // 8, t % 8
                    more = not (last and slot == 1)
                    if k == 2 and more:
                        q_part(2 * n + slot + 1, 1 - slot, 0, first and slot == 0)
                    if k == 3 and more:
                        q_part(2 * n + slot + 1, 1 - slot, 1)
                    if k in (4, 5, 6):
                        v_part(2 * n + slot, slot, k - 4, first)

            for i in range(2):
                q_part(0, 0, i, True)
            one_turn(0, True, False)
            with pool.Fori(1, turns - 1) as n:
                one_turn(n, False, False)
            one_turn(turns - 1, False, True)


def attend_b(st, q_dram, k_dram, v_dram, oT, ident):
    nc = st.nc
    heads = NB * HB
    turns = heads // 2
    vw = 2 * HDB
    turned_js = [j for j in range(TURN_J) if j % JB not in SENT]
    splits = [j for j in turned_js if j % JB not in FULL]
    act_js = [j for j in turned_js if j % JB not in DVE_FULL]
    dve_js = [j for j in turned_js if j % JB in DVE_FULL]
    fulls = [j for j in turned_js if j % JB in FULL]
    last_in_bank = [[j for m, j in enumerate(turned_js) if m % TURN_BANKS == bank][-1] for bank in range(TURN_BANKS)]
    n_sent = len(SENT)
    sent0 = (JB - n_sent) * P

    def index(kind, j):
        return sum(i < j for i in kind)

    with ExitStack() as s:
        probs = st.sb(s, "b_probs", [P, TURN_T, SEQ])
        pT = st.sb(s, "b_pT", [P, SPLIT_RING, 2, HALF], F16)
        pT32 = st.sb(s, "b_pT32", [P, FULL_RING, HALF])
        parts = st.sb(s, "b_sent_parts", [P, TILES, 2, n_sent * P], F16)
        pTs = st.sb(s, "b_sent_pT", [P, UNITS, 2, n_sent, HALF], F16)
        negmax = st.sb(s, "b_negmax", [P, TURN_T])
        den = st.sb(s, "b_den", [P, TURN_T])
        rden = st.sb(s, "b_rden", [P, TURN_T])
        qs = st.sb(s, "b_qs", [P, 2, SEQ], F16)
        ks = st.sb(s, "b_ks", [P, 2, SEQ], F16)
        vs = st.sb(s, "b_vs", [P, 2, JB, vw], F16)
        v32 = st.sb(s, "b_v32", [P, 2, JB, HDB])
        score_ps = [st.ps(s, f"b_score_ps{i}", [P, SEQ]) for i in range(2)]
        turn_ps = [st.ps(s, f"b_turn_ps{i}", [P, HALF]) for i in range(TURN_BANKS)]
        out_ps = [st.ps(s, f"b_out_ps{i}", [P, HALF]) for i in range(2)]
        half_sum = st.sb(s, "b_half_sum", [vw, HALF])

        scored = st.sem("b_scored")
        max_ready = st.sem("b_max_ready")
        exp_done = st.sem("b_exp_done")
        rden_ready = st.sem("b_rden_ready")
        normed = st.sem("b_normed")
        high_made = st.sem("b_high_made")
        parts_ready = st.sem("b_parts_ready")
        sent = [st.sem(f"b_sent{i}") for i in range(TILES)]
        turned = st.sem("b_turned")
        copied = st.sem("b_copied")
        dve_copied = st.sem("b_dve_copied")
        half_kept = st.sem("b_half_kept")
        lo_ready = st.sem("b_lo_ready")
        pv_done = st.sem("b_pv_done")
        out_kept = st.sem("b_out_kept")
        qk_in = [st.sem(f"b_qk_in{i}") for i in range(2)]
        v_in = [st.sem(f"b_v_in{i}") for i in range(2)]
        v_ready = st.sem("b_v_ready")
        pool_passed, sp_passed = st.sem("b_pool_passed"), st.sem("b_sp_passed")
        block = s.enter_context(nc.Block())

        def wait_slot(eng, n, kind, ring, j):
            i = index(kind, j)
            if not (isinstance(n, int) and n == 0 and i < ring):
                eng.wait_ge(pv_done, TURN_J * n + (kind[i - ring] if i >= ring else kind[i - ring] - TURN_J) + 1)

        @block.sync
        def _(sp):
            def load_qk(g, slot, part):
                rows = slice(part * HDB, (part + 1) * HDB)
                sp.dma_start(qs[rows, slot, :], q_dram[part // 2, bass.ds(g, 1)]
                             .rearrange("o d t -> (o d) t")).then_inc(qk_in[slot], 16)
                sp.dma_start(ks[rows, slot, :], k_dram[part % 2, bass.ds(g, 1)]
                             .rearrange("o d t -> (o d) t")).then_inc(qk_in[slot], 16)

            def transpose_sent(n, t):
                u, k = t // TILES, t % TILES
                if k == 0 and not (isinstance(n, int) and n == 0):
                    wait_apart(sp, sp_passed, pv_done, TURN_J * n - TURN_J + JB * (u + 1))
                wait_apart(sp, sp_passed, parts_ready, TURN_T * n + t + 1)
                sp.dma_start_transpose(pTs[:, u, :, :, k * P:(k + 1) * P].rearrange("p a j q -> p (a j) q"),
                                       parts[:, k, :, :].rearrange("p a c -> p (a c)")).then_inc(sent[k], 16)

            def load_v(g, slot):
                sp.dma_start(vs[:, slot, :, :].rearrange("p j d -> p (j d)"),
                             v_dram[bass.ds(g, 1)].rearrange("o p c -> (o p) c")).then_inc(v_in[slot], 16)

            def one_turn(n, first, last):
                for t in range(TURN_T):
                    transpose_sent(n, t)
                    if t == V_LOAD_AFTER[1] and not first:
                        wait_apart(sp, sp_passed, pv_done, TURN_J * n)
                        load_v(2 * n + 1, 1)
                    if t == V_LOAD_AFTER[0] and not last:
                        wait_apart(sp, sp_passed, pv_done, TURN_J * n + 2 * JB)
                        load_v(2 * n + 2, 0)
                    slot, part = t // (2 * TILES), t % (2 * TILES) - LOAD_AFTER
                    if part == 0 and not last:
                        wait_apart(sp, sp_passed, scored, TURN_T * n + 2 * TILES * (slot + 1))
                    if 0 <= part < 4 and not last:
                        load_qk(2 * n + 2 + slot, slot, part)

            for slot in range(2):
                for part in range(4):
                    load_qk(slot, slot, part)
                load_v(slot, slot)
            one_turn(0, True, False)
            with sp.Fori(1, turns - 1) as n:
                one_turn(n, False, False)
            one_turn(turns - 1, False, True)

        @block.tensor
        def _(pe):
            def scores(n, t):
                n, t = n + t // TURN_T, t % TURN_T
                slot, half, k = t // 8, t // 4 % 2, t % 4
                T = TURN_T * n + t
                if not (isinstance(n, int) and T < 2):
                    pe.wait_ge(exp_done, T - 1)
                cols = slice(half * HALF + k * P, half * HALF + (k + 1) * P)
                if t % 8 == 0:
                    pe.wait_ge(qk_in[slot], 128 * (n + 1))
                for c in range(2):
                    kc = slice(c * CH, (c + 1) * CH)
                    last = pe.matmul(score_ps[t % 2][:, kc], qs[:, slot, cols], ks[:, slot, kc],
                                     start=True, stop=True)
                last.then_inc(scored, 1)

            def turn(n, j):
                u, jb, m = j // JB, j % JB, index(turned_js, j)
                if jb == 0:
                    pe.wait_ge(normed, TURN_T * n + TILES * (u + 1))
                if not (isinstance(n, int) and n == 0 and m < TURN_BANKS):
                    back = turned_js[m - TURN_BANKS] if m >= TURN_BANKS else last_in_bank[m] - TURN_J
                    wait_parts(n, back)
                for k in range(TILES):
                    last = pe.transpose(turn_ps[m % TURN_BANKS][:, k * P:(k + 1) * P],
                                        probs[:, TILES * u + k, ORDER[jb] * P:(ORDER[jb] + 1) * P], ident[:])
                last.then_inc(turned, 1)

            def wait_parts(n, j):
                n, j = n + j // TURN_J, j % TURN_J
                if j % JB in SENT:
                    if j % JB == min(SENT):
                        for k in range(TILES):
                            pe.wait_ge(sent[k], 16 * (UNITS * n + j // JB + 1))
                elif j % JB in DVE_FULL:
                    pe.wait_ge(dve_copied, len(dve_js) * n + index(dve_js, j) + 1)
                elif j % JB in FULL:
                    pe.wait_ge(copied, len(act_js) * n + index(act_js, j) + 1)
                else:
                    pe.wait_ge(lo_ready, len(splits) * n + index(splits, j) + 1)

            def times_v(n, j):
                n, j = n + j // TURN_J, j % TURN_J
                u, jb = j // JB, j % JB
                slot, half, kb = u // 2, u % 2, ORDER[jb]
                wait_parts(n, j)
                if jb == 0:
                    if half == 0:
                        pe.wait_ge(v_ready, 2 * n + slot + 1)
                    if not (isinstance(n, int) and n == 0 and slot == 0):
                        pe.wait_ge(out_kept, UNITS * n + u - 1)
                out = out_ps[half]
                if jb in FULL:
                    for i in range(P // HDB):
                        own = slice(i * P, (i + 1) * P)
                        last = pe.matmul(out[i * HDB:(i + 1) * HDB, own], v32[:, slot, kb, :],
                                         pT32[:, index(fulls, j) % FULL_RING, own], start=False, stop=False,
                                         skip_group_check=True)
                else:
                    for part in range(2):
                        if jb in SENT:
                            moving = pTs[:, u, part, kb - (JB - n_sent), :]
                        else:
                            moving = pT[:, index(splits, j) % SPLIT_RING, part, :]
                        last = pe.matmul(out[part * vw:(part + 1) * vw, :], vs[:, slot, kb, :], moving,
                                         start=jb == 0, stop=jb == JB - 1, skip_group_check=True)
                last.then_inc(pv_done, 1)

            def one_turn(n, first, last):
                for t in range(TURN_T):
                    if not (last and t + AHEAD_B >= TURN_T):
                        scores(n, t + AHEAD_B)
                    for j in (2 * t, 2 * t + 1):
                        if j % JB not in SENT:
                            turn(n, j)
                        if not (first and j < LAG):
                            times_v(n, j - LAG)

            for t in range(AHEAD_B):
                scores(0, t)
            one_turn(0, True, False)
            with pe.Fori(1, turns - 1) as n:
                one_turn(n, False, False)
            one_turn(turns - 1, False, True)
            for j in range(LAG):
                times_v(turns, j - LAG)

        @block.scalar
        def _(act):
            def exponentiate(n, t):
                n, t = n + t // TURN_T, t % TURN_T
                act.wait_ge(max_ready, TURN_T * n + t + 1)
                if t % TILES == 0 and not (isinstance(n, int) and n == 0):
                    unit = JB - n_sent
                    act.wait_ge(turned, unit * (UNITS * n - UNITS + t // TILES + 1))
                    act.wait_ge(parts_ready, TURN_T * n - TURN_T + t + TILES)
                act.activation(probs[:, t, :], score_ps[t % 2][:], ACT.Exp, bias=negmax[:, t:t + 1],
                               accum_out=den[:, t:t + 1]).then_inc(exp_done, 1)

            def copy_block(n, j):
                m, full = index(turned_js, j), j % JB in FULL
                act.wait_ge(turned, len(turned_js) * n + m + 1)
                kind, ring = (fulls, FULL_RING) if full else (splits, SPLIT_RING)
                wait_slot(act, n, kind, ring, j)
                i = index(kind, j)
                to = pT32[:, i % ring, :] if full else pT[:, i % ring, 0, :]
                act.copy(to, turn_ps[m % TURN_BANKS][:]).then_inc(copied, 1)

            def one_turn(n, last):
                for t in range(TURN_T):
                    for j in (2 * t, 2 * t + 1):
                        if j in turned_js and j % JB not in DVE_FULL:
                            copy_block(n, j)
                    if not (last and t + AHEAD_B >= TURN_T):
                        exponentiate(n, t + AHEAD_B)

            for t in range(AHEAD_B):
                exponentiate(0, t)
            one_turn(0, False)
            with act.Fori(1, turns - 1) as n:
                one_turn(n, False)
            one_turn(turns - 1, True)

        @block.vector
        def _(dve):
            def row_max(n, t):
                n, t = n + t // TURN_T, t % TURN_T
                dve.wait_ge(scored, TURN_T * n + t + 1)
                dve.tensor_reduce(negmax[:, t:t + 1], score_ps[t % 2][:], AX.X, ALU.max,
                                  negate=True).then_inc(max_ready, 1)

            def invert(n, t):
                n, t = n + t // TURN_T, t % TURN_T
                dve.wait_ge(exp_done, TURN_T * n + t + 1)
                dve.reciprocal(rden[:, t:t + 1], den[:, t:t + 1]).then_inc(rden_ready, 1)

            def low(n, j):
                m, ring = index(turned_js, j), index(splits, j) % SPLIT_RING
                dve.wait_ge(copied, len(act_js) * n + index(act_js, j) + 1)
                dve.tensor_tensor(pT[:, ring, 1, :], turn_ps[m % TURN_BANKS][:], pT[:, ring, 0, :],
                                  ALU.subtract).then_inc(lo_ready, 1)

            def copy_block(n, j):
                m = index(turned_js, j)
                dve.wait_ge(turned, len(turned_js) * n + m + 1)
                wait_slot(dve, n, fulls, FULL_RING, j)
                dve.tensor_copy(pT32[:, index(fulls, j) % FULL_RING, :],
                                turn_ps[m % TURN_BANKS][:]).then_inc(dve_copied, 1)

            def keep(n, u, i):
                slot, half = u // 2, u % 2
                rows = slice(slot * vw, (slot + 1) * vw)
                out, unit = out_ps[half], UNITS * n + u
                if i == 0:
                    dve.wait_ge(pv_done, TURN_J * n + (u + 1) * JB)
                    if not (isinstance(n, int) and n == 0 and u == 0):
                        dve.wait_ge(out_kept, unit)
                    dve.tensor_copy(half_sum[:], out[vw:, :]).then_inc(half_kept, 1)
                else:
                    dve.wait_ge(half_kept, unit + 1)
                    dve.tensor_tensor(oT[rows, bass.ds(n * SEQ + half * HALF, HALF)], out[:vw, :], half_sum[:],
                                      ALU.add).then_inc(out_kept, 1)

            def one_turn(n, first, last):
                for t in range(TURN_T):
                    if not (last and t + AHEAD_B >= TURN_T):
                        row_max(n, t + AHEAD_B)
                    for j in (2 * t, 2 * t + 1):
                        if j in splits:
                            low(n, j)
                        elif j in dve_js:
                            copy_block(n, j)
                    if not (last and t + AHEAD_B > TURN_T):
                        invert(n, t + AHEAD_B - 1)
                    if t % 4 in (1, 2) and not (first and t < 4):
                        keep(n if t >= 4 else n - 1, (t // 4 - 1) % UNITS, t % 4 - 1)

            for t in range(AHEAD_B):
                row_max(0, t)
                if t:
                    invert(0, t - 1)
            one_turn(0, True, False)
            with dve.Fori(1, turns - 1) as n:
                one_turn(n, False, False)
            one_turn(turns - 1, False, True)
            for i in range(2):
                keep(turns - 1, UNITS - 1, i)

        @block.gpsimd
        def _(pool):
            def prepare_v(n, slot, first):
                if not first:
                    wait_apart(pool, pool_passed, pv_done, TURN_J * n - TURN_J + 2 * JB * (slot + 1))
                pool.wait_ge(v_in[slot], 16 * (n + 1))
                pool.tensor_tensor(v32[:, slot, :, :], vs[:, slot, :, :HDB], vs[:, slot, :, HDB:],
                                   ALU.add).then_inc(v_ready, 1)

            def normalise(n, t):
                wait_apart(pool, pool_passed, rden_ready, TURN_T * n + t + 1)
                pool.tensor_scalar(probs[:, t, :], probs[:, t, :], rden[:, t:t + 1], PSCALE,
                                   ALU.mult, ALU.mult).then_inc(normed, 1)

            def high(n, t):
                n, t = n + t // TURN_T, t % TURN_T
                if not (isinstance(n, int) and n == 0 and t < TILES):
                    wait_apart(pool, pool_passed, sent[t % TILES], 16 * (UNITS * n + t // TILES))
                wait_apart(pool, pool_passed, normed, TURN_T * n + t + 1)
                pool.tensor_scalar(parts[:, t % TILES, 0, :], probs[:, t, sent0:], 1.0, 1.0, ALU.mult,
                                   ALU.mult).then_inc(high_made, 1)

            def low(n, t):
                n, t = n + t // TURN_T, t % TURN_T
                pool.wait_ge(high_made, TURN_T * n + t + 1)
                pool.tensor_tensor(parts[:, t % TILES, 1, :], probs[:, t, sent0:], parts[:, t % TILES, 0, :],
                                   ALU.subtract).then_inc(parts_ready, 1)

            def one_turn(n, first):
                for t in range(TURN_T):
                    normalise(n, t)
                    if not (first and t < 1):
                        high(n, t - 1)
                    if not (first and t < 2):
                        low(n, t - 2)
                    if t % 8 == 3:
                        prepare_v(n, t // 8, first)

            one_turn(0, True)
            with pool.Fori(1, turns) as n:
                one_turn(n, False)
            low(turns, -2)
            high(turns, -1)
            low(turns, -1)


def project_a(st, io, x, accT):
    nc = st.nc
    with ExitStack() as s:
        wout = st.sb(s, "pa_wout", [P, D])
        bout = st.sb(s, "pa_bout", [P, D])
        xb = st.sb(s, "pa_xb", [P, NT, D])
        y = [st.ps(s, f"pa_y{i}", [P, 4, D]) for i in range(2)]
        w_in, y_done, bias_added, y_read = (st.sem("pa_w_in"), st.sem("pa_y_done"),
                                            st.sem("pa_bias_added"), st.sem("pa_y_read"))
        block = s.enter_context(nc.Block())

        @block.sync
        def _(sp):
            sp.dma_start(wout[:], io["wout_T"]).then_inc(w_in, 16)
            sp.dma_start(bout[:], io["bout"].broadcast_to([P, D])).then_inc(w_in, 16)

        @block.tensor
        def _(pe):
            pe.wait_ge(w_in, 32)
            for c in range(NCH):
                if c >= 2:
                    pe.wait_ge(y_read, c - 1)
                for k in range(4):
                    t = 4 * c + k
                    last = pe.matmul(y[c % 2][:, k, :], accT[:, t * P:(t + 1) * P], wout[:],
                                     start=(k == 0), stop=True, skip_group_check=True)
                last.then_inc(y_done, 1)

        @block.gpsimd
        def _(pool):
            pool.wait_ge(w_in, 32)
            for c in range(NCH):
                pool.tensor_tensor(xb[:, 4 * c:4 * c + 4, :], x[:, 4 * c:4 * c + 4, :],
                                   bout[:, None, :].broadcast_to([P, 4, D]), ALU.add).then_inc(bias_added, 1)

        @block.vector
        def _(dve):
            for c in range(NCH):
                dve.wait_ge(bias_added, c + 1)
                dve.wait_ge(y_done, c + 1)
                dve.scalar_tensor_tensor(out=x[:, 4 * c:4 * c + 4, :], in0=y[c % 2][:], scalar=1.0 / PSCALE,
                                         in1=xb[:, 4 * c:4 * c + 4, :], op0=ALU.mult,
                                         op1=ALU.add).then_inc(y_read, 1)


def route(st, io, w, tag, x, xn, oh, ohT, xsel, xh):
    nc = st.nc
    with ExitStack() as s:
        ln = LnWork(st, s, tag + "ln", xn)
        ident = st.sb(s, tag + "ident", [P, P])
        wr = st.sb(s, tag + "wr", [P, D])
        iota = st.sb(s, tag + "iota", [P, 2, 2 * CAP])
        below = st.sb(s, tag + "below", [P, P])
        junk = st.sb(s, tag + "junk", [P, 4, P])
        greater = st.sb(s, tag + "greater", [P, GT_RING, SEQ], F16)
        ones = st.sb(s, tag + "ones", [P, 1], F16)
        score = st.sb(s, tag + "score", [P, NT])
        part = st.sb(s, tag + "part", [P, NT, 3])
        rank = st.sb(s, tag + "rank", [P, NT])
        row = [st.ps(s, f"{tag}row{i}", [P, SEQ]) for i in range(2)]
        sel = st.ps(s, tag + "sel", [P, 2, D])
        passed_by = [st.ps(s, f"{tag}passed_by{i}", [P, TPB]) for i in range(2)]
        tps = st.ps(s, tag + "tps", [P, 4, P])
        w_in, row_ready, rank_ready = st.sem(tag + "w_in"), st.sem(tag + "row_ready"), st.sem(tag + "rank_ready")
        junked = st.sem(tag + "junked")
        compared, counted = st.sem(tag + "compared"), st.sem(tag + "counted")
        totalled, last_oh_ready = st.sem(tag + "totalled"), st.sem(tag + "last_oh_ready")
        tables = st.sem(tag + "tables")
        oh_ready, ohT_done, ohT_kept, sel_done = (st.sem(tag + "oh_ready"), st.sem(tag + "ohT_done"),
                                                  st.sem(tag + "ohT_kept"), st.sem(tag + "sel_done"))
        block = s.enter_context(nc.Block())

        @block.sync
        def _(sp):
            sp.dma_start(wr[:], io["w_router"].broadcast_to([P, D])).then_inc(w_in, 16)
            sp.dma_start(iota[:], io["iota"]).then_inc(w_in, 16)
            sp.dma_start(below[:], io["below"]).then_inc(w_in, 16)
            sp.dma_start(ident[:], io["ident"]).then_inc(w_in, 16)
            for to, source in w.sources:
                sp.dma_start(to[:], source).then_inc(w.loaded, 16)

        @block.scalar
        def _(act):
            layernorm_scalar(act, ln)
            for c in range(NCH):
                act.wait_ge(ohT_done, c + 1)
                act.copy(ohT[:, 4 * c:4 * c + 4, :], tps[:]).then_inc(ohT_kept, 1)
            act.wait_ge(sel_done, 2)
            act.copy(xsel[:], sel[:])

        @block.vector
        def _(dve):
            used = [0]

            def junk_slot(width):
                used[0] += 1
                if used[0] > 4:
                    dve.wait_ge(junked, used[0] - 4)
                return junk[:, used[0] % 4, 0:width]

            layernorm_vector(dve, ln, x, lambda b: None)
            dve.wait_ge(w_in, 64)
            dve.wait_ge(ln.normed, NT)
            for t in range(NT):
                dve.scalar_tensor_tensor(out=junk_slot(D), in0=xn[:, t, :], scalar=1.0, in1=wr[:], op0=ALU.mult,
                                         op1=ALU.mult, accum_out=score[:, t:t + 1]).then_inc(junked, 1)
            dve.wait_ge(junked, NT)
            dve.wait_ge(tables, TPB + 1)

            def finish(b):
                own = slice(b * TPB, (b + 1) * TPB)
                dve.wait_ge(compared, TPB * (b + 1))
                dve.wait_ge(junked, NT + TPB * (b + 1))
                dve.tensor_reduce(rank[:, own], part[:, own, :], AX.X, ALU.add).then_inc(totalled, 1)
                dve.wait_ge(totalled, b + 1)
                dve.wait_ge(counted, (TPB - 1) * (b + 1))
                later = slice(b * TPB + 1, (b + 1) * TPB)
                dve.tensor_tensor(rank[:, later], rank[:, later], passed_by[b % 2][:, 1:],
                                  ALU.subtract).then_inc(rank_ready, 1)

            for b in range(NB):
                dve.wait_ge(row_ready, b + 1)
                bc = row[b % 2]
                for i in range(TPB):
                    t = b * TPB + i
                    own = score[:, t:t + 1]
                    if t >= GT_RING:
                        before = t - GT_RING
                        dve.wait_ge(counted, (TPB - 1) * (before // TPB) + min(before % TPB + 1, TPB - 1))
                    dve.tensor_scalar(greater[:, t % GT_RING, i * P:], bc[:, i * P:], own, None, ALU.is_gt,
                                      ALU.add, accum_out=part[:, t, 1:2]).then_inc(compared, 1)
                    dve.scalar_tensor_tensor(out=junk_slot(P), in0=bc[:, i * P:(i + 1) * P], scalar=own,
                                             in1=below[:], op0=ALU.is_equal, op1=ALU.mult,
                                             accum_out=part[:, t, 2:3]).then_inc(junked, 1)
                    if i == 2 and b:
                        finish(b - 1)
            finish(NB - 1)
            dve.wait_ge(rank_ready, NB)
            for t in range(NT - TPB, NT):
                dve.tensor_scalar(oh[:, t, :], iota[:, (NB - 1) % 2, :], rank[:, t:t + 1], None,
                                  ALU.is_equal).then_inc(last_oh_ready, 1)

        @block.gpsimd
        def _(pool):
            pool.memset(ones[:], 1.0).then_inc(tables, 1)
            for i in range(TPB):
                pool.memset(part[:].rearrange("p (b i) k -> p b i k", i=TPB)[:, :, i, 0],
                            float(i * P)).then_inc(tables, 1)
            pool.wait_ge(w_in, 64)
            pool.wait_ge(ln.normed, NT)
            pool.tensor_tensor(xh[:], x[:], xn[:], ALU.add)
            for t in range(NT - TPB):
                b = t // TPB
                if t % TPB == 0:
                    pool.wait_ge(rank_ready, b + 1)
                pool.tensor_scalar(oh[:, t, :], iota[:, b % 2, :], rank[:, t:t + 1], None,
                                   ALU.is_equal).then_inc(oh_ready, 1)

        @block.tensor
        def _(pe):
            pe.wait_ge(w_in, 64)
            pe.wait_ge(junked, NT)

            def rows(b):
                for i in range(TPB):
                    t = b * TPB + i
                    last = pe.transpose(row[b % 2][:, i * P:(i + 1) * P],
                                        score[:, t:t + 1].broadcast_to([P, P]), ident[:])
                last.then_inc(row_ready, 1)

            def count(b):
                if b >= 2:
                    pe.wait_ge(rank_ready, b - 1)
                for i in range(TPB):
                    t = b * TPB + i
                    pe.wait_ge(compared, t + 1)
                    for j in range(i + 1, TPB):
                        last = pe.matmul(passed_by[b % 2][:, j:j + 1],
                                         greater[:, t % GT_RING, j * P:(j + 1) * P], ones[:],
                                         start=i == 0 and j == 1, stop=True,
                                         skip_group_check=True)
                    if i < TPB - 1:
                        last.then_inc(counted, 1)

            def pick(b):
                for i in range(TPB):
                    t = b * TPB + i
                    if b < NB - 1:
                        pe.wait_ge(oh_ready, t + 1)
                    else:
                        pe.wait_ge(last_oh_ready, i + 1)
                    last = pe.matmul(sel[:, b // 2, :], oh[:, t, :], xn[:, t, :], start=t % (2 * TPB) == 0,
                                     stop=t % (2 * TPB) == 2 * TPB - 1)
                    if t % (2 * TPB) == 2 * TPB - 1:
                        last.then_inc(sel_done, 1)

            def turn(b):
                for c in (2 * b, 2 * b + 1):
                    if c:
                        pe.wait_ge(ohT_kept, c)
                    for k in range(4):
                        last = pe.transpose(tps[:, k, :], oh[:, 4 * c + k, :], ident[:])
                    last.then_inc(ohT_done, 1)

            pe.wait_ge(tables, TPB + 1)
            rows(0)
            rows(1)
            for b in range(NB):
                count(b)
                if b + 2 < NB:
                    pe.wait_ge(junked, NT + TPB * (b + 1))
                    rows(b + 2)
                if b >= 1:
                    pick(b - 1)
                    turn(b - 1)
            pick(NB - 1)
            turn(NB - 1)


class BlockWeights:

    def __init__(self, st, stack, io, tag):
        def sb(name, shape):
            return st.sb(stack, tag + name, shape)

        self.ident, self.g, self.wqkv = sb("ident2", [P, P]), sb("g", [P, 2, D]), sb("wqkv", [P, 3, D])
        self.wout, self.w12, self.w3 = sb("wout", [P, D]), sb("w12", [P, 2, 3 * P]), sb("w3", [P, 3, D])
        self.headm, self.pairm, self.causal = sb("headm", [P, HA]), sb("pairm", [P, D]), sb("causal", [P, CAP])
        self.loaded = st.sem(tag + "w2_in")
        self.sources = ((self.ident, io["ident"]), (self.g, io["g"].broadcast_to([P, 2, D])),
                        (self.wqkv, io["fqkv_T"]), (self.wout, io["fout_T"]), (self.w12, io["w12_T"]),
                        (self.w3, io["w3_T"]), (self.headm, io["headm"]), (self.pairm, io["pairm"]),
                        (self.causal, io["causal"]))


def picked_block(st, wts, tag, x, ohT, xsel, xh):
    nc = st.nc
    QK = 2 * CAP
    with ExitStack() as s:
        def sb(name, shape):
            return st.sb(s, tag + name, shape)

        def sem(name):
            return st.sem(tag + name)

        ident, g, wqkv, wout = wts.ident, wts.g, wts.wqkv, wts.wout
        w12, w3, headm, pairm, causal = wts.w12, wts.w3, wts.headm, wts.pairm, wts.causal
        sq, ss, ve = sb("sq", [P, 2, D]), sb("ss", [P, 2]), sb("ve", [P, 2])
        sd, r0, t0, t1, rms = (sb(n, [P, 2]) for n in ("sd", "r0", "t0", "t1", "rms"))
        hn, hnT, qT = sb("hn", [P, 2, D]), sb("hnT", [P, 2, QK]), sb("qT", [P, 2 * QK])
        kx, vx = sb("kx", [P, NB, HA, CAP]), sb("vx", [P, NB, D])
        sm, mx = sb("sm", [P, 2, HA, CAP]), sb("mx", [P, 2, HA])
        pr_, dn, rd = sb("pr", [P, 2, HA, CAP]), sb("dn", [P, 2, HA]), sb("rd", [P, 2, HA])
        pT = sb("pT", [P, 2, HA // 2, P])
        o, oT = sb("o", [P, 2, D]), sb("oT", [P, 2, QK])
        xa, mid = sb("xa", [P, 2, D]), sb("mid", [P, 2, D])
        e, u = sb("e", [P, 3, 2 * QK]), sb("u", [P, 3, 2 * QK])
        delta = sb("delta", [P, 2, D])
        twice = sb("twice", [P, NB, 2, CAP])
        A, B, C, E = (st.ps(s, tag + n, [P, CH]) for n in "ABCE")
        wide = [st.ps(s, f"{tag}wide{i}", [P, SEQ]) for i in range(2)]
        w_in, step, var_ready, root_ready = wts.loaded, sem("step"), sem("var_ready"), sem("root_ready")
        twice_kept = sem("twice_kept")
        hn_ready, hnT_done, hnT_kept, qkv_done = (sem("hn_ready"), sem("hnT_done"), sem("hnT_kept"),
                                                  sem("qkv_done"))
        qT_kept, kx_ready, vx_ready, att_done = sem("qT_kept"), sem("kx_ready"), sem("vx_ready"), sem("att_done")
        shifted, exped, probs_ready = sem("shifted"), sem("exped"), sem("probs_ready")
        pT_done, pT_kept, o_done, o_kept = sem("pT_done"), sem("pT_kept"), sem("o_done"), sem("o_kept")
        oT_done, oT_kept, xa_done = sem("oT_done"), sem("oT_kept"), sem("xa_done")
        up_done, up_exped, u_ready, ff_done = sem("up_done"), sem("up_exped"), sem("u_ready"), sem("ff_done")
        delta_ready, put_done, put_read = sem("delta_ready"), sem("put_done"), sem("put_read")
        block = s.enter_context(nc.Block())
        LOADED = 16 * len(wts.sources)

        @block.vector
        def _(dve):
            chain = [0]

            def chained(ins):
                ins.then_inc(step, 1)
                chain[0] += 1
                dve.wait_ge(step, chain[0])

            def rms_rows(src, half):
                for pr in range(2):
                    last = dve.scalar_tensor_tensor(out=sq[:, pr, :], in0=src[:, pr, :], scalar=1.0, in1=src[:, pr, :],
                                                    op0=ALU.mult, op1=ALU.mult, accum_out=ss[:, pr:pr + 1])
                chained(last)
                dve.tensor_scalar(ve[:], ss[:], 1.0 / D, RMS_EPS, ALU.mult, ALU.add).then_inc(var_ready, 1)
                dve.wait_ge(root_ready, half + 1)
                chained(dve.reciprocal(r0[:], sd[:]))
                newton_rsqrt(dve, step, chain[0], ve, r0, t0, t1, rms)
                chain[0] += 4
                dve.wait_ge(step, chain[0])
                for pr in range(2):
                    last = dve.scalar_tensor_tensor(out=hn[:, pr, :], in0=src[:, pr, :], scalar=rms[:, pr:pr + 1],
                                                    in1=g[:, half, :], op0=ALU.mult, op1=ALU.mult)
                last.then_inc(hn_ready, 1)

            dve.wait_ge(w_in, LOADED)
            rms_rows(xsel, 0)
            dve.wait_ge(qkv_done, 1)
            for b in range(NB):
                k = E[:, b * CAP:(b + 1) * CAP][:, None, :].broadcast_to([P, HA, CAP])
                dve.tensor_tensor(kx[:, b, :, :], k, headm[:, :, None].broadcast_to([P, HA, CAP]),
                                  ALU.mult).then_inc(kx_ready, 1)
            dve.tensor_tensor(vx[:], C[:].rearrange("p (b d) -> p b d", b=NB),
                              pairm[:, None, :].broadcast_to([P, NB, D]), ALU.mult).then_inc(vx_ready, 1)
            for pr in range(2):
                dve.wait_ge(att_done, pr + 1)
                w = wide[pr][:].rearrange("p (h k) -> p h k", h=HA)
                chained(dve.tensor_tensor(sm[:, pr], w, causal[:, None, :].broadcast_to([P, HA, CAP]), ALU.add))
                chained(dve.tensor_reduce(mx[:, pr], sm[:, pr], AX.X, ALU.max))
                dve.tensor_tensor(sm[:, pr], sm[:, pr], mx[:, pr, :, None].broadcast_to([P, HA, CAP]),
                                  ALU.subtract).then_inc(shifted, 1)
            for pr in range(2):
                dve.wait_ge(exped, pr + 1)
                chained(dve.tensor_reduce(dn[:, pr], pr_[:, pr], AX.X, ALU.add))
                chained(dve.reciprocal(rd[:, pr], dn[:, pr]))
                dve.tensor_tensor(pr_[:, pr], pr_[:, pr], rd[:, pr, :, None].broadcast_to([P, HA, CAP]),
                                  ALU.mult).then_inc(probs_ready, 1)
            dve.wait_ge(o_done, 1)
            dve.tensor_copy(o[:], A[:, 0:2 * D].rearrange("p (r d) -> p r d", r=2)).then_inc(o_kept, 1)
            dve.wait_ge(xa_done, 1)
            chained(dve.tensor_copy(xa[:], C[:, 0:2 * D].rearrange("p (r d) -> p r d", r=2)))
            chained(dve.tensor_tensor(mid[:], xsel[:], xa[:], ALU.add))
            rms_rows(mid, 1)
            dve.wait_ge(up_exped, 1)
            chained(dve.tensor_scalar(e[:], e[:], 1.0, None, ALU.add))
            a3, b3 = (w[:, 0:6 * QK].rearrange("p (c t) -> p c t", c=3) for w in wide)
            chained(dve.reciprocal(e[:], e[:]))
            chained(dve.tensor_tensor(e[:], a3, e[:], ALU.mult))
            dve.tensor_tensor(u[:], b3, e[:], ALU.mult).then_inc(u_ready, 1)
            dve.wait_ge(ff_done, 1)
            dve.tensor_tensor(delta[:], A[:, 0:2 * D].rearrange("p (r d) -> p r d", r=2), xa[:],
                              ALU.add).then_inc(delta_ready, 1)
            for c in range(NCH):
                dve.wait_ge(put_done, c + 1)
                dve.tensor_tensor(x[:, 4 * c:4 * c + 4, :],
                                  (B, C, E)[c % 3][:].rearrange("p (k d) -> p k d", k=4),
                                  xh[:, 4 * c:4 * c + 4, :], ALU.add).then_inc(put_read, 1)

        @block.scalar
        def _(act):
            def root(half):
                act.wait_ge(var_ready, half + 1)
                act.activation(sd[:], ve[:], ACT.Sqrt).then_inc(root_ready, 1)

            root(0)
            act.wait_ge(hnT_done, 1)
            act.copy(twice[:], A[:, 0:2 * QK].rearrange("p (b t) -> p b t", b=NB)[:, :, None, :]
                     .broadcast_to([P, NB, 2, CAP])).then_inc(twice_kept, 1)
            act.copy(hnT[:], A[:, 0:2 * QK].rearrange("p (r t) -> p r t", r=2)).then_inc(hnT_kept, 1)
            act.wait_ge(qkv_done, 1)
            act.copy(qT[:], B[:, 0:2 * QK]).then_inc(qT_kept, 1)
            for pr in range(2):
                act.wait_ge(shifted, pr + 1)
                act.activation(pr_[:, pr], sm[:, pr], ACT.Exp).then_inc(exped, 1)
            for pr in range(2):
                act.wait_ge(pT_done, pr + 1)
                act.copy(pT[:, pr], wide[pr][:].rearrange("p (h t) -> p h t", t=P)).then_inc(pT_kept, 1)
            act.wait_ge(oT_done, 1)
            act.copy(oT[:], B[:, 0:2 * QK].rearrange("p (r t) -> p r t", r=2)).then_inc(oT_kept, 1)
            root(1)
            act.wait_ge(hnT_done, 2)
            act.copy(hnT[:], E[:, 0:2 * QK].rearrange("p (r t) -> p r t", r=2)).then_inc(hnT_kept, 1)
            act.wait_ge(up_done, 1)
            act.activation(e[:], wide[0][:, 0:6 * QK].rearrange("p (c t) -> p c t", c=3), ACT.Exp,
                           scale=-1.0).then_inc(up_exped, 1)

        @block.tensor
        def _(pe):
            def turned(half, to):
                pe.wait_ge(hn_ready, half + 1)
                for pr in range(2):
                    last = pe.transpose(to[:, pr * QK:(pr + 1) * QK], hn[:, pr, :], ident[:])
                last.then_inc(hnT_done, 1)
                pe.wait_ge(hnT_kept, half + 1)

            pe.wait_ge(w_in, LOADED)
            turned(0, A)
            pe.matmul(B[:, 0:2 * QK], wqkv[:, 0, :], hnT[:], start=True, stop=True)
            pe.matmul(E[:, 0:2 * QK], wqkv[:, 1, :], hnT[:], start=True, stop=True)
            pe.wait_ge(twice_kept, 1)
            for b in range(NB):
                last = pe.matmul(C[:, b * D:(b + 1) * D], twice[:, b, :, :], wqkv[:, 2, :], start=True, stop=True)
            last.then_inc(qkv_done, 1)
            pe.wait_ge(qT_kept, 1)
            for pr in range(2):
                pe.wait_ge(kx_ready, 2 * pr + 2)
                for b in (2 * pr, 2 * pr + 1):
                    rows = slice((b % 2) * CAP, (b % 2 + 1) * CAP)
                    for c in range(2):
                        last = pe.matmul(wide[pr][rows, c * CH:(c + 1) * CH], qT[:, b * CAP:(b + 1) * CAP],
                                         kx[:, b, c * HA // 2:(c + 1) * HA // 2, :], start=True, stop=True)
                last.then_inc(att_done, 1)
            for pr in range(2):
                pe.wait_ge(probs_ready, pr + 1)
                for h in range(HA // 2):
                    last = pe.transpose(wide[pr][:, h * P:(h + 1) * P], pr_[:, pr, 2 * h:2 * h + 2, :], ident[:])
                last.then_inc(pT_done, 1)
            pe.wait_ge(vx_ready, 1)
            for pr in range(2):
                pe.wait_ge(pT_kept, pr + 1)
                for b in (2 * pr, 2 * pr + 1):
                    rows = slice((b % 2) * CAP, (b % 2 + 1) * CAP)
                    for h in range(HA // 2):
                        last = pe.matmul(A[rows, pr * D + 2 * h * HDA:pr * D + 2 * (h + 1) * HDA],
                                         pT[:, pr, h, rows], vx[:, b, 2 * h * HDA:2 * (h + 1) * HDA],
                                         start=True, stop=True)
            last.then_inc(o_done, 1)
            pe.wait_ge(o_kept, 1)
            for pr in range(2):
                last = pe.transpose(B[:, pr * QK:(pr + 1) * QK], o[:, pr, :], ident[:])
            last.then_inc(oT_done, 1)
            pe.wait_ge(oT_kept, 1)
            for pr in range(2):
                last = pe.matmul(C[:, pr * D:(pr + 1) * D], oT[:, pr, :], wout[:], start=True, stop=True)
            last.then_inc(xa_done, 1)
            turned(1, E)
            for i in range(2):
                for c in range(3):
                    last = pe.matmul(wide[i][:, c * 2 * QK:(c + 1) * 2 * QK], w12[:, i, c * P:(c + 1) * P], hnT[:],
                                     start=True, stop=True)
            last.then_inc(up_done, 1)
            pe.wait_ge(u_ready, 1)
            for pr in range(2):
                for c in range(3):
                    last = pe.matmul(A[:, pr * D:(pr + 1) * D], u[:, c, pr * QK:(pr + 1) * QK], w3[:, c, :],
                                     start=c == 0, stop=c == 2)
            last.then_inc(ff_done, 1)
            pe.wait_ge(delta_ready, 1)
            for c in range(NCH):
                if c >= 3:
                    pe.wait_ge(put_read, c - 2)
                for k in range(4):
                    t = 4 * c + k
                    last = pe.matmul((B, C, E)[c % 3][:, k * D:(k + 1) * D], ohT[:, t, :],
                                     delta[:, t // (2 * TPB), :], start=True, stop=True)
                last.then_inc(put_done, 1)


def feed_forward(st, io, tag, x):
    with ExitStack() as s:
        ohT = st.sb(s, tag + "ohT", [P, NT, P])
        xsel = st.sb(s, tag + "xsel", [P, 2, D])
        xh = st.sb(s, tag + "xh", [P, NT, D])
        w = BlockWeights(st, s, io, tag)
        with ExitStack() as r:
            xn = st.sb(r, tag + "xn", [P, NT, D])
            oh = st.sb(r, tag + "oh", [P, NT, P])
            route(st, io, w, tag, x, xn, oh, ohT, xsel, xh)
        picked_block(st, w, tag, x, ohT, xsel, xh)


def prepare_b(st, io, x, q_dram, k_dram, v_dram, ident):
    nc = st.nc
    with ExitStack() as s:
        v_all = st.sb(s, "b_v_all", [P, NB * HB, JB, 2 * HDB], F16)
        xn = st.sb(s, "b_xn", [P, NT, D])
        ln = LnWork(st, s, "lnb", xn)
        wq, wdown = st.sb(s, "b_wq", [P, 2, P]), st.sb(s, "b_wdown", [P, 2 * RANK])
        wk, wv = st.sb(s, "b_wk", [2 * RANK, P]), st.sb(s, "b_wv", [2 * RANK, HB * HDB])
        hT = st.sb(s, "b_hT", [P, 2, CH])
        lat = st.sb(s, "b_lat", [2 * RANK, 2, CH])
        parts = st.sb(s, "b_parts", [P, 2, 4, 2, CH], F16)
        tps = st.ps(s, "b_tps", [P, CH])
        lps = st.ps(s, "b_lps", [2 * RANK, CH])
        qkps = [st.ps(s, f"b_qkps{i}", [P, CH]) for i in range(4)]
        vps = [st.ps(s, f"b_vps{i}", [P, CH]) for i in range(2)]
        w_in, transposed, hT_ready = st.sem("b_w_in"), st.sem("b_transposed"), st.sem("b_hT_ready")
        lat_done, lat_ready, qk_done = st.sem("b_lat_done"), st.sem("b_lat_ready"), st.sem("b_qk_done")
        v_done, hi_made, lo_made = st.sem("b_v_done"), st.sem("b_hi_made"), st.sem("b_lo_made")
        stored, v_stored = [st.sem(f"b_stored{i}") for i in range(2)], st.sem("b_v_stored")
        block = s.enter_context(nc.Block())
        scale = float(HDB) ** -0.5

        @block.sync
        def _(sp):
            for to, name in ((ident, "ident"), (wq, "bq_T"), (wdown, "bdown_T"), (wk, "bk_T"), (wv, "bv_T")):
                sp.dma_start(to[:], io[name]).then_inc(w_in, 16)
            for c in range(NCH):
                b, at = c // 2, c % 2 * CH
                for i in range(4):
                    sp.wait_ge(lo_made, 6 * c + i + 1)
                    dram = q_dram if i < 2 else k_dram
                    for part in range(2):
                        h0 = b * HB + i % 2 * 4
                        to = dram[part, h0:h0 + 4].rearrange("h d t -> (h d) t")[:, at:at + CH]
                        sp.dma_start(to, parts[:, c % 2, i, part, :]).then_inc(stored[c % 2], 16)
                if c % 2 == 1:
                    sp.wait_ge(lo_made, 6 * (c + 1))
                    sp.dma_start(v_dram[b * HB:(b + 1) * HB].rearrange("g p c -> p g c"),
                                 v_all[:, b * HB:(b + 1) * HB].rearrange("p g j d -> p g (j d)")).then_inc(v_stored, 16)
            for i in range(2):
                sp.wait_ge(stored[i], 16 * 8 * NCH // 2)
            sp.wait_ge(v_stored, 16 * NB)

        @block.tensor
        def _(pe):
            pe.wait_ge(w_in, 80)
            for c in range(NCH):
                pe.wait_ge(ln.normed, 4 * c + 4)
                for k in range(4):
                    if c and k == 0:
                        pe.wait_ge(hT_ready, c)
                    last = pe.transpose(tps[:, k * P:(k + 1) * P], xn[:, 4 * c + k, :], ident[:])
                last.then_inc(transposed, 1)
                pe.wait_ge(hT_ready, c + 1)
                if c:
                    pe.wait_ge(lat_ready, c)
                pe.matmul(lps[:], wdown[:], hT[:, c % 2, :], start=True, stop=True).then_inc(lat_done, 1)
                for i in range(2):
                    if c:
                        pe.wait_ge(lo_made, 6 * (c - 1) + i + 1)
                    pe.matmul(qkps[i][:], wq[:, i, :], hT[:, c % 2, :], start=True, stop=True).then_inc(qk_done, 1)
                pe.wait_ge(lat_ready, c + 1)
                if c:
                    pe.wait_ge(lo_made, 6 * (c - 1) + 4)
                for i in range(2):
                    own = slice(i * RANK, (i + 1) * RANK)
                    pe.matmul(qkps[2 + i][:], wk[own, :], lat[own, c % 2, :], start=True,
                              stop=True).then_inc(qk_done, 1)
                if c:
                    pe.wait_ge(lo_made, 6 * (c - 1) + 6)
                for k in range(2):
                    for i in range(2):
                        own, tok = slice(i * RANK, (i + 1) * RANK), (2 * i + k) * P
                        last = pe.matmul(vps[i][:, k * 256:(k + 1) * 256], lat[own, c % 2, tok:tok + P],
                                         wv[own, :], start=True, stop=True)
                        if k == 1:
                            last.then_inc(v_done, 1)

        def v_view(c, i, part):
            b, j = c // 2, c % 2 * 4 + 2 * i
            return v_all[:, b * HB:(b + 1) * HB, j:j + 2, part * HDB:(part + 1) * HDB].rearrange(
                "p h j d -> p j h d")

        @block.scalar
        def _(act):
            layernorm_scalar(act, ln)
            for c in range(NCH):
                act.wait_ge(transposed, c + 1)
                if c >= 2:
                    act.wait_ge(qk_done, 4 * (c - 2) + 2)
                act.copy(hT[:, c % 2, :], tps[:]).then_inc(hT_ready, 1)
                act.wait_ge(lat_done, c + 1)
                if c >= 2:
                    act.wait_ge(v_done, 2 * (c - 1))
                act.copy(lat[:, c % 2, :], lps[:]).then_inc(lat_ready, 1)
                for i in range(4):
                    act.wait_ge(qk_done, 4 * c + i + 1)
                    if i == 0 and c >= 2:
                        act.wait_ge(stored[c % 2], 16 * 8 * (c // 2))
                    act.activation(parts[:, c % 2, i, 0, :], qkps[i][:], ACT.Copy,
                                   scale=scale if i < 2 else 1.0).then_inc(hi_made, 1)
                for i in range(2):
                    act.wait_ge(v_done, 2 * c + i + 1)
                    src = vps[i][:].rearrange("p (j h d) -> p j h d", j=2, h=HB)
                    for k in range(2):
                        last = act.copy(v_view(c, i, 0)[:, k], src[:, k])
                    last.then_inc(hi_made, 1)

        @block.vector
        def _(dve):
            layernorm_vector(dve, ln, x, lambda b: None)
            for c in range(NCH):
                for i in range(4):
                    dve.wait_ge(hi_made, 6 * c + i + 1)
                    dve.scalar_tensor_tensor(out=parts[:, c % 2, i, 1, :], in0=qkps[i][:],
                                             scalar=scale if i < 2 else 1.0, in1=parts[:, c % 2, i, 0, :],
                                             op0=ALU.mult, op1=ALU.subtract).then_inc(lo_made, 1)
                for i in range(2):
                    dve.wait_ge(hi_made, 6 * c + i + 5)
                    src = vps[i][:].rearrange("p (j h d) -> p j h d", j=2, h=HB)
                    for k in range(2):
                        last = dve.tensor_tensor(v_view(c, i, 1)[:, k], src[:, k], v_view(c, i, 0)[:, k],
                                                 ALU.subtract)
                    last.then_inc(lo_made, 1)


def project_b(st, io, x, oT):
    nc = st.nc
    with ExitStack() as s:
        wo = st.sb(s, "pb_wo", [P, HB // 2, D])
        y = [st.ps(s, f"pb_y{i}", [P, 4, D]) for i in range(2)]
        w_in, y_done, y_read = st.sem("pb_w_in"), st.sem("pb_y_done"), st.sem("pb_y_read")
        block = s.enter_context(nc.Block())

        @block.sync
        def _(sp):
            sp.dma_start(wo[:], io["wo_T"]).then_inc(w_in, 16)

        @block.tensor
        def _(pe):
            pe.wait_ge(w_in, 16)
            for c in range(NCH):
                if c >= 2:
                    pe.wait_ge(y_read, c - 1)
                for k in range(4):
                    b, at = c // 2, (c % 2 * 4 + k) * P
                    for h in range(HB // 2):
                        col = (b * HB // 2 + h) * SEQ + at
                        last = pe.matmul(y[c % 2][:, k, :], oT[:, col:col + P], wo[:, h, :],
                                         start=h == 0, stop=h == HB // 2 - 1)
                last.then_inc(y_done, 1)

        @block.vector
        def _(dve):
            for c in range(NCH):
                dve.wait_ge(y_done, c + 1)
                dve.scalar_tensor_tensor(out=x[:, 4 * c:4 * c + 4, :], in0=y[c % 2][:], scalar=1.0 / PSCALE,
                                         in1=x[:, 4 * c:4 * c + 4, :], op0=ALU.mult,
                                         op1=ALU.add).then_inc(y_read, 1)


def store_x(st, x, out):
    nc = st.nc
    stored = st.sem("stored")
    with nc.Block() as block:
        @block.sync
        def _(sp):
            for b in range(NB):
                sp.dma_start(out[b].rearrange("(t p) d -> p t d", p=P),
                             x[:, b * TPB:(b + 1) * TPB, :]).then_inc(stored, 16)
            sp.wait_ge(stored, 16 * NB)


def build(nc, io, out):
    with ExitStack() as whole:
        st = Store(nc, whole)
        x = st.sb(whole, "x", [P, NT, D])
        ka_dram = nc.dram_tensor("ka_parts", (2, P, NTOK), F16, kind="Internal").ap()
        with ExitStack() as s:
            qT = st.sb(s, "qT", [P, NTOK])
            v = st.sb(s, "v", [P, NTOK])
            wpre = st.sb(s, "wpre", [P, HA])
            wpost = st.sb(s, "wpost", [P, HA * D])
            accT = st.sb(s, "accT", [P, NTOK])
            prepare_a(st, io, x, qT, v, ka_dram, wpre, wpost, accT)
            attend_a(st, qT, v, ka_dram, wpre, wpost, accT)
            project_a(st, io, x, accT)
        st.end_stage()
        feed_forward(st, io, "f1_", x)
        st.end_stage()
        q_dram = nc.dram_tensor("q_parts", (2, NB * HB, HDB, SEQ), F16, kind="Internal").ap()
        k_dram = nc.dram_tensor("k_parts", (2, NB * HB, HDB, SEQ), F16, kind="Internal").ap()
        v_dram = nc.dram_tensor("v_parts", (NB * HB, P, JB * 2 * HDB), F16, kind="Internal").ap()
        with ExitStack() as s:
            ident = st.sb(s, "b_ident", [P, P])
            prepare_b(st, io, x, q_dram, k_dram, v_dram, ident)
            oT = st.sb(s, "oT", [P, NB * HB // 2 * SEQ])
            attend_b(st, q_dram, k_dram, v_dram, oT, ident)
            project_b(st, io, x, oT)
        st.end_stage()
        feed_forward(st, io, "f2_", x)
        store_x(st, x, out)


def layouts(i):
    f = np.float32
    rows = np.ascontiguousarray
    wqkv, bqkv = i["L0_attn_a_Wqkv"], i["L0_attn_a_bqkv"]
    half = HDA // 2
    partner = np.arange(D).reshape(HA, 2, half)[:, ::-1].reshape(D)
    q, k = np.arange(D), D + np.arange(D)
    picks = [q, q[partner], k, k[partner]]
    inv = (f(1.0) / np.power(f(10000.0), np.arange(0, HDA, 2, dtype=f) / f(HDA))).astype(f)
    ang = np.arange(SEQ, dtype=f)[:, None] * inv[None, :]
    cos, sin = np.cos(ang).T, np.sin(ang).T
    sq = f(HDA) ** f(-0.5)
    rope = np.stack([np.tile(np.concatenate([cos, cos]), (HA, 1)),
                     np.tile(np.concatenate([-sin, sin]), (HA, 1))], axis=1).astype(f)
    rope = np.concatenate([rope * sq, rope], axis=1)

    def pad(w):
        return np.concatenate([w, np.zeros((3 * P - DFF, w.shape[1]), f)])

    return {
        "x": rows(i["L0_attn_a_x"]),
        "ident": np.eye(P, dtype=f),
        "wqk_T": rows(np.stack([wqkv[p].T for p in picks], axis=1)),
        "wv_T": rows(wqkv[2 * D:].T),
        "bqk": rows(np.stack([bqkv[p] for p in picks], axis=1)),
        "bv": rows(bqkv[None, 2 * D:]),
        "rope": rows(rope),
        "wpre": rows(np.repeat(i["L0_attn_a_Wpre"].T, HDA, axis=0)),
        "wpost": rows(np.repeat(i["L0_attn_a_Wpost"].T, HDA, axis=1).reshape(1, -1)),
        "wout_T": rows(i["L0_attn_a_Wout"].T),
        "bout": rows(i["L0_attn_a_bout"][None]),
        "w_router": rows(i["L0_ffn_w_router"][None]),
        "iota": rows(np.broadcast_to(np.stack([np.r_[np.arange(CAP), -np.ones(CAP)],
                                               np.r_[-np.ones(CAP), np.arange(CAP)]]), (P, 2, P)).astype(f)),
        "below": np.tril(np.ones((P, P), f), -1),
        "g": rows(np.stack([i["L0_ffn_g1"], i["L0_ffn_g2"]])[None]),
        "fqkv_T": rows(np.stack([i["L0_ffn_W_qkv"][k * D:(k + 1) * D].T for k in range(3)], axis=1)),
        "fout_T": rows(i["L0_ffn_W_out"].T),
        "w12_T": rows(np.stack([pad(i["L0_ffn_W1"]).T, pad(i["L0_ffn_W2"]).T], axis=1)),
        "w3_T": rows(pad(i["L0_ffn_W3"].T).reshape(3, P, D).transpose(1, 0, 2)),
        "headm": (np.kron(np.eye(HA), np.ones((HDA, 1))) * HDA ** -0.5).astype(f),
        "pairm": np.tile(np.kron(np.eye(2), np.ones((CAP, HDA))), (1, HA // 2)).astype(f),
        "causal": np.tile(np.triu(np.full((CAP, CAP), -1e30), 1), (2, 1)).astype(f),
        "bq_T": rows(i["L0_attn_b_Wq"].T.reshape(D, 2, P)),
        "bdown_T": rows(np.tile(i["L0_attn_b_Wkv_down"].T, (1, 2))),
        "bk_T": rows(i["L0_attn_b_Wk_up"].T.reshape(RANK, 2, P).transpose(1, 0, 2).reshape(2 * RANK, P)),
        "bv_T": rows(np.tile(i["L0_attn_b_Wv_up"].T, (2, 1))),
        "wo_T": rows(np.repeat(i["L0_attn_b_Wo"].T.reshape(HB // 2, 2, 1, HDB, D), 2, axis=2)
                     .reshape(HB // 2, P, D).transpose(1, 0, 2)),
    }


def kernel(**inputs):
    import concourse.bacc as bacc
    from concourse.bass_utils import run_bass_kernel_spmd

    arrays = layouts({k: np.asarray(v) for k, v in inputs.items()})
    nc = bacc.Bacc("TRN2", target_bir_lowering=False, num_devices=1)
    io = {n: nc.dram_tensor(n + "_dram", a.shape, mybir.dt.from_np(a.dtype), kind="ExternalInput").ap()
          for n, a in arrays.items()}
    out = nc.dram_tensor("out_dram", (NB, SEQ, D), F32, kind="ExternalOutput").ap()
    build(nc, io, out)
    result = run_bass_kernel_spmd(nc, [{n + "_dram": a for n, a in arrays.items()}], core_ids=[0])
    return result.results[0]["out_dram"]
```
